# Optimizing a Trainium2 kernel written in Bass

```python
import numpy as np
import jax
import jax.numpy as jnp

def _softmax(x, axis=-1):
    return jax.nn.softmax(x, axis=axis)

def _gelu(x):
    return jax.nn.gelu(x, approximate=True)

def _silu(x):
    return jax.nn.silu(x)

def _sigmoid(x):
    return jax.nn.sigmoid(x)

def _layernorm(x, axis=-1, eps=1e-05):
    m = jnp.mean(x, axis=axis, keepdims=True)
    v = jnp.var(x, axis=axis, keepdims=True)
    return (x - m) / jnp.sqrt(v + eps)

def _scatter_add(tgt, idx, src, axis=0):
    return tgt.at[idx].add(src)

def _segment_sum(src, seg, n):
    return jax.ops.segment_sum(src, seg, n)
kernel_name = 'mk_decoder_preln_d1_seqx_r4_b5cf95'

def setup_inputs(seed: int=0):
    np.random.seed(seed)
    _w = jnp.asarray

    def _rec_inputs():
        import jax
        import jax.numpy as jnp
        _rk = jax.random.key(seed)
        x = -0.000125 + 0.9999 * jax.random.normal(jax.random.fold_in(_rk, 1), (4, 512, 256), jnp.float32)
        _lenS = 512 - jax.random.randint(jax.random.fold_in(_rk, 7), (4,), 0, max(1, 512 // 4) + 1, jnp.int32)
        _lenS2 = 1601 - jax.random.randint(jax.random.fold_in(_rk, 8), (4,), 0, max(1, 1601 // 4) + 1, jnp.int32)
        _ctx_2048P = jax.random.normal(jax.random.fold_in(_rk, 11), (4, 16, 512), jnp.float32)
        _ctx_2048c = jax.random.dirichlet(jax.random.fold_in(_rk, 511), 0.3 * jnp.ones((16,), jnp.float32), (4, 1601))
        _ctx_2048t = jnp.einsum('bsk,bkd->bsd', _ctx_2048c, _ctx_2048P)
        _ctx_2048t = _ctx_2048t * jax.lax.rsqrt(jnp.mean(jnp.square(_ctx_2048t)) + 1e-12) * 0.953939
        ctx_2048 = -1.39393e-06 + 0.999914 * (_ctx_2048t + 0.3 * jax.random.normal(jax.random.fold_in(_rk, 611), (4, 1601, 512), jnp.float32))
        return (x, ctx_2048)
    x, ctx_2048 = _rec_inputs()

    def _L0_attn_setup():
        import jax, jax.numpy as jnp
        import numpy as np
        HEADS = 4
        DIM_HEAD = 32
        EPS = 1e-05
        key = jax.random.key(seed)
        ks = jax.random.split(key, 6)
        b, n, dim = (8, 1024, 256)
        hidden = HEADS * DIM_HEAD
        x = jax.random.normal(ks[0], (b, n, dim), dtype=jnp.float32)
        gamma = jnp.ones((1, 1, dim), dtype=jnp.float32)
        beta = jnp.zeros((1, 1, dim), dtype=jnp.float32)
        w_qkv = jax.random.normal(ks[1], (dim, hidden * 3), dtype=jnp.float32) / np.sqrt(dim)
        w_out = jax.random.normal(ks[2], (hidden, dim), dtype=jnp.float32) / np.sqrt(hidden)
        b_out = jnp.zeros((dim,), dtype=jnp.float32)
        return {'x': x, 'gamma': gamma, 'beta': beta, 'w_qkv': w_qkv, 'w_out': w_out, 'b_out': b_out}
    _L0_attn_all = _L0_attn_setup()
    _L0_attn_in = {k: v for k, v in _L0_attn_all.items() if k in ('gamma', 'beta', 'w_qkv', 'w_out', 'b_out')}
    del _L0_attn_all

    def _L0_xattn_setup():
        import jax, jax.numpy as jnp
        import numpy as np
        B, N, DIM = (8, 1024, 256)
        M, CTX = (64, 512)
        HEADS, DH = (16, 64)
        INNER = HEADS * DH
        EPS = 1e-06

        def _split_heads(t):
            b, n, _ = t.shape
            return t.reshape(b, n, HEADS, DH).transpose(0, 2, 1, 3)
        key = jax.random.key(seed)
        ks = jax.random.split(key, 6)
        x = jax.random.normal(ks[0], (B, N, DIM), dtype=jnp.float32)
        context = jax.random.normal(ks[1], (B, M, CTX), dtype=jnp.float32)
        Wq = jax.random.normal(ks[2], (DIM, INNER), dtype=jnp.float32) / np.sqrt(DIM)
        Wkv = jax.random.normal(ks[3], (CTX, 2 * INNER), dtype=jnp.float32) / np.sqrt(CTX)
        null_kv = jax.random.normal(ks[4], (2, DH), dtype=jnp.float32) / np.sqrt(2.0)
        Wout = jax.random.normal(ks[5], (INNER, DIM), dtype=jnp.float32) / np.sqrt(INNER)
        ln_scale = jnp.ones((DIM,), dtype=jnp.float32)
        ln_bias = jnp.zeros((DIM,), dtype=jnp.float32)
        return {'x': x, 'context': context, 'Wq': Wq, 'Wkv': Wkv, 'null_kv': null_kv, 'Wout': Wout, 'ln_scale': ln_scale, 'ln_bias': ln_bias}
    _L0_xattn_all = _L0_xattn_setup()
    _L0_xattn_in = {k: v for k, v in _L0_xattn_all.items() if k in ('Wq', 'Wkv', 'null_kv', 'Wout', 'ln_scale', 'ln_bias')}
    del _L0_xattn_all

    def _L0_ffn_setup():
        import jax, jax.numpy as jnp
        import numpy as np
        B, S, H = (4, 512, 256)
        E = 8
        GS = 2
        NG = E // GS
        F = int(H * 4 * (2.0 / 3.0))
        key = jax.random.key(seed)
        ks = jax.random.split(key, 7)
        sc_h = 1.0 / np.sqrt(H)
        sc_f = 1.0 / np.sqrt(F)
        return {'x': jax.random.normal(ks[0], (B, S, H), dtype=jnp.float32), 'Wr': jax.random.normal(ks[1], (H, E), dtype=jnp.float32) * sc_h, 'br': jnp.zeros((E,), dtype=jnp.float32), 'W_up': jax.random.normal(ks[2], (NG, H, F), dtype=jnp.float32) * sc_h, 'b_up': jax.random.normal(ks[3], (NG, F), dtype=jnp.float32) * 0.01, 'W_down': jax.random.normal(ks[4], (E, F, H), dtype=jnp.float32) * sc_f, 'b_down': jax.random.normal(ks[5], (E, H), dtype=jnp.float32) * 0.01}
    _L0_ffn_all = _L0_ffn_setup()
    _L0_ffn_in = {k: v for k, v in _L0_ffn_all.items() if k in ('Wr', 'br', 'W_up', 'b_up', 'W_down', 'b_down')}
    del _L0_ffn_all
    return {'x': x, 'ctx_2048': ctx_2048, 'L0_attn_gamma': _L0_attn_in['gamma'], 'L0_attn_beta': _L0_attn_in['beta'], 'L0_attn_w_qkv': _L0_attn_in['w_qkv'], 'L0_attn_w_out': _L0_attn_in['w_out'], 'L0_attn_b_out': _L0_attn_in['b_out'], 'L0_xattn_Wq': _L0_xattn_in['Wq'], 'L0_xattn_Wkv': _L0_xattn_in['Wkv'], 'L0_xattn_null_kv': _L0_xattn_in['null_kv'], 'L0_xattn_Wout': _L0_xattn_in['Wout'], 'L0_xattn_ln_scale': _L0_xattn_in['ln_scale'], 'L0_xattn_ln_bias': _L0_xattn_in['ln_bias'], 'L0_ffn_Wr': _L0_ffn_in['Wr'], 'L0_ffn_br': _L0_ffn_in['br'], 'L0_ffn_W_up': _L0_ffn_in['W_up'], 'L0_ffn_b_up': _L0_ffn_in['b_up'], 'L0_ffn_W_down': _L0_ffn_in['W_down'], 'L0_ffn_b_down': _L0_ffn_in['b_down']}

def reference(x, ctx_2048, L0_attn_gamma, L0_attn_beta, L0_attn_w_qkv, L0_attn_w_out, L0_attn_b_out, L0_xattn_Wq, L0_xattn_Wkv, L0_xattn_null_kv, L0_xattn_Wout, L0_xattn_ln_scale, L0_xattn_ln_bias, L0_ffn_Wr, L0_ffn_br, L0_ffn_W_up, L0_ffn_b_up, L0_ffn_W_down, L0_ffn_b_down):
    import jax
    import jax.numpy as jnp

    def _L0_attn_ref(x, gamma, beta, w_qkv, w_out, b_out):
        import jax, jax.numpy as jnp
        import numpy as np
        HEADS = 4
        DIM_HEAD = 32
        EPS = 1e-05
        b, n, dim = x.shape
        mean = jnp.mean(x, axis=2, keepdims=True)
        var = jnp.var(x, axis=2, keepdims=True)
        xn = (x - mean) / jnp.sqrt(var + EPS) * gamma + beta
        qkv = jnp.einsum('bnc,ck->bnk', xn, w_qkv)
        q, k, v = jnp.split(qkv, 3, axis=2)

        def to_heads(t):
            return t.reshape(b, n, HEADS, DIM_HEAD)
        q, k, v = (to_heads(q), to_heads(k), to_heads(v))
        q = q * DIM_HEAD ** (-0.5)
        k = jax.nn.softmax(k, axis=1)
        context = jnp.einsum('bnhd,bnhe->bhde', k, v)
        out = jnp.einsum('bhde,bnhd->bnhe', context, q)
        out = out.reshape(b, n, HEADS * DIM_HEAD)
        out = jnp.einsum('bnk,kc->bnc', out, w_out) + b_out
        return out + x

    def _L0_xattn_ref(x, context, Wq, Wkv, null_kv, Wout, ln_scale, ln_bias):
        import jax, jax.numpy as jnp
        import numpy as np
        B, N, DIM = (8, 1024, 256)
        M, CTX = (64, 512)
        HEADS, DH = (16, 64)
        INNER = HEADS * DH
        EPS = 1e-06

        def _split_heads(t):
            b, n, _ = t.shape
            return t.reshape(b, n, HEADS, DH).transpose(0, 2, 1, 3)
        scale = DH ** (-0.5)
        b = x.shape[0]
        q = _split_heads(jnp.einsum('bnd,df->bnf', x, Wq))
        kv = jnp.einsum('bmc,cf->bmf', context, Wkv)
        k, v = jnp.split(kv, 2, axis=-1)
        k, v = (_split_heads(k), _split_heads(v))
        nk = jnp.broadcast_to(null_kv[0], (b, HEADS, 1, DH))
        nv = jnp.broadcast_to(null_kv[1], (b, HEADS, 1, DH))
        k = jnp.concatenate((nk, k), axis=-2)
        v = jnp.concatenate((nv, v), axis=-2)
        q = q * scale
        sim = jnp.einsum('bhid,bhjd->bhij', q, k)
        attn = jax.nn.softmax(sim, axis=-1)
        out = jnp.einsum('bhij,bhjd->bhid', attn, v)
        out = out.transpose(0, 2, 1, 3).reshape(b, -1, INNER)
        out = jnp.einsum('bnf,fd->bnd', out, Wout)
        mu = jnp.mean(out, axis=-1, keepdims=True)
        var = jnp.var(out, axis=-1, keepdims=True)
        out = (out - mu) * jax.lax.rsqrt(var + EPS) * ln_scale + ln_bias
        return out

    def _L0_ffn_ref(x, Wr, br, W_up, b_up, W_down, b_down):
        import jax, jax.numpy as jnp
        import numpy as np
        B, S, H = (4, 512, 256)
        E = 8
        GS = 2
        NG = E // GS
        F = int(H * 4 * (2.0 / 3.0))
        b, s, h = x.shape
        n_tok = b * s
        k = n_tok // E
        xf = x.reshape(n_tok, h)
        logits = xf @ Wr + br
        Sm = jax.nn.softmax(logits, axis=-1)
        G_t, idx_t = jax.lax.top_k(Sm.T, k)
        G = G_t.T
        idx = idx_t.T
        tokens = xf[idx]
        group = jnp.arange(E) // GS
        Wu = W_up[group]
        bu = b_up[group]
        mid = jax.nn.silu(jnp.einsum('keh,ehf->kef', tokens, Wu) + bu)
        out = jnp.einsum('kef,efh->keh', mid, W_down) + b_down
        y = jnp.zeros_like(xf).at[idx].add(G[..., None] * out)
        return y.reshape(b, s, h)
    x = x + _L0_attn_ref(_layernorm(x, axis=-1), L0_attn_gamma, L0_attn_beta, L0_attn_w_qkv, L0_attn_w_out, L0_attn_b_out)
    x = x + _L0_xattn_ref(_layernorm(x, axis=-1), ctx_2048, L0_xattn_Wq, L0_xattn_Wkv, L0_xattn_null_kv, L0_xattn_Wout, L0_xattn_ln_scale, L0_xattn_ln_bias)
    x = x + _L0_ffn_ref(_layernorm(x, axis=-1), L0_ffn_Wr, L0_ffn_br, L0_ffn_W_up, L0_ffn_b_up, L0_ffn_W_down, L0_ffn_b_down)
    return x

_drawn_inputs = setup_inputs


def setup_inputs(seed=0):
    import zlib

    import numpy as np

    out = dict(_drawn_inputs(seed))
    spreads = {'L0_attn_gamma': (1.0, 0.6),
     'L0_attn_beta': (0.0, 0.1),
     'L0_attn_b_out': (0.0, 0.1),
     'L0_xattn_ln_scale': (1.0, 0.2),
     'L0_xattn_ln_bias': (0.0, 0.1),
     'L0_ffn_br': (0.0, 0.399)}
    factors = {'L0_xattn_null_kv': 8.0, 'L0_ffn_b_up': 53.822, 'L0_ffn_b_down': 32.491}
    for name, (base, spread) in spreads.items():
        noise = np.random.default_rng([zlib.crc32(name.encode()), seed]).standard_normal(out[name].shape)
        drawn = base * np.exp(spread * noise) if base else spread * noise
        out[name] = jnp.asarray(drawn.astype(out[name].dtype))
    for name, factor in factors.items():
        out[name] = (out[name] * factor).astype(out[name].dtype)
    return out
```

```python
from contextlib import ExitStack

import concourse.bass as bass
from concourse import mybir

ALU = mybir.AluOpType
ACT = mybir.ActivationFunctionType
AX = mybir.AxisListType
F32 = mybir.dt.float32
F32R = mybir.dt.float32r
I32 = mybir.dt.int32
P = 128


def build(nc, A, out):
    x_h, ctx_h = A["x"], A["ctx_2048"]
    B, S, D = x_h.shape
    CTX_LEN, CTX_DIM = ctx_h.shape[1:]
    TT = S // P
    NT = B * TT
    DC = D // P
    CC = CTX_DIM // P
    HID = A["L0_attn_w_out"].shape[0]
    LHEAD = 32
    LHEADS = HID // LHEAD
    LSCALE = LHEAD ** -0.5
    INNER = A["L0_xattn_Wq"].shape[1]
    DH = A["L0_xattn_null_kv"].shape[1]
    HEADS = INNER // DH
    XSCALE = DH ** -0.5
    HG = 4
    GROUPS = HEADS // HG
    GW = HG * DH
    PAIRS = HG // 2
    KT = (CTX_LEN + 1 + P - 1) // P
    LASTC = CTX_LEN - (KT - 1) * P
    LASTK = LASTC + 1
    KB = 4
    KCOL = (CTX_LEN + 1 + 2 * KB - 1) // (2 * KB) * 2
    KPAD = KB * KCOL
    NULL_COL = CTX_LEN - (KB - 1) * KCOL
    assert DH == 64 and S == 512 and KPAD <= KT * P and HID == P
    EXPERTS, F, _ = A["L0_ffn_W_down"].shape
    NGROUP = A["L0_ffn_W_up"].shape[0]
    SHARE = EXPERTS // NGROUP
    CAP = B * S // EXPERTS
    FC = (F + P - 1) // P
    FL = F - (FC - 1) * P
    SC = CAP // P
    REP = P // EXPERTS
    assert REP == 16
    LN_EPS, X_EPS = 1e-5, 1e-6
    RING = 4
    SIMS = HG * KT

    with ExitStack() as whole:
        def sb(name, shape, dt=F32, scope=whole):
            return scope.enter_context(nc.sbuf_tensor(name, shape, dt))

        def sem(name):
            return whole.enter_context(nc.semaphore(name))

        wide = whole.enter_context(nc.psum_tensor("wide", [P, 4, 512], F32))
        duo = whole.enter_context(nc.psum_tensor("duo", [P, 2, 512], F32))
        pv_ps = whole.enter_context(nc.psum_tensor("pv_ps", [P, 512], F32))
        misc = whole.enter_context(nc.psum_tensor("misc", [P, 512], F32))

        ident = sb("ident", [P, P])
        ones_row = sb("ones_row", [1, P])
        h3_dram = nc.dram_tensor("h3_scratch", (NT * P, D), F32, kind="Internal").ap()
        gate = sb("gate", [P, NT, EXPERTS])

        attention(nc, A, out, dict(locals()))
        experts(nc, A, out, dict(locals()))


class Chain:

    def __init__(self, eng, sem, rounds_before, per_round):
        self.eng, self.sem, self.n, self.base, self.per = eng, sem, 0, rounds_before, per_round

    def link(self, ins):
        self.n += 1
        ins.then_inc(self.sem, 1)
        self.eng.wait_ge(self.sem, self.base * self.per + self.n)

    def close(self):
        assert self.n == self.per, self.n


def rsqrt_steps(dve, chain, r, t, v, eps):
    chain.link(dve.tensor_scalar(v, v, eps, None, ALU.add))
    chain.link(dve.tensor_scalar(r.bitcast(I32), v.bitcast(I32), -0.5, 1597463007.0, ALU.mult, ALU.add))
    for _ in range(4):
        chain.link(dve.tensor_tensor(t, r, r, ALU.mult))
        chain.link(dve.scalar_tensor_tensor(out=t, in0=t, scalar=-0.5, in1=v, op0=ALU.mult, op1=ALU.mult))
        chain.link(dve.scalar_tensor_tensor(out=r, in0=t, scalar=1.5, in1=r, op0=ALU.add, op1=ALU.mult))


def attention(nc, A, out, c):
    (B, S, D, TT, DC, CC, CTX_LEN, HG, GROUPS, GW, PAIRS, KT, LASTC, LASTK, KB, KCOL, KPAD, NULL_COL, DH, HEADS,
     RING, SIMS, EXPERTS, LHEAD, LHEADS, HID, INNER) = (c[k] for k in (
        "B", "S", "D", "TT", "DC", "CC", "CTX_LEN", "HG", "GROUPS", "GW", "PAIRS", "KT", "LASTC", "LASTK", "KB",
        "KCOL", "KPAD", "NULL_COL", "DH", "HEADS", "RING", "SIMS", "EXPERTS", "LHEAD", "LHEADS", "HID", "INNER"))
    wide, duo, pv_ps, misc = c["wide"], c["duo"], c["pv_ps"], c["misc"]
    ident, ones_row, h3_dram, gate = (c[k] for k in ("ident", "ones_row", "h3_dram", "gate"))
    LSCALE, XSCALE, LN_EPS, X_EPS = c["LSCALE"], c["XSCALE"], c["LN_EPS"], c["X_EPS"]
    PR = HEADS // 2
    CRING = 4

    with ExitStack() as scope:
        def sb(name, shape, dt=F32):
            return scope.enter_context(nc.sbuf_tensor(name, shape, dt))

        def sem(name):
            return scope.enter_context(nc.semaphore(name))

        w_qkv = sb("w_qkv", [P, DC, 3 * HID])
        w_lout = sb("w_lout", [P, D])
        gamma = sb("gamma", [P, DC])
        beta = sb("beta", [P, DC])
        b_lout = sb("b_lout", [1, D])
        w_xout = sb("w_xout", [P, PR, D])
        ln_scale = sb("ln_scale", [P, D])
        ln_bias = sb("ln_bias", [P, D])
        w_r = sb("w_r", [P, DC, EXPERTS])
        b_r = sb("b_r", [1, EXPERTS])
        null_k = sb("null_k", [1, 2, DH])
        null_v = sb("null_v", [1, HG, DH])
        null_at_k = sb("null_at_k", [1, KCOL])
        null_at_v = sb("null_at_v", [1, LASTK])
        xb = sb("xb", [P, TT, D])
        xn0 = sb("xn0", [P, TT, D])
        xn = sb("xn", [P, TT, D])
        x1 = sb("x1", [P, TT, D])
        xT = sb("xT", [P, DC, S])
        stats = sb("stats", [P, TT, 6])
        mv = sb("mv", [P, TT, 2])
        rstd = sb("rstd", [P, TT])
        newton = sb("newton", [P, TT])
        kmax = sb("kmax", [P, 1])
        ksum = sb("ksum", [P, 1])
        ksum_r = sb("ksum_r", [P, 1])
        vl = sb("vl", [P, TT, HID])
        ekn = sb("ekn", [P, TT, HID])
        kv_bd = sb("kv_bd", [P, HID])
        ctx_in = sb("ctx_in", [P, CRING, CC * P])
        ctxT = sb("ctxT", [P, CC, KT * P])
        oT = sb("oT", [P, PR, S])
        lmax = sb("lmax", [P, TT])
        lexp = sb("lexp", [P, TT, EXPERTS])
        lsum = sb("lsum", [P, TT])
        wq = sb("wq", [P, DC, GW])
        wk = sb("wk", [P, CC, GW])
        wv = sb("wv", [P, CC, GW])
        q_hi = sb("q_hi", [P, HG, S], F32R)
        q_lo = sb("q_lo", [P, HG, S], F32R)
        k_hl = sb("k_hl", [P, HG, KPAD], F32R)
        k_h1 = sb("k_h1", [P, HG, KPAD], F32R)
        v_one = sb("v_one", [P, KT, PAIRS, 3, DH])
        probs = sb("probs", [P, RING, S])
        neg_max = sb("neg_max", [P, 2, TT])
        o_sb = sb("o_sb", [P, 2, S])
        o_rec = sb("o_rec", [P, S])
        ek, qT, loT = o_sb[:, 0, :], o_sb[:, 1, :], o_rec

        consts_ready = sem("consts_ready")
        pool_chain = sem("pool_chain")
        weights_in = sem("weights_in")
        x_in, ctx_in_s = sem("x_in"), [sem(f"ctx_in_{k}") for k in range(KT)]
        x_free = sem("x_free")
        wq_in, wk_in, wv_in = sem("wq_in"), sem("wk_in"), sem("wv_in")
        dve_batch, dve_item = sem("dve_batch"), sem("dve_item")
        act_batch = sem("act_batch")
        ctx_turned, ctx_kept = sem("ctx_turned"), sem("ctx_kept")
        ln_ready, turned, turn_kept = sem("ln_ready"), sem("turned"), sem("turn_kept")
        lin_proj, lin_kmax, lin_act, lin_v = sem("lin_proj"), sem("lin_kmax"), sem("lin_act"), sem("lin_v")
        ek_turned, ek_kept, lin_kv, lin_bd = sem("ek_turned"), sem("ek_kept"), sem("lin_kv"), sem("lin_bd")
        lin_o, lin_ok, lin_out = sem("lin_o"), sem("lin_ok"), sem("lin_out")
        q_made, q_rounded, q_split = sem("q_made"), sem("q_rounded"), sem("q_split")
        k_made, k_rounded, k_split = sem("k_made"), sem("k_rounded"), sem("k_split")
        v_made, v_kept = sem("v_made"), sem("v_kept")
        max_scores, max_taken, max_turned, max_row = (
            sem("max_scores"), sem("max_taken"), sem("max_turned"), sem("max_row"))
        scores_ready, probs_ready, probs_used = sem("scores_ready"), sem("probs_ready"), sem("probs_used")
        o_kept, o_normed = sem("o_kept"), sem("o_normed")
        x_out, x2_ready, h3_ready, rows_stored = sem("x_out"), sem("x2_ready"), sem("h3_ready"), sem("rows_stored")
        logits_ready, l_shift, l_exp = sem("logits_ready"), sem("l_shift"), sem("l_exp")

        block = scope.enter_context(nc.Block())

        @block.sync
        def _(sp):
            for dst, src in (
                (w_qkv[:, :, :], A["L0_attn_w_qkv"].rearrange("(c p) f -> p c f", p=P)),
                (w_lout[:, :], A["L0_attn_w_out"]),
                (b_lout[:, :], A["L0_attn_b_out"].rearrange("(a d) -> a d", a=1)),
                (w_xout[:, :, :], A["L0_xattn_Wout"].rearrange("(c p) f -> p c f", p=P)),
                (ln_scale[:, :], A["L0_xattn_ln_scale"].rearrange("(a d) -> a d", a=1).to_broadcast([P, D])),
                (ln_bias[:, :], A["L0_xattn_ln_bias"].rearrange("(a d) -> a d", a=1).to_broadcast([P, D])),
                (w_r[:, :, :], A["L0_ffn_Wr"].rearrange("(c p) f -> p c f", p=P)),
                (b_r[:, :], A["L0_ffn_br"].rearrange("(a d) -> a d", a=1)),
            ):
                sp.dma_start(dst, src).then_inc(weights_in, 16)
            for n in range(2):
                sp.dma_start(null_k[:, n, :], A["L0_xattn_null_kv"][0:1, :]).then_inc(weights_in, 16)
            for n in range(HG):
                sp.dma_start(null_v[:, n, :], A["L0_xattn_null_kv"][1:2, :]).then_inc(weights_in, 16)
            with nc.allow_non_contiguous_dma(reason="a column of the model dimension on partitions"):
                sp.dma_start(gamma[:, :], A["L0_attn_gamma"].rearrange("a b (c p) -> p (a b c)", p=P)).then_inc(weights_in, 16)
                sp.dma_start(beta[:, :], A["L0_attn_beta"].rearrange("a b (c p) -> p (a b c)", p=P)).then_inc(weights_in, 16)
            x_v = A["x"].rearrange("b (t p) d -> b p t d", p=P)
            sp.sem_inc(rows_stored, 1)
            with sp.Fori(0, B) as b:
                sp.wait_ge(x_free, b + 1)
                sp.dma_start(xb[:, :, :], x_v[bass.ds(b, 1)].rearrange("a p t d -> p (a t) d")).then_inc(x_in, 16)
                ctx_b = A["ctx_2048"][bass.ds(b, 1)].rearrange("a s d -> (a s) d")
                for k in range(KT):
                    sp.wait_ge(ctx_turned, b * KT + max(k - CRING + 1, 0) + CRING)
                    rows = P if k < KT - 1 else LASTC
                    sp.dma_start(ctx_in[0:rows, k % CRING, :], ctx_b[k * P:k * P + rows, :]).then_inc(ctx_in_s[k], 16)
                with sp.Fori(0, GROUPS) as g:
                    sp.wait_ge(v_made, (b * GROUPS + g + 1) * KT)
                    for dst, src, base, s in ((wq, "L0_xattn_Wq", 0, wq_in), (wk, "L0_xattn_Wkv", 0, wk_in),
                                              (wv, "L0_xattn_Wkv", INNER, wv_in)):
                        w = A[src].rearrange("(c p) f -> p c f", p=P)
                        sp.dma_start(dst[:, :, :], w[:, :, bass.ds(base + g * GW, GW)]).then_inc(s, 16)
                sp.wait_ge(x2_ready, b + 1)
                sp.dma_start(out.rearrange("b (t p) d -> b p t d", p=P)[bass.ds(b, 1)].rearrange("a p t d -> p (a t) d"),
                             x1[:, :, :]).then_inc(rows_stored, 16)
                sp.wait_ge(h3_ready, b + 1)
                sp.dma_start(h3_dram.rearrange("(b t p) d -> b p t d", p=P, t=TT)[bass.ds(b, 1)]
                             .rearrange("a p t d -> p (a t) d"), xn[:, :, :]).then_inc(rows_stored, 16)
            sp.wait_ge(rows_stored, B * 32 + 1)

        @block.gpsimd
        def _(pool):
            n = 0

            def link(ins):
                nonlocal n
                n += 1
                ins.then_inc(pool_chain, 1)
                pool.wait_ge(pool_chain, n)

            link(pool.memset(ident[:, :], 0.0))
            link(pool.affine_select(out=ident[:, :], in_=ident[:, :], compare_op=ALU.not_equal, fill=1.0, base=0,
                                    pattern=[[-1, P]], channel_multiplier=1))
            link(pool.memset(ones_row[:, :], 1.0))
            link(pool.memset(null_at_k[:, :], 0.0))
            link(pool.memset(null_at_k[:, NULL_COL:KCOL], 1.0))
            link(pool.memset(null_at_v[:, :], 0.0))
            link(pool.memset(null_at_v[:, LASTC:LASTK], 1.0))
            link(pool.memset(ctxT[:, :, CTX_LEN:KT * P], 0.0))
            link(pool.memset(kv_bd[:, :], 0.0))
            link(pool.memset(v_one[:, KT - 1, :, :, :], 0.0))
            link(pool.memset(v_one[:, 0:KT - 1, :, 1, :], 1.0))
            link(pool.memset(v_one[0:LASTK, KT - 1, :, 1, :], 1.0))
            link(pool.memset(q_lo[:, :, :].bitcast(F32), 0.0))
            link(pool.memset(k_h1[DH:P, :, :].bitcast(F32), 0.0))
            link(pool.memset(k_h1[DH:DH + 1, :, :].bitcast(F32), 1.0))
            pool.nop().then_inc(consts_ready, 1)

        @block.tensor
        def _(pe):
            pe.sem_inc(ctx_turned, CRING)
            pe.sem_inc(v_made, KT)
            pe.sem_inc(probs_used, RING)
            pe.wait_ge(consts_ready, 1)
            pe.wait_ge(weights_in, 16 * 16)

            def turn_rows(src, rows):
                for ck in range(DC):
                    for i in range(rows):
                        ins = pe.transpose(wide[:, ck, i * P:(i + 1) * P], src[:, i, ck * P:(ck + 1) * P], ident[:, :])
                ins.then_inc(turned, 1)

            with pe.Fori(0, B) as b:
                for k in range(KT):
                    rows = P if k < KT - 1 else LASTC
                    pe.wait_ge(ctx_in_s[k], b * 16 + 16)
                    if k >= 2:
                        pe.wait_ge(ctx_kept, b * KT + k - 1)
                    for ck in range(CC):
                        ins = pe.transpose(duo[:, k % 2, ck * P:ck * P + rows], ctx_in[0:rows, k % CRING, ck * P:(ck + 1) * P],
                                           ident[0:rows, 0:rows])
                    ins.then_inc(ctx_turned, 1)
                pe.wait_ge(ctx_kept, b * KT + KT)
                pe.wait_ge(ln_ready, b * 3 + 1)
                turn_rows(xn, TT)
                pe.wait_ge(turn_kept, b * 3 + 1)
                for n, bank in ((0, duo[:, 1, :]), (1, duo[:, 0, :])):
                    for ck in range(DC):
                        pe.matmul(bank, w_qkv[:, ck, n * HID:(n + 1) * HID], xT[:, ck, :],
                                  start=ck == 0, stop=ck == DC - 1)
                for i in range(TT):
                    for ck in range(DC):
                        ins = pe.matmul(wide[:, 2, i * HID:(i + 1) * HID], xT[:, ck, i * P:(i + 1) * P],
                                        w_qkv[:, ck, 2 * HID:3 * HID], start=ck == 0, stop=ck == DC - 1)
                ins.then_inc(lin_proj, 1)
                pe.wait_ge(lin_act, b * 2 + 1)
                for i in range(TT):
                    ins = pe.transpose(wide[:, 3, i * P:(i + 1) * P], ek[:, i * P:(i + 1) * P], ident[:, :])
                ins.then_inc(ek_turned, 1)
                pe.wait_ge(ek_kept, b + 1)
                pe.wait_ge(lin_v, b + 1)
                for i in range(TT):
                    ins = pe.matmul(misc[:, 0:HID], ekn[:, i, :], vl[:, i, :], start=i == 0, stop=i == TT - 1)
                ins.then_inc(lin_kv, 1)
                pe.wait_ge(lin_bd, b + 1)
                pe.wait_ge(lin_act, b * 2 + 2)
                pe.matmul(duo[:, 0, :], kv_bd[:, :], qT[:, :], start=True, stop=True).then_inc(lin_o, 1)
                pe.wait_ge(lin_ok, b + 1)
                for i in range(TT):
                    pe.matmul(wide[:, i, 0:D], loT[:, i * P:(i + 1) * P], w_lout[:, :], start=True, stop=False)
                    ins = pe.matmul(wide[:, i, 0:D], ones_row[:, :], b_lout[:, :], start=False, stop=True)
                ins.then_inc(lin_out, 1)
                pe.wait_ge(ln_ready, b * 3 + 2)
                turn_rows(xn, TT)

                with pe.Fori(0, GROUPS) as g:
                    t = b * GROUPS + g
                    pe.wait_ge(turn_kept, b * 3 + 2)
                    pe.wait_ge(wq_in, t * 16 + 16)
                    for p in range(PAIRS):
                        for ck in range(DC):
                            ins = pe.matmul(duo[:, p, :], wq[:, ck, p * P:(p + 1) * P], xT[:, ck, :],
                                            start=ck == 0, stop=ck == DC - 1)
                        ins.then_inc(q_made, 1)
                    pe.wait_ge(wk_in, t * 16 + 16)
                    for p in range(PAIRS):
                        for n in range(KB):
                            if p >= 1:
                                pe.wait_ge(k_split, t * PAIRS * KB + (p - 1) * KB + n + 1)
                                pe.wait_ge(k_rounded, t * PAIRS * KB + (p - 1) * KB + n + 1)
                            last = n == KB - 1
                            for ck in range(CC):
                                ins = pe.matmul(wide[:, n, 0:KCOL], wk[:, ck, p * P:(p + 1) * P],
                                                ctxT[:, ck, n * KCOL:(n + 1) * KCOL],
                                                start=ck == 0, stop=ck == CC - 1 and not last)
                            if last:
                                ins = pe.matmul(wide[:, n, 0:KCOL], null_k[:, :, :].rearrange("a n d -> a (n d)"),
                                                null_at_k[:, :], start=False, stop=True)
                            ins.then_inc(k_made, 1)

                    def values(k):
                        rows = P if k < KT - 1 else LASTK
                        if k < 2:
                            pe.wait_ge(q_rounded, t * PAIRS + k + 1)
                            pe.wait_ge(q_split, t * PAIRS + k + 1)
                        else:
                            pe.wait_ge(v_kept, t * KT + k - 1)
                        for ck in range(CC):
                            ins = pe.matmul(duo[0:rows, k % 2, 0:GW], ctxT[:, ck, k * P:k * P + rows], wv[:, ck, :],
                                            start=ck == 0, stop=ck == CC - 1 and k < KT - 1)
                        if k == KT - 1:
                            ins = pe.matmul(duo[0:rows, k % 2, 0:GW], null_at_v[:, :],
                                            null_v[:, :, :].rearrange("a n d -> a (n d)"), start=False, stop=True)
                        ins.then_inc(v_made, 1)

                    def scores_for_max(j, i):
                        if j or i:
                            pe.wait_ge(max_taken, t * HG * TT + j * TT + i)
                        for n in range(KB):
                            ins = pe.matmul(wide[:, n, 0:KCOL], q_hi[:, j, i * P:(i + 1) * P],
                                            k_hl[:, j, n * KCOL:(n + 1) * KCOL], start=True, stop=True)
                        ins.then_inc(max_scores, 1)

                    def turn_max(j):
                        pe.wait_ge(max_taken, t * HG * TT + (j + 1) * TT)
                        for i in range(TT):
                            ins = pe.transpose(misc[0:1, i * P:(i + 1) * P], neg_max[:, j % 2, i:i + 1], ident[:, :])
                        ins.then_inc(max_turned, 1)

                    def scores(j, k):
                        n = j * KT + k
                        rows = P if k < KT - 1 else LASTK
                        if k == 0:
                            pe.wait_ge(max_row, t * HG + j + 1)
                        pe.wait_ge(probs_ready, t * SIMS + n - 1) if n >= 2 else None
                        cols = slice(k * P, k * P + rows)
                        pe.matmul(duo[0:rows, n % 2, :], k_hl[:, j, cols], q_hi[:, j, :], start=True, stop=False)
                        pe.matmul(duo[0:rows, n % 2, :], k_h1[:, j, cols], q_lo[:, j, :], start=False,
                                  stop=True).then_inc(scores_ready, 1)

                    def weigh(n):
                        j, k = divmod(n, KT)
                        pe.wait_ge(probs_ready, t * SIMS + n + 1)
                        if k == 0 and j >= 1:
                            pe.wait_ge(o_kept, t * HG + j)
                        pe.matmul(pv_ps[:, :], v_one[:, k, j // 2, j % 2:j % 2 + 2, :].rearrange("p n d -> p (n d)"), probs[:, n % RING, :], start=k == 0,
                                  stop=k == KT - 1).then_inc(probs_used, 1)

                    pe.wait_ge(wv_in, t * 16 + 16)
                    for k in range(KT):
                        values(k)
                        if k == 2:
                            pe.wait_ge(k_split, (t + 1) * PAIRS * KB)
                            pe.wait_ge(k_rounded, (t + 1) * PAIRS * KB)
                        if k >= 2 and (k - 2) % 3 == 0 and (k - 2) // 3 < TT:
                            scores_for_max(0, (k - 2) // 3)
                    turn_max(0)
                    pe.wait_ge(v_kept, (t + 1) * KT)
                    for n in range(SIMS):
                        j, k = divmod(n, KT)
                        scores(j, k)
                        if j + 1 < HG:
                            if k % 3 == 1 and k // 3 < TT:
                                scores_for_max(j + 1, k // 3)
                            if k == KT - 1:
                                turn_max(j + 1)
                        if n >= 2:
                            weigh(n - 2)
                    weigh(SIMS - 2)
                    weigh(SIMS - 1)
                    pe.wait_ge(o_kept, (t + 1) * HG)

                pe.wait_ge(o_normed, (b + 1) * HEADS)
                for i in range(TT):
                    for h in range(PR):
                        ins = pe.matmul(wide[:, i, 0:D], oT[:, h, i * P:(i + 1) * P], w_xout[:, h, :],
                                        start=h == 0, stop=h == PR - 1)
                ins.then_inc(x_out, 1)
                pe.wait_ge(ln_ready, b * 3 + 3)
                turn_rows(xn, TT)
                pe.wait_ge(turn_kept, b * 3 + 3)
                for i in range(TT):
                    for ck in range(DC):
                        pe.matmul(misc[:, i * EXPERTS:(i + 1) * EXPERTS], xT[:, ck, i * P:(i + 1) * P], w_r[:, ck, :],
                                  start=ck == 0, stop=False)
                    ins = pe.matmul(misc[:, i * EXPERTS:(i + 1) * EXPERTS], ones_row[:, :], b_r[:, :], start=False,
                                    stop=True)
                ins.then_inc(logits_ready, 1)
                pe.wait_ge(l_shift, b + 1)

        @block.scalar
        def _(act):
            act.wait_ge(consts_ready, 1)
            act.wait_ge(weights_in, 16 * 16)
            with act.Fori(0, B) as b:
                for k in range(1, KT, 2):
                    act.wait_ge(ctx_turned, b * KT + k + 1 + CRING)
                    act.wait_ge(ctx_kept, b * KT + k)
                    rows = P if k < KT - 1 else LASTC
                    act.activation(ctxT[:, :, k * P:k * P + rows],
                                   duo[:, 1, :].rearrange("p (c n) -> p c n", c=CC)[:, :, 0:rows],
                                   ACT.Copy).then_inc(ctx_kept, 1)

                def keep_turned(n, affine):
                    act.wait_ge(turned, b * 3 + n + 1)
                    for ck in range(DC):
                        if affine:
                            ins = act.activation(xT[:, ck, :], wide[:, ck, :], ACT.Identity, bias=beta[:, ck:ck + 1],
                                                 scale=gamma[:, ck:ck + 1])
                        else:
                            ins = act.activation(xT[:, ck, :], wide[:, ck, :], ACT.Copy)
                    ins.then_inc(turn_kept, 1)

                keep_turned(0, True)
                act.wait_ge(lin_kmax, b + 1)
                act.activation(ek[:, :], duo[:, 0 + 0, :] if False else duo[:, 0, :], ACT.Exp, bias=kmax[:, 0:1],
                               accum_out=ksum[:, 0:1]).then_inc(lin_act, 1)
                act.activation(qT[:, :], duo[:, 1, :], ACT.Copy, scale=LSCALE).then_inc(lin_act, 1)
                act.wait_ge(ek_turned, b + 1)
                act.activation(ekn[:, :, :].rearrange("p t h -> p (t h)"), wide[:, 3, :], ACT.Copy).then_inc(ek_kept, 1)
                act.wait_ge(lin_o, b + 1)
                act.activation(loT[:, :], duo[:, 0, :], ACT.Copy).then_inc(lin_ok, 1)
                keep_turned(1, False)

                with act.Fori(0, GROUPS) as g:
                    t = b * GROUPS + g
                    for p in range(PAIRS):
                        act.wait_ge(q_made, t * PAIRS + p + 1)
                        for n in range(2):
                            j, rows = 2 * p + n, slice(n * DH, (n + 1) * DH)
                            for half in range(2):
                                ins = act.activation(q_hi[half * DH:(half + 1) * DH, j, :], duo[rows, p, :], ACT.Copy,
                                                     scale=XSCALE)
                        ins.then_inc(q_rounded, 1)
                    for p in range(PAIRS):
                        for m in range(KB):
                            act.wait_ge(k_made, t * PAIRS * KB + p * KB + m + 1)
                            for n in range(2):
                                j, rows = 2 * p + n, slice(n * DH, (n + 1) * DH)
                                for dst in (k_hl, k_h1):
                                    ins = act.activation(dst[0:DH, j, m * KCOL:(m + 1) * KCOL], wide[rows, m, 0:KCOL],
                                                         ACT.Copy)
                            ins.then_inc(k_rounded, 1)
                    for k in range(KT):
                        act.wait_ge(v_made, t * KT + k + 1 + KT)
                        rows = P if k < KT - 1 else LASTK
                        act.activation(v_one[0:rows, k, :, 0:3:2, :],
                                       duo[0:rows, k % 2, 0:GW].rearrange("p (h n d) -> p h n d", h=PAIRS, n=2),
                                       ACT.Copy).then_inc(v_kept, 1)

                    def keep_o(j):
                        act.wait_ge(probs_used, t * SIMS + (j + 1) * KT + RING)
                        act.wait_ge(o_normed, t * HG + j - 1) if j >= 2 else None
                        act.activation(o_sb[:, j % 2, :], pv_ps[:, :], ACT.Copy).then_inc(o_kept, 1)

                    for n in range(SIMS):
                        j, k = divmod(n, KT)
                        rows = P if k < KT - 1 else LASTK
                        act.wait_ge(scores_ready, t * SIMS + n + 1)
                        act.wait_ge(probs_used, t * SIMS + n + 1)
                        act.activation(probs[0:rows, n % RING, :], duo[0:rows, n % 2, :], ACT.Exp)\
                           .then_inc(probs_ready, 1)
                        if k == 2 and j >= 1:
                            keep_o(j - 1)
                    keep_o(HG - 1)
                    act.wait_ge(o_normed, (t + 1) * HG)

                keep_turned(2, False)
                act.wait_ge(l_shift, b + 1)
                act.activation(lexp[:, :, :], lexp[:, :, :], ACT.Exp).then_inc(l_exp, 1)

        @block.vector
        def _(dve):
            dve.sem_inc(x_free, 1)
            dve.memset(probs[:, :, :], 0.0).then_inc(act_batch, 1)
            dve.wait_ge(act_batch, 1)
            dve.wait_ge(weights_in, 16 * 16)
            dve.wait_ge(consts_ready, 1)
            with dve.Fori(0, B) as b:
                chain = Chain(dve, dve_batch, b, 93)
                for k in range(0, KT, 2):
                    dve.wait_ge(ctx_turned, b * KT + k + 1 + CRING)
                    if k:
                        dve.wait_ge(ctx_kept, b * KT + k)
                    rows = P if k < KT - 1 else LASTC
                    dve.tensor_copy(ctxT[:, :, k * P:k * P + rows],
                                    duo[:, 0, :].rearrange("p (c n) -> p c n", c=CC)[:, :, 0:rows])\
                       .then_inc(ctx_kept, 1)

                def moments(src, eps):
                    for i in range(TT):
                        ins = dve.bn_stats(stats[:, i, :], src(i))
                    chain.link(ins)
                    dve.memset(newton[:, :], 0.0)
                    for i in range(TT):
                        ins = dve.bn_aggr(mv[:, i, :], stats[:, i, :])
                    chain.link(ins)
                    rsqrt_steps(dve, chain, rstd[:, :], newton[:, :], mv[:, :, 1], eps)

                def normalise(dst, src):
                    for i in range(TT):
                        ins = dve.tensor_scalar(dst(i), src(i), mv[:, i, 0:1], rstd[:, i:i + 1], ALU.subtract, ALU.mult)
                    return ins

                def at(buf):
                    return lambda i: buf[:, i, :]

                dve.wait_ge(x_in, b * 16 + 16)
                moments(at(xb), LN_EPS)
                chain.link(normalise(at(xn0), at(xb)))
                moments(at(xn0), LN_EPS)
                dve.wait_ge(rows_stored, b * 32 + 1)
                normalise(at(xn), at(xn0)).then_inc(ln_ready, 1)
                dve.wait_ge(lin_proj, b + 1)
                dve.tensor_reduce(kmax[:, 0:1], duo[:, 0, :], AX.X, ALU.max, negate=True).then_inc(lin_kmax, 1)
                dve.tensor_copy(vl[:, :, :].rearrange("p t h -> p (t h)"), wide[:, 2, :]).then_inc(lin_v, 1)
                dve.wait_ge(lin_act, b * 2 + 1)
                chain.link(dve.reciprocal(ksum_r[:, :], ksum[:, :]))
                dve.wait_ge(lin_kv, b + 1)
                for h in range(LHEADS):
                    r = slice(h * LHEAD, (h + 1) * LHEAD)
                    ins = dve.tensor_scalar(kv_bd[r, r], misc[r, r], ksum_r[r, 0:1], None, ALU.mult)
                ins.then_inc(lin_bd, 1)
                dve.wait_ge(lin_out, b + 1)
                for i in range(TT):
                    ins = dve.tensor_tensor(x1[:, i, :], wide[:, i, 0:D], xn0[:, i, :], ALU.add)
                chain.link(ins)
                chain.link(dve.tensor_tensor(x1[:, :, :], x1[:, :, :], xb[:, :, :], ALU.add))
                dve.sem_inc(x_free, 1)
                moments(at(x1), LN_EPS)
                normalise(at(xn), at(x1)).then_inc(ln_ready, 1)

                with dve.Fori(0, GROUPS) as g:
                    t = b * GROUPS + g
                    for p in range(PAIRS):
                        dve.wait_ge(q_rounded, t * PAIRS + p + 1)
                        for n in range(2):
                            j, rows = 2 * p + n, slice(n * DH, (n + 1) * DH)
                            ins = dve.scalar_tensor_tensor(out=q_lo[0:DH, j, :], in0=duo[rows, p, :], scalar=XSCALE,
                                                           in1=q_hi[0:DH, j, :].bitcast(F32), op0=ALU.mult,
                                                           op1=ALU.subtract)
                        ins.then_inc(q_split, 1)
                    for p in range(PAIRS):
                        for m in range(KB):
                            dve.wait_ge(k_rounded, t * PAIRS * KB + p * KB + m + 1)
                            cols = slice(m * KCOL, (m + 1) * KCOL)
                            for n in range(2):
                                j, rows = 2 * p + n, slice(n * DH, (n + 1) * DH)
                                ins = dve.tensor_tensor(k_hl[DH:P, j, cols], wide[rows, m, 0:KCOL],
                                                        k_hl[0:DH, j, cols].bitcast(F32), ALU.subtract)
                            ins.then_inc(k_split, 1)

                    def norm(j):
                        dve.wait_ge(o_kept, t * HG + j + 1)
                        half, other = slice((j % 2) * DH, (j % 2 + 1) * DH), slice((1 - j % 2) * DH, (2 - j % 2) * DH)
                        dve.reciprocal(o_rec[half, :], o_sb[other, j % 2, :]).then_inc(dve_item, 1)
                        dve.wait_ge(dve_item, t * HG + j + 1)
                        dve.tensor_tensor(oT[half, bass.ds(g * PAIRS + j // 2, 1), :].rearrange("p a s -> p (a s)"),
                                          o_sb[half, j % 2, :], o_rec[half, :], ALU.mult).then_inc(o_normed, 1)

                    for j in range(HG):
                        for i in range(TT):
                            dve.wait_ge(max_scores, t * HG * TT + j * TT + i + 1)
                            dve.tensor_reduce(neg_max[:, j % 2, i:i + 1], wide[:, :, 0:KCOL], AX.XY, ALU.max,
                                              negate=True).then_inc(max_taken, 1)
                        dve.wait_ge(max_turned, t * HG + j + 1)
                        dve.tensor_copy(q_lo[DH:DH + 1, j, :], misc[0:1, :]).then_inc(max_row, 1)
                        if j >= 1:
                            norm(j - 1)
                    norm(HG - 1)

                dve.wait_ge(x_out, b + 1)
                moments(lambda i: wide[:, i, 0:D], X_EPS)
                chain.link(normalise(at(xn), lambda i: wide[:, i, 0:D]))
                for i in range(TT):
                    ins = dve.tensor_tensor(xn[:, i, :], xn[:, i, :], ln_scale[:, :], ALU.mult)
                chain.link(ins)
                for i in range(TT):
                    ins = dve.tensor_tensor(xn[:, i, :], xn[:, i, :], ln_bias[:, :], ALU.add)
                chain.link(ins)
                chain.link(dve.tensor_tensor(x1[:, :, :], x1[:, :, :], xn[:, :, :], ALU.add))
                dve.sem_inc(x2_ready, 1)
                moments(at(x1), LN_EPS)
                ins = normalise(at(xn), at(x1))
                chain.link(ins)
                dve.sem_inc(ln_ready, 1)
                dve.sem_inc(h3_ready, 1)
                dve.wait_ge(logits_ready, b + 1)
                lg = misc[:, 0:TT * EXPERTS].rearrange("p (t e) -> p t e", e=EXPERTS)
                chain.link(dve.tensor_reduce(lmax[:, :], lg, AX.X, ALU.max))
                for i in range(TT):
                    ins = dve.tensor_scalar(lexp[:, i, :], lg[:, i, :], lmax[:, i:i + 1], None, ALU.subtract)
                ins.then_inc(l_shift, 1)
                dve.wait_ge(l_exp, b + 1)
                chain.link(dve.tensor_reduce(lsum[:, :], lexp[:, :, :], AX.X, ALU.add))
                chain.link(dve.reciprocal(lsum[:, :], lsum[:, :]))
                for i in range(TT):
                    ins = dve.tensor_scalar(gate[:, bass.ds(b * TT + i, 1), :].rearrange("p a e -> p (a e)"),
                                            lexp[:, i, :], lsum[:, i:i + 1], None, ALU.mult)
                chain.link(ins)
                chain.close()


def experts(nc, A, out, c):
    (B, S, D, P_, NT, DC, EXPERTS, F, SHARE, CAP, FC, FL, SC, REP) = (c[k] for k in (
        "B", "S", "D", "TT", "NT", "DC", "EXPERTS", "F", "SHARE", "CAP", "FC", "FL", "SC", "REP"))
    wide, duo, pv_ps, misc = c["wide"], c["duo"], c["pv_ps"], c["misc"]
    ident, ones_row, h3_dram, gate = (c[k] for k in ("ident", "ones_row", "h3_dram", "gate"))
    N = B * S
    SHIFTS = [28, 24, 20, 16, 12, 8, 4, 0]

    with ExitStack() as scope:
        def sb(name, shape, dt=F32):
            return scope.enter_context(nc.sbuf_tensor(name, shape, dt))

        def sem(name):
            return scope.enter_context(nc.semaphore(name))

        x2 = sb("x2", [P, NT, D])
        h3 = sb("h3", [P, NT, D])
        gate_rep = sb("gate_rep", [P, NT, EXPERTS, REP])
        gateT = sb("gateT", [P, N])
        same = sb("same", [P, EXPERTS, REP])
        digit = sb("digit", [P, 1], I32)
        base = sb("base", [P, 1], I32)
        tried = sb("tried", [P, 1], I32)
        step = sb("step", [P, 1], I32)
        count = sb("count", [P, 1])
        enough = sb("enough", [P, 1])
        above = sb("above", [P, N])
        equal = sb("equal", [P, N])
        run = sb("run", [P, N])
        zeros = sb("zeros", [P, N])
        slot = sb("slot", [P, NT, EXPERTS])
        slot_no = sb("slot_no", [P, CAP])
        slot_i = sb("slot_i", [P, CAP], I32)
        pick = sb("pick", [P, NT, CAP])
        pickT = sb("pickT", [P, SC, N])
        w_up = sb("w_up", [P, DC, F])
        w_dn = sb("w_dn", [P, FC, D])
        b_up = sb("b_up", [P, FC])
        b_dn = sb("b_dn", [1, D])
        taken = sb("taken", [P, DC, CAP])
        mid = sb("mid", [P, FC, CAP])
        made = sb("made", [P, SC, D])

        e_const, e_chain, e_dve = sem("e_const"), sem("e_chain"), sem("e_dve")
        spread, gate_turned, gate_kept, tried_count, tried_sum = (
            sem("spread"), sem("gate_turned"), sem("gate_kept"), sem("tried_count"), sem("tried_sum"))
        slots_known, slots_turned = sem("slots_known"), sem("slots_turned")
        slots_kept = sem("slots_kept")
        up_in, dn_in, up_free, dn_free = sem("up_in"), sem("dn_in"), sem("up_free"), sem("dn_free")
        picked, pick_turned, pick_kept = sem("picked"), sem("pick_turned"), sem("pick_kept")
        gathered, taken_kept = sem("gathered"), sem("taken_kept")
        up_done, mid_ready, dn_done, made_ready = sem("up_done"), sem("mid_ready"), sem("dn_done"), sem("made_ready")
        spread_back, added = sem("spread_back"), sem("added")
        stored, rows_in = sem("stored"), sem("rows_in")

        block = scope.enter_context(nc.Block())
        TURNS = NT * SC // 4

        @block.sync
        def _(sp):
            sp.dma_start(h3[:, :, :], h3_dram.rearrange("(t p) d -> p t d", p=P)).then_inc(rows_in, 16)
            sp.dma_start(x2[:, :, :], out.rearrange("b (t p) d -> p (b t) d", p=P)).then_inc(rows_in, 16)
            with sp.Fori(0, EXPERTS) as e:
                sp.wait_ge(up_free, e + 1)
                up = A["L0_ffn_W_up"][bass.ds(e // SHARE, 1)].rearrange("a (c p) f -> p (a c) f", p=P)
                sp.dma_start(w_up[:, :, :], up).then_inc(up_in, 16)
                bu = A["L0_ffn_b_up"][bass.ds(e // SHARE, 1)]
                with nc.allow_non_contiguous_dma(reason="a column of the hidden dimension on partitions"):
                    sp.dma_start(b_up[:, 0:FC - 1], bu[:, 0:(FC - 1) * P].rearrange("a (c p) -> p (a c)", p=P))\
                      .then_inc(up_in, 16)
                    sp.dma_start(b_up[0:FL, FC - 1:FC], bu[:, (FC - 1) * P:F].rearrange("a p -> p a")).then_inc(up_in, 16)
                sp.wait_ge(dn_free, e + 1)
                dn = A["L0_ffn_W_down"][bass.ds(e, 1)].rearrange("a f d -> (a f) d")
                sp.dma_start(w_dn[:, 0:FC - 1, :], dn[0:(FC - 1) * P, :].rearrange("(c p) d -> p c d", p=P))\
                  .then_inc(dn_in, 16)
                sp.dma_start(w_dn[0:FL, FC - 1, :], dn[(FC - 1) * P:F, :]).then_inc(dn_in, 16)
                sp.dma_start(b_dn[:, :], A["L0_ffn_b_down"][bass.ds(e, 1)]).then_inc(dn_in, 16)
            sp.wait_ge(added, EXPERTS * NT)
            sp.dma_start(out.rearrange("b (t p) d -> p (b t) d", p=P), x2[:, :, :]).then_inc(stored, 16)
            sp.wait_ge(stored, 16)

        @block.gpsimd
        def _(pool):
            n = 0

            def link(ins):
                nonlocal n
                n += 1
                ins.then_inc(e_const, 1)
                pool.wait_ge(e_const, n)

            link(pool.memset(same[:, :, :], 1.0))
            link(pool.affine_select(out=same[:, :, :], in_=same[:, :, :], compare_op=ALU.is_ge, fill=0.0, base=0,
                                    pattern=[[-REP, EXPERTS], [0, REP]], channel_multiplier=1))
            link(pool.affine_select(out=same[:, :, :], in_=same[:, :, :], compare_op=ALU.is_ge, fill=0.0, base=REP - 1,
                                    pattern=[[REP, EXPERTS], [0, REP]], channel_multiplier=-1))
            link(pool.iota(slot_i[:, :], [[1, CAP]], base=0, channel_multiplier=0))
            link(pool.iota(digit[:, :], [[0, 1]], base=0, channel_multiplier=1))
            link(pool.memset(zeros[:, :], 0.0))

        CONSTS = 6

        @block.tensor
        def _(pe):
            pe.sem_inc(up_free, 1)
            pe.sem_inc(dn_free, 1)
            pe.wait_ge(e_const, CONSTS)
            pe.wait_ge(spread, 1)
            for i in range(NT):
                ins = pe.transpose(wide[:, i // 4, (i % 4) * P:(i % 4 + 1) * P],
                                   gate_rep[:, i, :, :].rearrange("p e r -> p (e r)"), ident[:, :])
            ins.then_inc(gate_turned, 1)
            for n in range(len(SHIFTS)):
                pe.wait_ge(tried_count, n + 1)
                pe.matmul(misc[:, n:n + 1], same[:, :, :].rearrange("p e r -> p (e r)"), enough[:, :], start=True,
                          stop=True).then_inc(tried_sum, 1)
            pe.wait_ge(slots_known, 1)
            for i in range(NT):
                ins = pe.transpose(wide[:, i // 4, (i % 4) * P:(i % 4 + 1) * P], run[:, i * P:(i + 1) * P], ident[:, :])
            ins.then_inc(slots_turned, 1)
            pe.wait_ge(slots_kept, 1)
            pe.wait_ge(rows_in, 32)
            with pe.Fori(0, EXPERTS) as e:
                for i in range(NT):
                    pe.wait_ge(picked, e * NT + i + 1)
                for ck in range(DC):
                    for i in range(NT):
                        ins = pe.matmul(wide[:, ck, 0:CAP], h3[:, i, ck * P:(ck + 1) * P], pick[:, i, :],
                                        start=i == 0, stop=i == NT - 1)
                ins.then_inc(gathered, 1)
                for n in range(TURNS):
                    if n >= 2:
                        pe.wait_ge(pick_kept, e * TURNS + n - 1)
                    for m in range(4):
                        sc, i = divmod(n * 4 + m, NT)
                        ins = pe.transpose(duo[:, n % 2, m * P:(m + 1) * P], pick[:, i, sc * P:(sc + 1) * P], ident[:, :])
                    ins.then_inc(pick_turned, 1)
                pe.wait_ge(up_in, e * 48 + 48)
                pe.wait_ge(taken_kept, e + 1)
                for f in range(FC):
                    M = P if f < FC - 1 else FL
                    bank = (pv_ps, misc)[f % 2]
                    if f >= 2:
                        pe.wait_ge(mid_ready, e * FC + f - 1)
                    for ck in range(DC):
                        ins = pe.matmul(bank[0:M, 0:CAP], w_up[:, ck, f * P:f * P + M], taken[:, ck, :],
                                        start=ck == 0, stop=ck == DC - 1)
                    ins.then_inc(up_done, 1)
                pe.wait_ge(mid_ready, e * FC + FC)
                pe.sem_inc(up_free, 1)
                pe.wait_ge(dn_in, e * 48 + 48)
                for sc in range(SC):
                    for f in range(FC):
                        M = P if f < FC - 1 else FL
                        pe.matmul(wide[:, 2 + sc, 0:D], mid[0:M, f, sc * P:(sc + 1) * P], w_dn[0:M, f, :],
                                  start=f == 0, stop=False)
                    ins = pe.matmul(wide[:, 2 + sc, 0:D], ones_row[:, :], b_dn[:, :], start=False, stop=True)
                ins.then_inc(dn_done, 1)
                pe.wait_ge(made_ready, e + 1)
                pe.sem_inc(dn_free, 1)
                pe.wait_ge(pick_kept, (e + 1) * TURNS)
                for i in range(NT):
                    if i >= 2:
                        pe.wait_ge(added, e * NT + i - 1)
                    for sc in range(SC):
                        ins = pe.matmul(duo[:, i % 2, 0:D], pickT[:, sc, i * P:(i + 1) * P], made[:, sc, :],
                                        start=sc == 0, stop=sc == SC - 1)
                    ins.then_inc(spread_back, 1)
                pe.wait_ge(added, (e + 1) * NT)

        @block.scalar
        def _(act):
            act.wait_ge(gate_turned, 1)
            act.activation(gateT[:, :], wide[:, :, :].rearrange("p b n -> p (b n)"), ACT.Copy).then_inc(gate_kept, 1)
            with act.Fori(0, EXPERTS) as e:
                act.wait_ge(gathered, e + 1)
                act.activation(taken[:, :, :], wide[:, 0:DC, 0:CAP], ACT.Copy).then_inc(taken_kept, 1)
                for n in range(TURNS):
                    act.wait_ge(pick_turned, e * TURNS + n + 1)
                    sc, i = divmod(n * 4, NT)
                    act.activation(pickT[:, sc, i * P:(i + 4) * P], duo[:, n % 2, :], ACT.Copy).then_inc(pick_kept, 1)
                for f in range(FC):
                    M = P if f < FC - 1 else FL
                    act.wait_ge(up_done, e * FC + f + 1)
                    act.activation(mid[0:M, f, :], (pv_ps, misc)[f % 2][0:M, 0:CAP], ACT.Silu,
                                   bias=b_up[0:M, f:f + 1]).then_inc(mid_ready, 1)
                act.wait_ge(dn_done, e + 1)
                act.activation(made[:, :, :], wide[:, 2:2 + SC, 0:D], ACT.Copy).then_inc(made_ready, 1)

        @block.vector
        def _(dve):
            n = 0

            def link(ins):
                nonlocal n
                n += 1
                ins.then_inc(e_chain, 1)
                dve.wait_ge(e_chain, n)

            dve.wait_ge(e_const, CONSTS)
            for r in range(REP):
                ins = dve.tensor_copy(gate_rep[:, :, :, r], gate[:, :, :])
            ins.then_inc(spread, 1)
            link(dve.tensor_copy(slot_no[:, :], slot_i[:, :]))
            link(dve.tensor_single_scalar(digit[:, :], digit[:, :], REP - 1, ALU.bitwise_and))
            link(dve.memset(base[:, :], 0))
            dve.wait_ge(gate_kept, 1)
            for k, shift in enumerate(SHIFTS):
                fold = 2 if k == 0 else 0
                link(dve.tensor_scalar(tried[:, :], digit[:, :], fold, shift, ALU.logical_shift_right,
                                       ALU.logical_shift_left))
                link(dve.tensor_tensor(tried[:, :], tried[:, :], base[:, :], ALU.bitwise_or))
                link(dve.tensor_scalar(above[:, :], gateT[:, :], tried[:, 0:1].bitcast(F32), 0.0, ALU.is_ge, ALU.add,
                                       accum_out=count[:, :]))
                dve.tensor_single_scalar(enough[:, :], count[:, :], float(CAP), ALU.is_ge).then_inc(tried_count, 1)
                dve.wait_ge(tried_sum, k + 1)
                link(dve.tensor_scalar(step[:, :], misc[:, k:k + 1], 1.0 / (1 << fold), -1.0, ALU.mult, ALU.add))
                link(dve.tensor_single_scalar(step[:, :], step[:, :], shift, ALU.logical_shift_left))
                link(dve.tensor_tensor(base[:, :], base[:, :], step[:, :], ALU.bitwise_or))
            cut = base[:, 0:1].bitcast(F32)
            link(dve.tensor_scalar(above[:, :], gateT[:, :], cut, 0.0, ALU.is_gt, ALU.add, accum_out=count[:, :]))
            link(dve.tensor_scalar(count[:, :], count[:, :], -1.0, float(CAP), ALU.mult, ALU.add))
            link(dve.tensor_scalar(equal[:, :], gateT[:, :], cut, None, ALU.is_equal))
            link(dve.tensor_tensor_scan(run[:, :], equal[:, :], zeros[:, :], 0.0, ALU.add, ALU.add))
            link(dve.scalar_tensor_tensor(out=equal[:, :], in0=run[:, :], scalar=count[:, 0:1], in1=equal[:, :],
                                          op0=ALU.is_le, op1=ALU.mult))
            link(dve.tensor_tensor(above[:, :], above[:, :], equal[:, :], ALU.add))
            link(dve.tensor_tensor_scan(run[:, :], above[:, :], zeros[:, :], 0.0, ALU.add, ALU.add))
            link(dve.tensor_tensor(run[:, :], run[:, :], above[:, :], ALU.mult))
            dve.tensor_single_scalar(run[:, :], run[:, :], -1.0, ALU.add).then_inc(slots_known, 1)
            dve.wait_ge(slots_turned, 1)
            rows = wide[:, :, :].rearrange("p b (i e r) -> p (b i) e r", e=EXPERTS, r=REP)
            dve.tensor_copy(slot[:, :, :], rows[:, :, :, 0]).then_inc(slots_kept, 1)
            dve.wait_ge(slots_kept, 1)
            dve.wait_ge(rows_in, 32)
            with dve.Fori(0, EXPERTS) as e:
                for i in range(NT):
                    dve.tensor_scalar(pick[:, i, :], slot_no[:, :],
                                      slot[:, i, bass.ds(e, 1)], None,
                                      ALU.is_equal).then_inc(picked, 1)
                for i in range(NT):
                    dve.wait_ge(spread_back, e * NT + i + 1)
                    dve.scalar_tensor_tensor(out=x2[:, i, :], in0=duo[:, i % 2, 0:D],
                                             scalar=gate[:, i, bass.ds(e, 1)],
                                             in1=x2[:, i, :], op0=ALU.mult, op1=ALU.add).then_inc(added, 1)


_INS = ['x', 'ctx_2048', 'L0_attn_gamma', 'L0_attn_beta', 'L0_attn_w_qkv', 'L0_attn_w_out', 'L0_attn_b_out',
        'L0_xattn_Wq', 'L0_xattn_Wkv', 'L0_xattn_null_kv', 'L0_xattn_Wout', 'L0_xattn_ln_scale', 'L0_xattn_ln_bias',
        'L0_ffn_Wr', 'L0_ffn_br', 'L0_ffn_W_up', 'L0_ffn_b_up', 'L0_ffn_W_down', 'L0_ffn_b_down']


def kernel(**inputs):
    import numpy as _np
    import concourse.bacc as _bacc
    from concourse import mybir as _mybir
    from concourse.bass_utils import run_bass_kernel_spmd as _run

    nc = _bacc.Bacc("TRN2", target_bir_lowering=False, num_devices=1)
    arrays, aps = {}, {}
    for name in _INS:
        a = _np.ascontiguousarray(inputs[name])
        arrays[f"in_{name}_dram"] = a
        aps[name] = nc.dram_tensor(f"in_{name}_dram", a.shape, _mybir.dt.from_np(a.dtype), kind="ExternalInput").ap()
    shape = inputs["x"].shape
    res = nc.dram_tensor("out_0_dram", shape, _mybir.dt.float32, kind="ExternalOutput").ap()
    build(nc, aps, res)
    r = _run(nc, [arrays], core_ids=[0])
    return r.results[0]["out_0_dram"]
```

```python
from contextlib import ExitStack

import concourse.bass as bass
from concourse import mybir

ALU = mybir.AluOpType
ACT = mybir.ActivationFunctionType
AX = mybir.AxisListType
F32 = mybir.dt.float32
F32R = mybir.dt.float32r
I32 = mybir.dt.int32
P = 128


def build(nc, A, out):
    x_h, ctx_h = A["x"], A["ctx_2048"]
    B, S, D = x_h.shape
    CTX_LEN, CTX_DIM = ctx_h.shape[1:]
    TT = S // P
    NT = B * TT
    DC = D // P
    CC = CTX_DIM // P
    HID = A["L0_attn_w_out"].shape[0]
    LHEAD = 32
    LHEADS = HID // LHEAD
    LSCALE = LHEAD ** -0.5
    INNER = A["L0_xattn_Wq"].shape[1]
    DH = A["L0_xattn_null_kv"].shape[1]
    HEADS = INNER // DH
    XSCALE = DH ** -0.5
    HG = 4
    GROUPS = HEADS // HG
    GW = HG * DH
    PAIRS = HG // 2
    KT = (CTX_LEN + 1 + P - 1) // P
    LASTC = CTX_LEN - (KT - 1) * P
    LASTK = LASTC + 1
    KB = 4
    KCOL = (CTX_LEN + 1 + 2 * KB - 1) // (2 * KB) * 2
    KPAD = KB * KCOL
    NULL_COL = CTX_LEN - (KB - 1) * KCOL
    assert DH == 64 and S == 512 and KPAD <= KT * P and HID == P
    EXPERTS, F, _ = A["L0_ffn_W_down"].shape
    NGROUP = A["L0_ffn_W_up"].shape[0]
    SHARE = EXPERTS // NGROUP
    CAP = B * S // EXPERTS
    FC = (F + P - 1) // P
    FL = F - (FC - 1) * P
    SC = CAP // P
    REP = P // EXPERTS
    assert REP == 16
    LN_EPS, X_EPS = 1e-5, 1e-6
    RAW = 3
    HIRING = 4
    LORING = 3
    LAG = 3
    SIMS = HG * KT
    FIRST_MAX_AT = (7, 8, 9, 10)
    MAX_AT = (3, 5, 7, 9)
    TURN_AT = 11

    with ExitStack() as whole:
        wide = whole.enter_context(nc.psum_tensor("wide", [P, 4, 512], F32))
        trio = whole.enter_context(nc.psum_tensor("trio", [P, 3, 512], F32))
        pv_ps = whole.enter_context(nc.psum_tensor("pv_ps", [P, 512], F32))
        ident = whole.enter_context(nc.sbuf_tensor("ident", [P, P], F32))
        x1_dram = nc.dram_tensor("x1_scratch", (B, S, D), F32, kind="Internal").ap()
        h2_dram = nc.dram_tensor("h2_scratch", (B, P, DC * S), F32, kind="Internal").ap()
        x2_dram = nc.dram_tensor("x2_scratch", (B, S, D), F32, kind="Internal").ap()
        h3_dram = nc.dram_tensor("h3_scratch", (B, S, D), F32, kind="Internal").ap()

        linear_attention(nc, A, dict(locals()))
        cross_attention(nc, A, dict(locals()))
        experts(nc, A, out, dict(locals()))


class Chain:

    def __init__(self, eng, sem, rounds_before, per_round):
        self.eng, self.sem, self.n, self.base, self.per = eng, sem, 0, rounds_before, per_round

    def link(self, ins):
        self.n += 1
        ins.then_inc(self.sem, 1)
        self.eng.wait_ge(self.sem, self.base * self.per + self.n)

    def close(self):
        assert self.n == self.per, self.n


def rsqrt_steps(dve, chain, r, t, v, eps):
    chain.link(dve.tensor_scalar(v, v, eps, None, ALU.add))
    chain.link(dve.tensor_scalar(r.bitcast(I32), v.bitcast(I32), -0.5, 1597463007.0, ALU.mult, ALU.add))
    for _ in range(4):
        chain.link(dve.tensor_tensor(t, r, r, ALU.mult))
        chain.link(dve.scalar_tensor_tensor(out=t, in0=t, scalar=-0.5, in1=v, op0=ALU.mult, op1=ALU.mult))
        chain.link(dve.scalar_tensor_tensor(out=r, in0=t, scalar=1.5, in1=r, op0=ALU.add, op1=ALU.mult))


def moments(dve, chain, stats, mv, rstd, newton, srcs, eps):
    for i, src in enumerate(srcs):
        ins = dve.bn_stats(stats[:, i, :], src)
    chain.link(ins)
    dve.memset(newton, 0.0)
    for i in range(len(srcs)):
        ins = dve.bn_aggr(mv[:, i, :], stats[:, i, :])
    chain.link(ins)
    rsqrt_steps(dve, chain, rstd, newton, mv[:, 0:len(srcs), 1], eps)


def normalise(dve, mv, rstd, dsts, srcs):
    for i, (dst, src) in enumerate(zip(dsts, srcs)):
        ins = dve.tensor_scalar(dst, src, mv[:, i, 0:1], rstd[:, i:i + 1], ALU.subtract, ALU.mult)
    return ins


def linear_attention(nc, A, c):
    B, S, D, TT, NT, DC, LHEAD, LHEADS, HID, LSCALE, LN_EPS = (c[k] for k in (
        "B", "S", "D", "TT", "NT", "DC", "LHEAD", "LHEADS", "HID", "LSCALE", "LN_EPS"))
    wide, trio, pv_ps, ident = (c[k] for k in ("wide", "trio", "pv_ps", "ident"))
    x1_dram, h2_dram = c["x1_dram"], c["h2_dram"]
    HALF = NT // 2

    with ExitStack() as scope:
        def sb(name, shape, dt=F32):
            return scope.enter_context(nc.sbuf_tensor(name, shape, dt))

        def sem(name):
            return scope.enter_context(nc.semaphore(name))

        ones_row = sb("ones_row", [1, P])
        w_qkv = sb("w_qkv", [P, DC, 3 * HID])
        w_lout = sb("w_lout", [P, D])
        gamma = sb("gamma", [P, DC])
        beta = sb("beta", [P, DC])
        b_lout = sb("b_lout", [1, D])
        x = sb("x", [P, NT, D])
        xn0 = sb("xn0", [P, NT, D])
        xn = sb("xn", [P, NT, D])
        xT = sb("xT", [P, 2, DC, S])
        h2T = sb("h2T", [P, B, DC, S])
        stats = sb("stats", [P, HALF, 6])
        mv = sb("mv", [P, HALF, 2])
        rstd = sb("rstd", [P, HALF])
        newton = sb("newton", [P, HALF])
        kmax = sb("kmax", [P, B])
        ksum = sb("ksum", [P, B])
        ksum_r = sb("ksum_r", [P, B])
        ek = sb("ek", [P, 2, S])
        qT = sb("qT", [P, 2, S])
        vl = sb("vl", [P, 2, TT, HID])
        ekn = sb("ekn", [P, 2, TT, HID])
        kv_bd = sb("kv_bd", [P, 2, HID])
        loT = sb("loT", [P, 2, S])

        consts, weights_in = sem("consts"), sem("weights_in")
        x_in = [sem(f"x_in_{b}") for b in range(B)]
        steps = sem("steps")
        ln_ready, turned, turn_kept = sem("ln_ready"), sem("turned"), sem("turn_kept")
        projected, kmax_ready, keys_ready, q_ready, v_ready = (
            sem("projected"), sem("kmax_ready"), sem("keys_ready"), sem("q_ready"), sem("v_ready"))
        keys_turned, keys_kept, kv_made, kv_ready = sem("keys_turned"), sem("keys_kept"), sem("kv_made"), sem("kv_ready")
        o_made, o_kept, out_made, x1_ready, h2_ready = (
            sem("o_made"), sem("o_kept"), sem("out_made"), sem("x1_ready"), sem("h2_ready"))
        stored = sem("stored")
        WEIGHTS = 5

        block = scope.enter_context(nc.Block())

        @block.sync
        def _(sp):
            for b in range(B):
                sp.dma_start(x[:, b * TT:(b + 1) * TT, :], A["x"][b].rearrange("(t p) d -> p t d", p=P)).then_inc(x_in[b], 16)
            for dst, src in (
                (w_qkv[:, :, :], A["L0_attn_w_qkv"].rearrange("(c p) f -> p c f", p=P)),
                (w_lout[:, :], A["L0_attn_w_out"]),
                (b_lout[:, :], A["L0_attn_b_out"].rearrange("(a d) -> a d", a=1)),
            ):
                sp.dma_start(dst, src).then_inc(weights_in, 16)
            with nc.allow_non_contiguous_dma(reason="a column of the model dimension on partitions"):
                for dst, src in ((gamma, "L0_attn_gamma"), (beta, "L0_attn_beta")):
                    sp.dma_start(dst[:, :], A[src].rearrange("a b (c p) -> p (a b c)", p=P)).then_inc(weights_in, 16)
            for b in range(B):
                sp.wait_ge(x1_ready, b + 1)
                sp.dma_start(x1_dram[b].rearrange("(t p) d -> p t d", p=P), xn0[:, b * TT:(b + 1) * TT, :])\
                  .then_inc(stored, 16)
            for b in range(B):
                sp.wait_ge(h2_ready, b + 1)
                sp.dma_start(h2_dram[b], h2T[:, b, :, :].rearrange("p c s -> p (c s)")).then_inc(stored, 16)
            sp.wait_ge(stored, 2 * B * 16)

        @block.gpsimd
        def _(pool):
            pool.memset(ident[:, :], 0.0).then_inc(consts, 1)
            pool.wait_ge(consts, 1)
            pool.affine_select(out=ident[:, :], in_=ident[:, :], compare_op=ALU.not_equal, fill=1.0, base=0,
                               pattern=[[-1, P]], channel_multiplier=1).then_inc(consts, 1)
            pool.memset(ones_row[:, :], 1.0).then_inc(consts, 1)
            pool.memset(kv_bd[:, :, :], 0.0).then_inc(consts, 1)

        CONSTS = 4

        @block.tensor
        def _(pe):
            pe.wait_ge(consts, CONSTS)
            pe.wait_ge(weights_in, WEIGHTS * 16)

            def turn(n):
                b = n % B
                pe.wait_ge(ln_ready, 2 * (n // B) + b // 2 + 1)
                if n >= 1:
                    pe.wait_ge(turn_kept, n)
                for ck in range(DC):
                    for i in range(TT):
                        ins = pe.transpose(wide[:, ck, i * P:(i + 1) * P], xn[:, b * TT + i, ck * P:(ck + 1) * P],
                                           ident[:, :])
                ins.then_inc(turned, 1)

            def project(b):
                pe.wait_ge(turn_kept, b + 1)
                if b >= 1:
                    pe.wait_ge(x1_ready, b)
                for n in range(2):
                    for ck in range(DC):
                        pe.matmul(trio[:, n, :], w_qkv[:, ck, (1 - n) * HID:(2 - n) * HID], xT[:, b % 2, ck, :],
                                  start=ck == 0, stop=ck == DC - 1)
                for i in range(TT):
                    for ck in range(DC):
                        ins = pe.matmul(wide[:, 2, i * HID:(i + 1) * HID], xT[:, b % 2, ck, i * P:(i + 1) * P],
                                        w_qkv[:, ck, 2 * HID:3 * HID], start=ck == 0, stop=ck == DC - 1)
                ins.then_inc(projected, 1)

            def attend(b):
                pe.wait_ge(keys_ready, b + 1)
                for i in range(TT):
                    ins = pe.transpose(wide[:, 3, i * P:(i + 1) * P], ek[:, b % 2, i * P:(i + 1) * P], ident[:, :])
                ins.then_inc(keys_turned, 1)
                pe.wait_ge(keys_kept, b + 1)
                pe.wait_ge(v_ready, b + 1)
                for i in range(TT):
                    ins = pe.matmul(trio[:, 2, 0:HID], ekn[:, b % 2, i, :], vl[:, b % 2, i, :], start=i == 0,
                                    stop=i == TT - 1)
                ins.then_inc(kv_made, 1)
                pe.wait_ge(kv_ready, b + 1)
                pe.wait_ge(q_ready, b + 1)
                pe.matmul(pv_ps[:, :], kv_bd[:, b % 2, :], qT[:, b % 2, :], start=True, stop=True).then_inc(o_made, 1)
                pe.wait_ge(o_kept, b + 1)
                for i in range(TT):
                    bank = trio[:, i // 2, (i % 2) * D:(i % 2 + 1) * D]
                    pe.matmul(bank, loT[:, b % 2, i * P:(i + 1) * P], w_lout[:, :], start=True, stop=False)
                    ins = pe.matmul(bank, ones_row[:, :], b_lout[:, :], start=False, stop=True)
                ins.then_inc(out_made, 1)

            turn(0)
            project(0)
            turn(1)
            attend(0)
            project(1)
            turn(2)
            attend(1)
            project(2)
            turn(3)
            turn(4)
            turn(5)
            attend(2)
            project(3)
            attend(3)
            turn(6)
            turn(7)

        @block.scalar
        def _(act):
            act.wait_ge(weights_in, WEIGHTS * 16)

            def keep_turned(n):
                act.wait_ge(turned, n + 1)
                b = n % B
                for ck in range(DC):
                    if n < B:
                        ins = act.activation(xT[:, b % 2, ck, :], wide[:, ck, :], ACT.Identity, bias=beta[:, ck:ck + 1],
                                             scale=gamma[:, ck:ck + 1])
                    else:
                        ins = act.activation(h2T[:, b, ck, :], wide[:, ck, :], ACT.Copy)
                ins.then_inc(turn_kept, 1)
                if n >= B:
                    act.wait_ge(turn_kept, n + 1)
                    act.sem_inc(h2_ready, 1)

            def keys(b):
                act.wait_ge(kmax_ready, b + 1)
                act.activation(ek[:, b % 2, :], trio[:, 0, :], ACT.Exp, bias=kmax[:, b:b + 1],
                               accum_out=ksum[:, b:b + 1]).then_inc(keys_ready, 1)
                act.activation(qT[:, b % 2, :], trio[:, 1, :], ACT.Copy, scale=LSCALE).then_inc(q_ready, 1)

            def keep(b):
                act.wait_ge(keys_turned, b + 1)
                act.activation(ekn[:, b % 2, :, :].rearrange("p t h -> p (t h)"), wide[:, 3, :], ACT.Copy)\
                   .then_inc(keys_kept, 1)
                act.wait_ge(o_made, b + 1)
                act.activation(loT[:, b % 2, :], pv_ps[:, :], ACT.Copy).then_inc(o_kept, 1)

            keep_turned(0)
            keys(0)
            keep_turned(1)
            keep(0)
            keys(1)
            keep_turned(2)
            keep(1)
            keys(2)
            keep_turned(3)
            keep_turned(4)
            keep_turned(5)
            keep(2)
            keys(3)
            keep(3)
            keep_turned(6)
            keep_turned(7)

        @block.vector
        def _(dve):
            chain = Chain(dve, steps, 0, 114)
            dve.wait_ge(consts, CONSTS)

            def tiles(buf, half):
                return [buf[:, half * HALF + i, :] for i in range(HALF)]

            def norm_twice(half):
                for b in range(half * B // 2, (half + 1) * B // 2):
                    dve.wait_ge(x_in[b], 16)
                moments(dve, chain, stats, mv, rstd[:, :], newton[:, :], tiles(x, half), LN_EPS)
                chain.link(normalise(dve, mv, rstd, tiles(xn0, half), tiles(x, half)))
                moments(dve, chain, stats, mv, rstd[:, :], newton[:, :], tiles(xn0, half), LN_EPS)
                chain.link(normalise(dve, mv, rstd, tiles(xn, half), tiles(xn0, half)))
                dve.sem_inc(ln_ready, 1)

            def norm_out(half):
                dve.wait_ge(turned, (half + 1) * B // 2)
                moments(dve, chain, stats, mv, rstd[:, :], newton[:, :], tiles(xn0, half), LN_EPS)
                chain.link(normalise(dve, mv, rstd, tiles(xn, half), tiles(xn0, half)))
                dve.sem_inc(ln_ready, 1)

            def key_max(b):
                dve.wait_ge(projected, b + 1)
                dve.tensor_reduce(kmax[:, b:b + 1], trio[:, 0, :], AX.X, ALU.max, negate=True).then_inc(kmax_ready, 1)
                dve.tensor_copy(vl[:, b % 2, :, :].rearrange("p t h -> p (t h)"), wide[:, 2, :]).then_inc(v_ready, 1)

            def rest(b):
                dve.wait_ge(keys_ready, b + 1)
                chain.link(dve.reciprocal(ksum_r[:, b:b + 1], ksum[:, b:b + 1]))
                dve.wait_ge(kv_made, b + 1)
                for h in range(LHEADS):
                    r = slice(h * LHEAD, (h + 1) * LHEAD)
                    ins = dve.tensor_scalar(kv_bd[r, b % 2, r], trio[r, 2, r], ksum_r[r, b:b + 1], None, ALU.mult)
                ins.then_inc(kv_ready, 1)
                dve.wait_ge(out_made, b + 1)
                rows = slice(b * TT, (b + 1) * TT)
                flat = xn0[:, rows, :].rearrange("p t d -> p (t d)")
                chain.link(dve.tensor_tensor(flat, trio[:, 0:2, :].rearrange("p n d -> p (n d)"), flat, ALU.add))
                chain.link(dve.tensor_tensor(xn0[:, rows, :], xn0[:, rows, :], x[:, rows, :], ALU.add))
                dve.sem_inc(x1_ready, 1)

            norm_twice(0)
            key_max(0)
            norm_twice(1)
            rest(0)
            key_max(1)
            rest(1)
            key_max(2)
            norm_out(0)
            rest(2)
            key_max(3)
            rest(3)
            norm_out(1)
            chain.close()


def cross_attention(nc, A, c):
    (B, S, D, TT, DC, CC, CTX_LEN, HG, GROUPS, GW, PAIRS, KT, LASTC, LASTK, KB, KCOL, KPAD, DH, RAW,
     HIRING, LORING, LAG, SIMS, FIRST_MAX_AT, MAX_AT, TURN_AT, INNER, XSCALE, LN_EPS, X_EPS) = (c[k] for k in (
        "B", "S", "D", "TT", "DC", "CC", "CTX_LEN", "HG", "GROUPS", "GW", "PAIRS", "KT", "LASTC", "LASTK", "KB",
        "KCOL", "KPAD", "DH", "RAW", "HIRING", "LORING", "LAG", "SIMS", "FIRST_MAX_AT", "MAX_AT", "TURN_AT", "INNER", "XSCALE",
        "LN_EPS", "X_EPS"))
    wide, trio, pv_ps, ident = (c[k] for k in ("wide", "trio", "pv_ps", "ident"))
    x1_dram, h2_dram, x2_dram, h3_dram = (c[k] for k in ("x1_dram", "h2_dram", "x2_dram", "h3_dram"))
    CRING = RAW + 2 * PAIRS
    VRAW = 4
    WRING = 2
    CHUNKS = 2 * CC
    NULL_ROWS = slice(LASTC // 32 * 32, LASTK)
    ONES = 32
    T = B * GROUPS
    BANKS = PAIRS * KB
    BANK_ORDER = (1, 2, 3, 0)
    NORM_AT = (4, 6, 8, 10)
    ON_DVE = [k for k in range(KT) if k % 2 == 0]
    ON_POOL = [k for k in range(KT) if k % 2 == 1]
    W_TILES = [n for n in range(2, SIMS) if n % KT not in ON_POOL][:2 * CHUNKS]
    assert len(W_TILES) == 2 * CHUNKS and KB == 4 and RAW * S >= TT * D + 2 * D

    with ExitStack() as scope:
        def sb(name, shape, dt=F32):
            return scope.enter_context(nc.sbuf_tensor(name, shape, dt))

        def sem(name):
            return scope.enter_context(nc.semaphore(name))

        null_k = sb("null_k", [DH, 1])
        zero = sb("zero", [P, 1])
        acc = sb("acc", [P, TT, D])
        null_v = acc[:, 0, 0:DH]
        null_wide = acc[0:DH, 1, 0:HG * (KPAD - CTX_LEN)].rearrange("p (j n) -> p j n", j=HG)
        xT = sb("h2T_in", [P, DC, S])
        stats = sb("x_stats", [P, TT, 6])
        mv = sb("x_mv", [P, TT, 2])
        rstd = sb("x_rstd", [P, TT])
        newton = sb("x_newton", [P, TT])
        c_hi = sb("c_hi", [P, CC, KPAD], F32R)
        c_lo = sb("c_lo", [P, CC, KPAD], F32R)
        wq = sb("wq", [P, DC, GW])
        wo = sb("wo", [P, PAIRS, D])
        w_in = sb("w_in", [P, WRING, GW])
        w_hi, w_lo = sb("w_hi", [P, 2, CC, GW], F32R), sb("w_lo", [P, 2, CC, GW], F32R)
        q_hi = sb("q_hi", [P, HG, S], F32R)
        q_lo = sb("q_lo", [P, HG, S], F32R)
        k_hl = sb("k_hl", [P, HG, KPAD], F32R)
        k_h1 = sb("k_h1", [P, HG, KPAD], F32R)
        v_one = sb("v_one", [P, KT, HG, DH + ONES], F32R)
        v_lo = sb("v_lo", [P, KT, HG, DH], F32R)
        probs = sb("probs", [P, RAW, S])
        p_hi = sb("p_hi", [P, HIRING, S], F32R)
        p_lo = sb("p_lo", [P, LORING, S], F32R)
        neg_max = sb("neg_max", [P, 2, TT])
        den_pair = sb("den_pair", [P, PAIRS, S])
        oT = sb("oT", [P, PAIRS, S])
        ctx_in = [probs[:, n, :] for n in range(RAW)] + [b_[:, n, :] for b_ in (den_pair, oT) for n in range(PAIRS)]
        x1 = probs[:, 0:2, :].rearrange("p a (i d) -> p (a i) d", d=D)
        ln_scale, ln_bias = probs[:, 2, 0:D], probs[:, 2, D:2 * D]
        v_raw = oT[:, :, :].rearrange("p h (n d) -> p (h n) d", d=GW)

        pool_step, consts_in, null_ready = sem("pool_step"), sem("consts_in"), sem("null_ready")
        h2_in, x1_in, rows_stored = sem("h2_in"), sem("x1_in"), sem("rows_stored")
        ctx_in_s = [sem(f"ctx_in_{k}") for k in range(KT)]
        wq_in_s, wo_in_s = sem("wq_in_s"), sem("wo_in_s")
        w_in_s = [sem(f"w_in_{k}") for k in range(WRING)]
        w_rounded, w_split = sem("w_rounded"), sem("w_split")
        dve_batch, dve_norm = sem("dve_batch"), sem("dve_norm")
        ctx_turned, c_rounded, c_split = sem("ctx_turned"), sem("c_rounded"), sem("c_split")
        q_made, q_rounded, q_split = sem("q_made"), sem("q_rounded"), sem("q_split")
        k_made, k_rounded, k_split = sem("k_made"), sem("k_rounded"), sem("k_split")
        v_made, v_kept, v_split = sem("v_made"), sem("v_kept"), sem("v_split")
        max_scores, max_taken, max_turned, max_row = (
            sem("max_scores"), sem("max_taken"), sem("max_turned"), sem("max_row"))
        scores_ready, probs_ready, p_rounded, split_dve, split_pool, probs_used = (
            sem("scores_ready"), sem("probs_ready"), sem("p_rounded"), sem("split_dve"), sem("split_pool"),
            sem("probs_used"))
        o_kept, o_normed, x_out, acc_added = sem("o_kept"), sem("o_normed"), sem("x_out"), sem("acc_added")
        x2_ready, h3_ready = sem("x2_ready"), sem("h3_ready")

        block = scope.enter_context(nc.Block())
        w_v = A["L0_xattn_Wq"].rearrange("(c p) f -> p c f", p=P)
        wo_v = A["L0_xattn_Wout"].rearrange("(g h p) f -> g p h f", p=P, h=PAIRS)
        CONSTS_IN = 2
        POOL_STEPS = 12
        NULLS = 4
        FINISH = 37
        acc_rows = [acc[:, i, :] for i in range(TT)]

        def split_by(n, t):
            j, k = divmod(n, KT)
            s, tiles = (split_dve, ON_DVE) if k in ON_DVE else (split_pool, ON_POOL)
            return s, (t * HG + j) * len(tiles) + tiles.index(k) + 1

        def rows_of(k):
            return P if k < KT - 1 else LASTK

        @block.sync
        def _(sp):
            def load_chunk(t, g, i):
                w, ck = divmod(i, CC)
                sp.dma_start(w_in[:, i % WRING, :],
                             A["L0_xattn_Wkv"][ck * P:(ck + 1) * P, bass.ds(g * GW + w * INNER, GW)])\
                  .then_inc(w_in_s[i % WRING], 16)

            def load_ctx(b, k):
                sp.wait_ge(ctx_turned, b * KT + max(k - CRING + 1, 0) + CRING)
                rows = P if k < KT - 1 else LASTC
                ctx_b = A["ctx_2048"][bass.ds(b, 1)].rearrange("a s d -> (a s) d")
                sp.dma_start(ctx_in[k % CRING][0:rows, :], ctx_b[k * P:k * P + rows, :]).then_inc(ctx_in_s[k], 16)

            def load_h2(b):
                sp.dma_start(xT[:, :, :].rearrange("p c s -> p (c s)"),
                             h2_dram[bass.ds(b, 1)].rearrange("a p n -> (a p) n")).then_inc(h2_in, 16)

            def load_weights(b):
                with sp.Fori(0, GROUPS) as g:
                    t = b * GROUPS + g
                    after = (g + 1) % GROUPS
                    sp.wait_ge(q_made, (t + 1) * PAIRS)
                    sp.dma_start(wq[:, :, :], w_v[:, :, bass.ds(after * GW, GW)]).then_inc(wq_in_s, 16)
                    sp.wait_ge(x_out, t + 1)
                    sp.dma_start(wo[:, :, :], wo_v[bass.ds(g, 1)].rearrange("a p h f -> p (a h) f")).then_inc(wo_in_s, 16)
                    for i in range(CHUNKS):
                        sp.wait_ge(w_split, (t + 1) * CHUNKS + i - WRING + 1)
                        load_chunk(t + 1, after, i)
                after = (b + 1) % B
                sp.wait_ge(q_made, (b + 1) * GROUPS * PAIRS)
                load_h2(after)

            def probs_free(t):
                sp.wait_ge(probs_used, t * SIMS + HIRING)

            def finish_rows(b):
                sp.dma_start(x1, x1_dram[bass.ds(b, 1)].rearrange("a (t p) d -> p (a t) d", p=P)).then_inc(x1_in, 16)
                for dst, src in ((ln_scale, "L0_xattn_ln_scale"), (ln_bias, "L0_xattn_ln_bias")):
                    sp.dma_start(dst, A[src].rearrange("(a d) -> a d", a=1).to_broadcast([P, D])).then_inc(x1_in, 16)
                for buf, ready, rows in ((x1, x2_ready, x2_dram), (acc[:, :, :], h3_ready, h3_dram)):
                    sp.wait_ge(ready, b + 1)
                    sp.dma_start(rows[bass.ds(b, 1)].rearrange("a (t p) d -> p (a t) d", p=P), buf)\
                      .then_inc(rows_stored, 16)

            with nc.allow_non_contiguous_dma(reason="a column of the head dimension on partitions"):
                sp.dma_start(null_k[:, :], A["L0_xattn_null_kv"][0:1, :].rearrange("a d -> d a")).then_inc(consts_in, 16)
            sp.wait_ge(pool_step, 1)
            sp.dma_start(null_v[LASTC:LASTK, :], A["L0_xattn_null_kv"][1:2, :]).then_inc(consts_in, 16)
            load_h2(0)
            sp.dma_start(wq[:, :, :], w_v[:, :, 0:GW]).then_inc(wq_in_s, 16)
            for k in range(KT):
                load_ctx(0, k)
                if k < CHUNKS:
                    if k >= WRING:
                        sp.wait_ge(w_split, k - WRING + 1)
                    load_chunk(0, 0, k)
            load_weights(0)
            with sp.Fori(1, B) as b:
                probs_free(b * GROUPS)
                for k in range(KT):
                    if k == RAW:
                        sp.wait_ge(x_out, b * GROUPS + 1)
                    load_ctx(b, k)
                sp.wait_ge(ctx_turned, (b + 1) * KT + CRING)
                finish_rows(b - 1)
                load_weights(b)
            probs_free(T)
            finish_rows(B - 1)
            sp.wait_ge(rows_stored, B * 32 + 1)
            sp.wait_ge(h2_in, (B + 1) * 16)
            sp.wait_ge(wq_in_s, (T + 1) * 16)
            for k in range(WRING):
                sp.wait_ge(w_in_s[k], (T + 1) * CHUNKS // WRING * 16)

        @block.gpsimd
        def _(pool):
            for n, (dst, value) in enumerate((
                (null_v, 0.0),
                (zero[:, :], 0.0),
                (v_one[:, KT - 1, :, :].bitcast(F32), 0.0),
                (v_one[0:LASTK, KT - 1, :, DH:DH + ONES].bitcast(F32), 1.0),
                (v_one[:, 0:KT - 1, :, DH:DH + ONES].bitcast(F32), 1.0),
                (v_lo[:, KT - 1, :, :].bitcast(F32), 0.0),
                (null_wide, 0.0),
                (q_lo[DH:P, :, :].bitcast(F32), 0.0),
                (k_h1[DH:P, :, :].bitcast(F32), 0.0),
                (k_h1[DH:DH + 1, :, :].bitcast(F32), 1.0),
                (c_hi[:, :, CTX_LEN:KPAD].bitcast(F32), 0.0),
                (c_lo[:, :, CTX_LEN:KPAD].bitcast(F32), 0.0),
            )):
                pool.memset(dst, value).then_inc(pool_step, 1)
                pool.wait_ge(pool_step, n + 1)

            def split_weights(t, n):
                i, low = divmod(n, 2)
                src, hi, lo = w_in[:, i % WRING, :], w_hi[:, i // CC, i % CC, :], w_lo[:, i // CC, i % CC, :]
                if low:
                    pool.wait_ge(w_rounded, t * CHUNKS + i + 1)
                    pool.tensor_tensor(lo, src, hi.bitcast(F32), ALU.subtract).then_inc(w_split, 1)
                else:
                    pool.wait_ge(w_in_s[i % WRING], (t * (CHUNKS // WRING) + i // WRING + 1) * 16)
                    pool.tensor_tensor(hi, src, zero[:, :].to_broadcast([P, GW]), ALU.add).then_inc(w_rounded, 1)

            for n in range(2 * CHUNKS):
                split_weights(0, n)
            with pool.Fori(0, T) as t:
                for k in range(KT):
                    pool.wait_ge(v_kept, t * KT + k + 1)
                    rows = P if k < KT - 1 else LASTC
                    pool.tensor_tensor(v_lo[0:rows, k, :, :],
                                       v_raw[0:rows, k % VRAW, :].rearrange("p (j d) -> p j d", j=HG),
                                       v_one[0:rows, k, :, 0:DH].bitcast(F32), ALU.subtract).then_inc(v_split, 1)
                for n in range(SIMS):
                    k = n % KT
                    if k in ON_POOL:
                        pool.wait_ge(p_rounded, t * SIMS + n + 1)
                        pool.wait_ge(probs_used, t * SIMS + n + 1 - LORING + HIRING)
                        pool.tensor_tensor(p_lo[0:rows_of(k), n % LORING, :], probs[0:rows_of(k), n % RAW, :],
                                           p_hi[0:rows_of(k), n % HIRING, :].bitcast(F32), ALU.subtract)\
                            .then_inc(split_pool, 1)
                    if n in W_TILES:
                        split_weights(t + 1, W_TILES.index(n))

        @block.tensor
        def _(pe):
            pe.sem_inc(ctx_turned, CRING)
            pe.sem_inc(x_out, 1)
            pe.sem_inc(probs_used, HIRING)
            pe.wait_ge(null_ready, NULLS)

            def products(out_, hi, lo, hi2, lo2):
                terms = ((hi, hi2), (hi, lo2), (lo, hi2))
                for ck in range(CC):
                    for n, (w, m) in enumerate(terms):
                        ins = pe.matmul(out_, w(ck), m(ck), start=ck == 0 and n == 0, stop=ck == CC - 1 and n == 2)
                return ins

            def queries(t, batch):
                pe.wait_ge(h2_in, batch * 16 + 16)
                pe.wait_ge(wq_in_s, t * 16 + 16)
                for p in range(PAIRS):
                    for ck in range(DC):
                        ins = pe.matmul(trio[:, p, :], wq[:, ck, p * P:(p + 1) * P], xT[:, ck, :],
                                        start=ck == 0, stop=ck == DC - 1)
                    ins.then_inc(q_made, 1)

            queries(0, 0)
            with pe.Fori(0, B) as b:
                for k in range(KT):
                    rows = P if k < KT - 1 else LASTC
                    pe.wait_ge(ctx_in_s[k], b * 16 + 16)
                    if k == 0:
                        pe.wait_ge(q_split, (b * GROUPS + 1) * PAIRS)
                        pe.wait_ge(acc_added, b * GROUPS + 1)
                    if k >= 3:
                        pe.wait_ge(c_split, b * KT + k - 2)
                    for ck in range(CC):
                        ins = pe.transpose(trio[:, k % 3, ck * P:ck * P + rows],
                                           ctx_in[k % CRING][0:rows, ck * P:(ck + 1) * P], ident[0:rows, 0:rows])
                    ins.then_inc(ctx_turned, 1)

                with pe.Fori(0, GROUPS) as g:
                    t = b * GROUPS + g

                    def keys(p):
                        for n in range(KB):
                            if p >= 1 and BANK_ORDER[n] == 0:
                                pe.wait_ge(max_row, t * HG + 1)
                            m = BANK_ORDER[n]
                            cols = slice(m * KCOL, (m + 1) * KCOL)
                            products(wide[:, m, 0:KCOL], lambda ck: w_hi[:, 0, ck, p * P:(p + 1) * P],
                                     lambda ck: w_lo[:, 0, ck, p * P:(p + 1) * P], lambda ck: c_hi[:, ck, cols],
                                     lambda ck: c_lo[:, ck, cols]).then_inc(k_made, 1)

                    def values(k):
                        if k == 0:
                            pe.wait_ge(q_split, (t + 1) * PAIRS)
                            pe.wait_ge(acc_added, t + 1)
                        elif k >= 3:
                            pe.wait_ge(v_kept, t * KT + k - 2)
                        rows = P if k < KT - 1 else LASTC
                        cols = slice(k * P, k * P + rows)
                        products(trio[0:rows, k % 3, 0:GW], lambda ck: c_hi[:, ck, cols], lambda ck: c_lo[:, ck, cols],
                                 lambda ck: w_hi[:, 1, ck, :], lambda ck: w_lo[:, 1, ck, :]).then_inc(v_made, 1)

                    def scores_for_max(j, i):
                        if i:
                            pe.wait_ge(max_taken, t * HG * TT + j * TT + i)
                        elif j:
                            pe.wait_ge(max_row, t * HG + j)
                        for n in range(KB):
                            ins = pe.matmul(wide[:, n, 0:KCOL], q_hi[:, j, i * P:(i + 1) * P],
                                            k_hl[:, j, n * KCOL:(n + 1) * KCOL], start=True, stop=True)
                        ins.then_inc(max_scores, 1)

                    def turn_max(j):
                        pe.wait_ge(max_taken, t * HG * TT + (j + 1) * TT)
                        for i in range(TT):
                            ins = pe.transpose(wide[0:1, 0, i * P:(i + 1) * P], neg_max[:, j % 2, i:i + 1], ident[:, :])
                        ins.then_inc(max_turned, 1)

                    def scores(n):
                        j, k = divmod(n, KT)
                        if k == 0:
                            pe.wait_ge(max_row, t * HG + j + 1)
                        if n >= 3:
                            pe.wait_ge(p_rounded, t * SIMS + n - 2)
                        cols = slice(k * P, k * P + rows_of(k))
                        bank = trio[0:rows_of(k), n % 3, :]
                        pe.matmul(bank, k_hl[:, j, cols], q_hi[:, j, :], start=True, stop=False)
                        pe.matmul(bank, k_h1[:, j, cols], q_lo[:, j, :], start=False, stop=True).then_inc(scores_ready, 1)

                    def weigh(n):
                        j, k = divmod(n, KT)
                        pe.wait_ge(*split_by(n, t))
                        if k == 0:
                            pe.wait_ge(o_kept, t * HG + j + 1)
                        made = pv_ps[0:DH + ONES, :]
                        pe.matmul(made, v_one[:, k, j, :], p_hi[:, n % HIRING, :], start=k == 0, stop=False)
                        pe.matmul(pv_ps[0:DH, :], v_lo[:, k, j, :], p_hi[:, n % HIRING, :], start=False, stop=False)
                        pe.matmul(made, v_one[:, k, j, :], p_lo[:, n % LORING, :], start=False, stop=k == KT - 1)\
                          .then_inc(probs_used, 1)

                    def ahead(n):
                        return n // KT >= 1 and n % KT == LAG

                    pe.wait_ge(c_split, (b + 1) * KT)
                    pe.wait_ge(w_split, (t + 1) * CHUNKS)
                    keys(0)
                    for k in range(KT):
                        values(k)
                        if k == FIRST_MAX_AT[0]:
                            pe.wait_ge(k_split, t * BANKS + KB)
                        if k in FIRST_MAX_AT:
                            scores_for_max(0, FIRST_MAX_AT.index(k))
                    turn_max(0)
                    keys(1)
                    pe.wait_ge(v_kept, (t + 1) * KT)
                    pe.wait_ge(v_split, (t + 1) * KT)
                    for n in range(SIMS):
                        j, k = divmod(n, KT)
                        if not ahead(n - 1):
                            scores(n)
                        if j + 1 < HG:
                            if k in MAX_AT:
                                if k == MAX_AT[0] and j == 0:
                                    pe.wait_ge(k_split, (t + 1) * BANKS)
                                scores_for_max(j + 1, MAX_AT.index(k))
                            if k == TURN_AT:
                                turn_max(j + 1)
                        if ahead(n):
                            scores(n + 1)
                        if n >= LAG:
                            weigh(n - LAG)
                    for n in range(SIMS - LAG, SIMS):
                        weigh(n)
                    queries(t + 1, (t + 1) // GROUPS)
                    pe.wait_ge(wo_in_s, t * 16 + 16)
                    for i in range(TT):
                        pe.wait_ge(o_normed, (t + 1) * PAIRS * TT - TT + i + 1)
                        bank = (trio[:, 2, :], pv_ps[:, :])[i // 2]
                        for h in range(PAIRS):
                            ins = pe.matmul(bank[:, (i % 2) * D:(i % 2 + 1) * D], oT[:, h, i * P:(i + 1) * P], wo[:, h, :],
                                            start=h == 0, stop=h == PAIRS - 1)
                    ins.then_inc(x_out, 1)

        @block.scalar
        def _(act):
            act.sem_inc(o_kept, 1)

            def round_queries(t):
                for p in range(PAIRS):
                    act.wait_ge(q_made, t * PAIRS + p + 1)
                    for n in range(2):
                        j, rows = 2 * p + n, slice(n * DH, (n + 1) * DH)
                        for half in range(2):
                            ins = act.activation(q_hi[half * DH:(half + 1) * DH, j, :], trio[rows, p, :], ACT.Copy,
                                                 scale=XSCALE)
                    ins.then_inc(q_rounded, 1)

            act.wait_ge(null_ready, NULLS)
            round_queries(0)
            with act.Fori(0, B) as b:
                for k in range(KT):
                    act.wait_ge(ctx_turned, b * KT + k + 1 + CRING)
                    rows = P if k < KT - 1 else LASTC
                    act.activation(c_hi[:, :, k * P:k * P + rows],
                                   trio[:, k % 3, :].rearrange("p (c n) -> p c n", c=CC)[:, :, 0:rows],
                                   ACT.Copy).then_inc(c_rounded, 1)
                with act.Fori(0, GROUPS) as g:
                    t = b * GROUPS + g

                    def round_keys(p):
                        for n in range(KB):
                            m = BANK_ORDER[n]
                            act.wait_ge(k_made, t * BANKS + p * KB + n + 1)
                            cols = slice(m * KCOL, min((m + 1) * KCOL, CTX_LEN))
                            for dst in (k_hl, k_h1):
                                for half in range(2):
                                    j, rows = 2 * p + half, slice(half * DH, (half + 1) * DH)
                                    ins = act.activation(dst[0:DH, j, cols], wide[rows, m, 0:cols.stop - cols.start],
                                                         ACT.Copy)
                            ins.then_inc(k_rounded, 1)

                    def keep_o(j):
                        act.wait_ge(probs_used, t * SIMS + (j + 1) * KT + HIRING)
                        rows = (j % 2) * DH
                        act.activation(oT[rows:rows + DH, j // 2, :], pv_ps[0:DH, :], ACT.Copy)
                        for r in range(rows, rows + DH, ONES):
                            ins = act.activation(den_pair[r:r + ONES, j // 2, :], pv_ps[DH:DH + ONES, :], ACT.Copy)
                        ins.then_inc(o_kept, 1)

                    round_keys(0)
                    for k in range(KT):
                        act.wait_ge(v_made, t * KT + k + 1)
                        if k >= VRAW:
                            act.wait_ge(v_split, t * KT + k - VRAW + 1)
                        rows = P if k < KT - 1 else LASTC
                        act.activation(v_raw[0:rows, k % VRAW, :], trio[0:rows, k % 3, 0:GW], ACT.Copy)
                        act.activation(v_one[0:rows, k, :, 0:DH],
                                       trio[0:rows, k % 3, 0:GW].rearrange("p (j d) -> p j d", j=HG), ACT.Copy).then_inc(v_kept, 1)
                    round_keys(1)
                    act.wait_ge(rows_stored, b * 32 + 1)
                    for n in range(SIMS):
                        j, k = divmod(n, KT)
                        act.wait_ge(scores_ready, t * SIMS + n + 1)
                        if k == LAG and j >= 1:
                            keep_o(j - 1)
                        if n >= RAW:
                            act.wait_ge(*split_by(n - RAW, t))
                        bank = trio[0:rows_of(k), n % 3, :]
                        act.activation(probs[0:rows_of(k), n % RAW, :], bank, ACT.Exp).then_inc(probs_ready, 1)
                        act.wait_ge(probs_used, t * SIMS + n + 1)
                        act.activation(p_hi[0:rows_of(k), n % HIRING, :], bank, ACT.Exp).then_inc(p_rounded, 1)
                    keep_o(HG - 1)
                    round_queries(t + 1)

        @block.vector
        def _(dve):
            dve.sem_inc(rows_stored, 1)
            dve.wait_ge(consts_in, CONSTS_IN * 16)
            dve.wait_ge(pool_step, POOL_STEPS)
            dve.tensor_scalar(null_wide, null_wide, null_k[:, 0:1], None, ALU.add).then_inc(null_ready, 1)
            dve.wait_ge(null_ready, 1)
            dve.tensor_copy(k_hl[0:DH, :, CTX_LEN:KPAD], null_wide)
            dve.tensor_copy(k_h1[0:DH, :, CTX_LEN:KPAD], null_wide).then_inc(null_ready, 1)
            for j in range(HG):
                ins = dve.tensor_copy(v_one[NULL_ROWS, KT - 1, j, 0:DH], null_v[NULL_ROWS, :])
            ins.then_inc(null_ready, 1)
            dve.wait_ge(null_ready, 3)
            for j in range(HG):
                dve.tensor_tensor(v_lo[NULL_ROWS, KT - 1, j, :], null_v[NULL_ROWS, :],
                                  v_one[NULL_ROWS, KT - 1, j, 0:DH].bitcast(F32), ALU.subtract)
            dve.tensor_tensor(k_hl[DH:P, :, CTX_LEN:KPAD], null_wide, k_hl[0:DH, :, CTX_LEN:KPAD].bitcast(F32),
                              ALU.subtract).then_inc(null_ready, 1)

            def split_queries(t):
                for p in range(PAIRS):
                    dve.wait_ge(q_rounded, t * PAIRS + p + 1)
                    for n in range(2):
                        j, rows = 2 * p + n, slice(n * DH, (n + 1) * DH)
                        ins = dve.scalar_tensor_tensor(out=q_lo[0:DH, j, :], in0=trio[rows, p, :], scalar=XSCALE,
                                                       in1=q_hi[0:DH, j, :].bitcast(F32), op0=ALU.mult,
                                                       op1=ALU.subtract)
                    ins.then_inc(q_split, 1)

            def split_context(b):
                for k in range(KT):
                    dve.wait_ge(c_rounded, b * KT + k + 1)
                    rows = P if k < KT - 1 else LASTC
                    cols = slice(k * P, k * P + rows)
                    dve.tensor_tensor(c_lo[:, :, cols], trio[:, k % 3, :].rearrange("p (c n) -> p c n", c=CC)[:, :, 0:rows],
                                      c_hi[:, :, cols].bitcast(F32), ALU.subtract).then_inc(c_split, 1)

            def norm_rows(b):
                chain = Chain(dve, dve_batch, b, FINISH)
                dve.wait_ge(acc_added, (b + 1) * GROUPS + 1)
                moments(dve, chain, stats, mv, rstd[:, :], newton[:, :], acc_rows, X_EPS)
                chain.link(normalise(dve, mv, rstd, acc_rows, acc_rows))
                return chain

            def finish_rows(b, chain):
                dve.wait_ge(x1_in, (b + 1) * 48)
                for i in range(TT):
                    ins = dve.tensor_tensor(acc[:, i, :], acc[:, i, :], ln_scale, ALU.mult)
                chain.link(ins)
                for i in range(TT):
                    ins = dve.tensor_tensor(acc[:, i, :], acc[:, i, :], ln_bias, ALU.add)
                chain.link(ins)
                chain.link(dve.tensor_tensor(x1, x1, acc[:, :, :], ALU.add))
                dve.sem_inc(x2_ready, 1)
                out_rows = [x1[:, i, :] for i in range(TT)]
                moments(dve, chain, stats, mv, rstd[:, :], newton[:, :], out_rows, LN_EPS)
                chain.link(normalise(dve, mv, rstd, acc_rows, out_rows))
                dve.sem_inc(h3_ready, 1)
                chain.close()

            def split_keys(t, p):
                for n in range(KB):
                    m = BANK_ORDER[n]
                    dve.wait_ge(k_rounded, t * BANKS + p * KB + n + 1)
                    cols = slice(m * KCOL, min((m + 1) * KCOL, CTX_LEN))
                    for half in range(2):
                        j, rows = 2 * p + half, slice(half * DH, (half + 1) * DH)
                        ins = dve.tensor_tensor(k_hl[DH:P, j, cols], wide[rows, m, 0:cols.stop - cols.start],
                                                k_hl[0:DH, j, cols].bitcast(F32), ALU.subtract)
                    ins.then_inc(k_split, 1)

            def take_max(t, j, i):
                dve.wait_ge(max_scores, t * HG * TT + j * TT + i + 1)
                dve.tensor_reduce(neg_max[:, j % 2, i:i + 1], wide[:, :, 0:KCOL], AX.XY, ALU.max,
                                  negate=True).then_inc(max_taken, 1)

            def keep_max(t, j):
                dve.wait_ge(max_turned, t * HG + j + 1)
                dve.tensor_copy(q_lo[DH:DH + 1, j, :], wide[0:1, 0, :]).then_inc(max_row, 1)

            def split_probs(t, n):
                k = n % KT
                if k in ON_DVE:
                    dve.wait_ge(p_rounded, t * SIMS + n + 1)
                    dve.wait_ge(probs_used, t * SIMS + n + 1 - LORING + HIRING)
                    dve.tensor_tensor(p_lo[0:rows_of(k), n % LORING, :], probs[0:rows_of(k), n % RAW, :],
                                      p_hi[0:rows_of(k), n % HIRING, :].bitcast(F32), ALU.subtract).then_inc(split_dve, 1)

            def norm(t, h, i):
                cols = slice(i * P, (i + 1) * P)
                if i == 0:
                    dve.wait_ge(o_kept, t * HG + 2 * h + 3)
                dve.reciprocal(den_pair[:, h, cols], den_pair[:, h, cols]).then_inc(dve_norm, 1)
                dve.wait_ge(dve_norm, (t * PAIRS + h) * TT + i + 1)
                dve.tensor_tensor(oT[:, h, cols], oT[:, h, cols], den_pair[:, h, cols], ALU.mult).then_inc(o_normed, 1)

            def group(t, first=False, before=None):
                if before is not None:
                    chain = norm_rows(before)
                split_keys(t, 0)
                if before is not None:
                    finish_rows(before, chain)
                for i in range(TT):
                    take_max(t, 0, i)
                keep_max(t, 0)
                split_keys(t, 1)
                for n in range(SIMS):
                    j, k = divmod(n, KT)
                    if n >= 1:
                        split_probs(t, n - 1)
                    if j + 1 < HG:
                        if k in MAX_AT:
                            take_max(t, j + 1, MAX_AT.index(k))
                        if k == TURN_AT:
                            keep_max(t, j + 1)
                    elif k in NORM_AT:
                        norm(t, 0, NORM_AT.index(k))
                split_probs(t, SIMS - 1)
                for i in range(TT):
                    norm(t, 1, i)
                split_queries(t + 1)
                if before is not None:
                    dve.wait_ge(rows_stored, (before + 1) * 32 + 1)
                dve.wait_ge(acc_added, t + 1)
                dve.wait_ge(x_out, t + 2)
                for n, bank in enumerate((trio[:, 2, :], pv_ps[:, :])):
                    rows = acc[:, 2 * n:2 * n + 2, :].rearrange("p i d -> p (i d)")
                    if first:
                        ins = dve.tensor_copy(rows, bank)
                    else:
                        ins = dve.tensor_tensor(rows, rows, bank, ALU.add)
                ins.then_inc(acc_added, 1)

            dve.sem_inc(acc_added, 1)
            split_queries(0)
            split_context(0)
            group(0, True)
            with dve.Fori(1, GROUPS) as g:
                group(g)
            with dve.Fori(1, B) as b:
                split_context(b)
                group(b * GROUPS, True, b - 1)
                with dve.Fori(1, GROUPS) as g:
                    group(b * GROUPS + g)
            finish_rows(B - 1, norm_rows(B - 1))


def experts(nc, A, out, c):
    (B, S, D, NT, DC, EXPERTS, F, SHARE, CAP, FC, FL, SC, REP) = (c[k] for k in (
        "B", "S", "D", "NT", "DC", "EXPERTS", "F", "SHARE", "CAP", "FC", "FL", "SC", "REP"))
    wide, trio, pv_ps, ident = (c[k] for k in ("wide", "trio", "pv_ps", "ident"))
    x2_dram, h3_dram = c["x2_dram"], c["h3_dram"]
    N = B * S
    SHIFTS = [28, 24, 20, 16, 12, 8, 4, 0]
    FIRST_FOLD = 2

    with ExitStack() as scope:
        def sb(name, shape, dt=F32):
            return scope.enter_context(nc.sbuf_tensor(name, shape, dt))

        def sem(name):
            return scope.enter_context(nc.semaphore(name))

        x2 = sb("x2", [P, NT, D])
        h3 = sb("h3", [P, NT, D])
        h3_hi = sb("h3_hi", [P, NT, D], F32R)
        h3_lo = sb("h3_lo", [P, NT, D], F32R)
        ones_row = sb("e_ones_row", [1, P])
        w_r = sb("w_r", [P, DC, EXPERTS])
        b_r = sb("b_r", [1, EXPERTS])
        lmax = sb("lmax", [P, NT])
        lsum = sb("lsum", [P, NT])
        lexp = sb("lexp", [P, NT, EXPERTS])
        gate = sb("gate", [P, NT, EXPERTS])
        same = sb("same", [P, EXPERTS, REP])
        digit = sb("digit", [P, 1], I32)
        base = sb("base", [P, 1], I32)
        tried = sb("tried", [P, 1], I32)
        step = sb("step", [P, 1], I32)
        count = sb("count", [P, 1])
        enough = sb("enough", [P, 1])
        gateT = sb("gateT", [P, N])
        above = sb("above", [P, N])
        equal = sb("equal", [P, N])
        run = sb("run", [P, N])
        zeros = sb("zeros", [P, N])
        slot = sb("slot", [P, NT, EXPERTS + 1])
        slot_no = sb("slot_no", [P, CAP])
        slot_i = sb("slot_i", [P, CAP], I32)
        picks = sb("picks", [P, 2, NT, CAP], F32R)
        h3T = sb("h3T", [P, DC, N])
        gate_rep = sb("gate_rep", [P, NT, EXPERTS, REP])
        pickT = sb("pickT", [P, SC, N], F32R)
        w_up = sb("w_up", [P, DC, F])
        w_dn = sb("w_dn", [P, FC, D])
        b_up = sb("b_up", [P, FC])
        b_dn = sb("b_dn", [1, D])
        taken = sb("taken", [P, DC, CAP])
        mid = sb("mid", [P, FC, CAP])
        made_hi = sb("made_hi", [P, SC, D], F32R)
        made_lo = sb("made_lo", [P, SC, D], F32R)

        e_const, e_chain, router_in = sem("e_const"), sem("e_chain"), sem("router_in")
        h3_in, x2_in, h3_turned, h3_kept, h3_split = (
            sem("h3_in"), sem("x2_in"), sem("h3_turned"), sem("h3_kept"), sem("h3_split"))
        logits_ready, l_shift, l_exp = sem("logits_ready"), sem("l_shift"), sem("l_exp")
        spread, gate_turned, gate_kept, tried_count, tried_sum = (
            sem("spread"), sem("gate_turned"), sem("gate_kept"), sem("tried_count"), sem("tried_sum"))
        slots_known, slots_turned, slots_kept = sem("slots_known"), sem("slots_turned"), sem("slots_kept")
        up_in, dn_in, dn_free = sem("up_in"), sem("dn_in"), sem("dn_free")
        picked, pick_turned, pick_kept = sem("picked"), sem("pick_turned"), sem("pick_kept")
        gathered, taken_kept = sem("gathered"), sem("taken_kept")
        up_done, mid_ready, dn_done, made_rounded, made_split = (
            sem("up_done"), sem("mid_ready"), sem("dn_done"), sem("made_rounded"), sem("made_split"))
        spread_back, added = sem("spread_back"), sem("added")
        stored = sem("e_stored")

        block = scope.enter_context(nc.Block())
        TURNS = NT * SC // 4
        H_TURNS = NT * DC // 4

        @block.sync
        def _(sp):
            sp.dma_start(h3[:, :, :], h3_dram.rearrange("b (t p) d -> p (b t) d", p=P)).then_inc(h3_in, 16)
            sp.dma_start(w_r[:, :, :], A["L0_ffn_Wr"].rearrange("(c p) f -> p c f", p=P)).then_inc(router_in, 16)
            sp.dma_start(b_r[:, :], A["L0_ffn_br"].rearrange("(a d) -> a d", a=1)).then_inc(router_in, 16)
            sp.dma_start(x2[:, :, :], x2_dram.rearrange("b (t p) d -> p (b t) d", p=P)).then_inc(x2_in, 16)
            with sp.Fori(0, EXPERTS // SHARE) as g:
                sp.wait_ge(mid_ready, (g + 1) * SHARE * FC)
                up = A["L0_ffn_W_up"][bass.ds(g, 1)].rearrange("a (c p) f -> p (a c) f", p=P)
                sp.dma_start(w_up[:, :, :], up).then_inc(up_in, 16)
                bu = A["L0_ffn_b_up"][bass.ds(g, 1)]
                with nc.allow_non_contiguous_dma(reason="a column of the hidden dimension on partitions"):
                    sp.dma_start(b_up[:, 0:FC - 1], bu[:, 0:(FC - 1) * P].rearrange("a (c p) -> p (a c)", p=P))\
                      .then_inc(up_in, 16)
                    sp.dma_start(b_up[0:FL, FC - 1:FC], bu[:, (FC - 1) * P:F].rearrange("a p -> p a")).then_inc(up_in, 16)
                for n in range(SHARE):
                    e = g * SHARE + n
                    sp.wait_ge(dn_done, e + 1)
                    dn = A["L0_ffn_W_down"][bass.ds(e, 1)].rearrange("a f d -> (a f) d")
                    sp.dma_start(w_dn[:, 0:FC - 1, :], dn[0:(FC - 1) * P, :].rearrange("(c p) d -> p c d", p=P))\
                      .then_inc(dn_in, 16)
                    sp.dma_start(w_dn[0:FL, FC - 1, :], dn[(FC - 1) * P:F, :]).then_inc(dn_in, 16)
                    sp.dma_start(b_dn[:, :], A["L0_ffn_b_down"][bass.ds(e, 1)]).then_inc(dn_in, 16)
            sp.wait_ge(added, EXPERTS * NT)
            sp.dma_start(out.rearrange("b (t p) d -> p (b t) d", p=P), x2[:, :, :]).then_inc(stored, 16)
            sp.wait_ge(stored, 16)

        @block.gpsimd
        def _(pool):
            n = 0

            def link(ins):
                nonlocal n
                n += 1
                ins.then_inc(e_const, 1)
                pool.wait_ge(e_const, n)

            link(pool.memset(ones_row[:, :], 1.0))
            link(pool.memset(same[:, :, :], 1.0))
            link(pool.affine_select(out=same[:, :, :], in_=same[:, :, :], compare_op=ALU.is_ge, fill=0.0, base=0,
                                    pattern=[[-REP, EXPERTS], [0, REP]], channel_multiplier=1))
            link(pool.affine_select(out=same[:, :, :], in_=same[:, :, :], compare_op=ALU.is_ge, fill=0.0, base=REP - 1,
                                    pattern=[[REP, EXPERTS], [0, REP]], channel_multiplier=-1))
            link(pool.iota(slot_i[:, :], [[1, CAP]], base=0, channel_multiplier=0))
            link(pool.iota(digit[:, :], [[0, 1]], base=0, channel_multiplier=1))
            link(pool.memset(zeros[:, :], 0.0))
            link(pool.memset(slot[:, :, EXPERTS:EXPERTS + 1], -1.0))

        CONSTS = 8

        @block.tensor
        def _(pe):
            pe.sem_inc(dn_done, 1)
            pe.wait_ge(h3_in, 16)
            for n in range(H_TURNS):
                if n >= 4:
                    pe.wait_ge(h3_kept, n - 3)
                for m in range(4):
                    ck, i = divmod(n * 4 + m, NT)
                    ins = pe.transpose(wide[:, n % 4, m * P:(m + 1) * P], h3[:, i, ck * P:(ck + 1) * P], ident[:, :])
                ins.then_inc(h3_turned, 1)
            pe.wait_ge(e_const, 1)
            pe.wait_ge(router_in, 32)
            pe.wait_ge(h3_kept, H_TURNS)
            for i in range(NT):
                bank = pv_ps[:, i * EXPERTS:(i + 1) * EXPERTS]
                for ck in range(DC):
                    pe.matmul(bank, h3T[:, ck, i * P:(i + 1) * P], w_r[:, ck, :], start=ck == 0, stop=False)
                ins = pe.matmul(bank, ones_row[:, :], b_r[:, :], start=False, stop=True)
            ins.then_inc(logits_ready, 1)
            pe.wait_ge(e_const, CONSTS)
            pe.wait_ge(spread, 1)
            for i in range(NT):
                ins = pe.transpose(wide[:, i // 4, (i % 4) * P:(i % 4 + 1) * P],
                                   gate_rep[:, i, :, :].rearrange("p e r -> p (e r)"), ident[:, :])
            ins.then_inc(gate_turned, 1)
            for n in range(len(SHIFTS)):
                pe.wait_ge(tried_count, n + 1)
                pe.matmul(pv_ps[:, n:n + 1], same[:, :, :].rearrange("p e r -> p (e r)"), enough[:, :], start=True,
                          stop=True).then_inc(tried_sum, 1)
            pe.wait_ge(slots_known, 1)
            for i in range(NT):
                ins = pe.transpose(wide[:, i // 4, (i % 4) * P:(i % 4 + 1) * P], run[:, i * P:(i + 1) * P], ident[:, :])
            ins.then_inc(slots_turned, 1)
            pe.wait_ge(slots_kept, 1)
            pe.wait_ge(h3_split, 2)
            with pe.Fori(0, EXPERTS // SHARE) as g:
                for n in range(SHARE):
                    e = g * SHARE + n
                    pick = picks[:, n % 2, :, :]
                    for i in range(NT):
                        pe.wait_ge(picked, e * NT + i + 1)
                        for ck in range(DC):
                            for m, part in enumerate((h3_hi, h3_lo)):
                                ins = pe.matmul(wide[:, ck, 0:CAP], part[:, i, ck * P:(ck + 1) * P], pick[:, i, :],
                                                start=i == 0 and m == 0, stop=i == NT - 1 and m == 1)
                    ins.then_inc(gathered, 1)
                    for k in range(TURNS):
                        if k >= 3:
                            pe.wait_ge(pick_kept, e * TURNS + k - 2)
                        for m in range(4):
                            sc, i = divmod(k * 4 + m, NT)
                            ins = pe.transpose(trio[:, k % 3, m * P:(m + 1) * P],
                                               pick[:, i, sc * P:(sc + 1) * P].bitcast(F32), ident[:, :])
                        ins.then_inc(pick_turned, 1)
                    pe.wait_ge(up_in, g * 48 + 48)
                    pe.wait_ge(taken_kept, e + 1)
                    for f in range(FC):
                        M = P if f < FC - 1 else FL
                        if f >= 3:
                            pe.wait_ge(mid_ready, e * FC + f - 2 + SHARE * FC)
                        bank = (pv_ps[:, :], wide[:, 0, :], wide[:, 1, :])[f % 3]
                        for ck in range(DC):
                            ins = pe.matmul(bank[0:M, 0:CAP], w_up[:, ck, f * P:f * P + M], taken[:, ck, :],
                                            start=ck == 0, stop=ck == DC - 1)
                        ins.then_inc(up_done, 1)
                    pe.wait_ge(dn_in, e * 48 + 48)
                    for f in range(FC):
                        M = P if f < FC - 1 else FL
                        pe.wait_ge(mid_ready, e * FC + f + 1 + SHARE * FC)
                        for sc in range(SC):
                            pe.matmul(wide[:, 2 + sc, 0:D], mid[0:M, f, sc * P:(sc + 1) * P], w_dn[0:M, f, :],
                                      start=f == 0, stop=False)
                    for sc in range(SC):
                        ins = pe.matmul(wide[:, 2 + sc, 0:D], ones_row[:, :], b_dn[:, :], start=False, stop=True)
                    ins.then_inc(dn_done, 1)
                    pe.wait_ge(made_split, e + 1)
                    pe.wait_ge(pick_kept, (e + 1) * TURNS)
                    for i in range(NT):
                        if i >= 3:
                            pe.wait_ge(added, e * NT + i - 2)
                        for sc in range(SC):
                            for m, part in enumerate((made_hi, made_lo)):
                                ins = pe.matmul(trio[:, i % 3, 0:D], pickT[:, sc, i * P:(i + 1) * P], part[:, sc, :],
                                                start=sc == 0 and m == 0, stop=sc == SC - 1 and m == 1)
                        ins.then_inc(spread_back, 1)
                    pe.wait_ge(added, (e + 1) * NT)

        @block.scalar
        def _(act):
            act.sem_inc(mid_ready, SHARE * FC)
            for n in range(H_TURNS):
                act.wait_ge(h3_turned, n + 1)
                ck, i = divmod(n * 4, NT)
                act.activation(h3T[:, ck, i * P:(i + 4) * P], wide[:, n % 4, :], ACT.Copy).then_inc(h3_kept, 1)
            act.wait_ge(l_shift, 1)
            act.activation(lexp[:, :, :], lexp[:, :, :], ACT.Exp).then_inc(l_exp, 1)
            act.wait_ge(gate_turned, 1)
            act.activation(gateT[:, :], wide[:, :, :].rearrange("p b n -> p (b n)"), ACT.Copy).then_inc(gate_kept, 1)
            with act.Fori(0, EXPERTS // SHARE) as g:
                for n in range(SHARE):
                    e = g * SHARE + n
                    act.wait_ge(gathered, e + 1)
                    act.activation(taken[:, :, :], wide[:, 0:DC, 0:CAP], ACT.Copy).then_inc(taken_kept, 1)
                    for k in range(TURNS):
                        act.wait_ge(pick_turned, e * TURNS + k + 1)
                        sc, i = divmod(k * 4, NT)
                        act.activation(pickT[:, sc, i * P:(i + 4) * P], trio[:, k % 3, :], ACT.Copy).then_inc(pick_kept, 1)
                    for f in range(FC):
                        M = P if f < FC - 1 else FL
                        act.wait_ge(up_done, e * FC + f + 1)
                        bank = (pv_ps[:, :], wide[:, 0, :], wide[:, 1, :])[f % 3]
                        act.activation(mid[0:M, f, :], bank[0:M, 0:CAP], ACT.Silu,
                                       bias=b_up[0:M, f:f + 1]).then_inc(mid_ready, 1)
                    act.wait_ge(dn_done, e + 2)
                    act.activation(made_hi[:, :, :], wide[:, 2:2 + SC, 0:D], ACT.Copy).then_inc(made_rounded, 1)

        @block.vector
        def _(dve):
            n = 0

            def link(ins):
                nonlocal n
                n += 1
                ins.then_inc(e_chain, 1)
                dve.wait_ge(e_chain, n)

            def over_experts(v):
                return v[:, :].rearrange("p (t a) -> p t a", a=1).to_broadcast([P, NT, EXPERTS])

            dve.wait_ge(e_const, CONSTS)
            link(dve.tensor_copy(slot_no[:, :], slot_i[:, :]))
            link(dve.tensor_single_scalar(digit[:, :], digit[:, :], REP - 1, ALU.bitwise_and))
            link(dve.memset(base[:, :], 0))
            dve.wait_ge(h3_in, 16)
            dve.tensor_copy(h3_hi[:, :, :], h3[:, :, :]).then_inc(h3_split, 1)
            dve.wait_ge(logits_ready, 1)
            logits = pv_ps[:, 0:NT * EXPERTS].rearrange("p (t e) -> p t e", e=EXPERTS)
            link(dve.tensor_reduce(lmax[:, :], logits, AX.X, ALU.max))
            dve.tensor_tensor(lexp[:, :, :], logits, over_experts(lmax), ALU.subtract).then_inc(l_shift, 1)
            dve.wait_ge(l_exp, 1)
            link(dve.tensor_reduce(lsum[:, :], lexp[:, :, :], AX.X, ALU.add))
            link(dve.reciprocal(lsum[:, :], lsum[:, :]))
            link(dve.tensor_tensor(gate[:, :, :], lexp[:, :, :], over_experts(lsum), ALU.mult))
            dve.tensor_copy(gate_rep[:, :, :, :],
                            gate[:, :, :].rearrange("p t (e a) -> p t e a", a=1).to_broadcast([P, NT, EXPERTS, REP]))\
               .then_inc(spread, 1)
            dve.wait_ge(h3_split, 1)
            dve.tensor_tensor(h3_lo[:, :, :], h3[:, :, :], h3_hi[:, :, :].bitcast(F32), ALU.subtract).then_inc(h3_split, 1)
            dve.wait_ge(gate_kept, 1)
            for k, shift in enumerate(SHIFTS):
                fold = FIRST_FOLD if k == 0 else 0
                link(dve.tensor_scalar(tried[:, :], digit[:, :], fold, shift, ALU.logical_shift_right,
                                       ALU.logical_shift_left))
                link(dve.tensor_tensor(tried[:, :], tried[:, :], base[:, :], ALU.bitwise_or))
                link(dve.tensor_scalar(above[:, :], gateT[:, :], tried[:, 0:1].bitcast(F32), 0.0, ALU.is_ge, ALU.add,
                                       accum_out=count[:, :]))
                dve.tensor_single_scalar(enough[:, :], count[:, :], float(CAP), ALU.is_ge).then_inc(tried_count, 1)
                dve.wait_ge(tried_sum, k + 1)
                link(dve.tensor_scalar(step[:, :], pv_ps[:, k:k + 1], 1.0 / (1 << fold), -1.0, ALU.mult, ALU.add))
                link(dve.tensor_single_scalar(step[:, :], step[:, :], shift, ALU.logical_shift_left))
                link(dve.tensor_tensor(base[:, :], base[:, :], step[:, :], ALU.bitwise_or))
            cut = base[:, 0:1].bitcast(F32)
            link(dve.tensor_scalar(above[:, :], gateT[:, :], cut, 0.0, ALU.is_gt, ALU.add, accum_out=count[:, :]))
            link(dve.tensor_scalar(count[:, :], count[:, :], -1.0, float(CAP), ALU.mult, ALU.add))
            link(dve.tensor_scalar(equal[:, :], gateT[:, :], cut, None, ALU.is_equal))
            link(dve.tensor_tensor_scan(run[:, :], equal[:, :], zeros[:, :], 0.0, ALU.add, ALU.add))
            link(dve.scalar_tensor_tensor(out=equal[:, :], in0=run[:, :], scalar=count[:, 0:1], in1=equal[:, :],
                                          op0=ALU.is_le, op1=ALU.mult))
            link(dve.tensor_tensor(above[:, :], above[:, :], equal[:, :], ALU.add))
            link(dve.tensor_tensor_scan(run[:, :], above[:, :], zeros[:, :], 0.0, ALU.add, ALU.add))
            link(dve.tensor_tensor(run[:, :], run[:, :], above[:, :], ALU.mult))
            dve.tensor_single_scalar(run[:, :], run[:, :], -1.0, ALU.add).then_inc(slots_known, 1)
            dve.wait_ge(slots_turned, 1)
            ranks = wide[:, :, :].rearrange("p b (i e r) -> p (b i) e r", e=EXPERTS, r=REP)
            dve.tensor_copy(slot[:, :, 0:EXPERTS], ranks[:, :, :, 0]).then_inc(slots_kept, 1)
            dve.wait_ge(slots_kept, 1)
            dve.wait_ge(x2_in, 16)

            def choose(e, half):
                for i in range(NT):
                    col = e if isinstance(e, slice) else bass.ds(e, 1)
                    dve.tensor_scalar(picks[:, half, i, :], slot_no[:, :], slot[:, i, col], None,
                                      ALU.is_equal).then_inc(picked, 1)

            choose(slice(0, 1), 0)
            with dve.Fori(0, EXPERTS // SHARE) as g:
                for m in range(SHARE):
                    e = g * SHARE + m
                    if m:
                        dve.wait_ge(pick_turned, e * TURNS)
                    choose(e + 1, (m + 1) % 2)
                    dve.wait_ge(made_rounded, e + 1)
                    dve.tensor_tensor(made_lo[:, :, :], wide[:, 2:2 + SC, 0:D], made_hi[:, :, :].bitcast(F32),
                                      ALU.subtract).then_inc(made_split, 1)
                    for i in range(NT):
                        dve.wait_ge(spread_back, e * NT + i + 1)
                        dve.scalar_tensor_tensor(out=x2[:, i, :], in0=trio[:, i % 3, 0:D],
                                                 scalar=gate[:, i, bass.ds(e, 1)],
                                                 in1=x2[:, i, :], op0=ALU.mult, op1=ALU.add).then_inc(added, 1)


_INS = ['x', 'ctx_2048', 'L0_attn_gamma', 'L0_attn_beta', 'L0_attn_w_qkv', 'L0_attn_w_out', 'L0_attn_b_out',
        'L0_xattn_Wq', 'L0_xattn_Wkv', 'L0_xattn_null_kv', 'L0_xattn_Wout', 'L0_xattn_ln_scale', 'L0_xattn_ln_bias',
        'L0_ffn_Wr', 'L0_ffn_br', 'L0_ffn_W_up', 'L0_ffn_b_up', 'L0_ffn_W_down', 'L0_ffn_b_down']


def kernel(**inputs):
    import numpy as _np
    import concourse.bacc as _bacc
    from concourse import mybir as _mybir
    from concourse.bass_utils import run_bass_kernel_spmd as _run

    nc = _bacc.Bacc("TRN2", target_bir_lowering=False, num_devices=1)
    arrays, aps = {}, {}
    for name in _INS:
        a = _np.ascontiguousarray(inputs[name])
        arrays[f"in_{name}_dram"] = a
        aps[name] = nc.dram_tensor(f"in_{name}_dram", a.shape, _mybir.dt.from_np(a.dtype), kind="ExternalInput").ap()
    shape = inputs["x"].shape
    res = nc.dram_tensor("out_0_dram", shape, _mybir.dt.float32, kind="ExternalOutput").ap()
    build(nc, aps, res)
    r = _run(nc, [arrays], core_ids=[0])
    return r.results[0]["out_0_dram"]
```

```python
from contextlib import ExitStack

import concourse.bass as bass
from concourse import mybir

ALU = mybir.AluOpType
ACT = mybir.ActivationFunctionType
AX = mybir.AxisListType
F32 = mybir.dt.float32
F32R = mybir.dt.float32r
I32 = mybir.dt.int32
P = 128


def build(nc, A, out):
    x_h, ctx_h = A["x"], A["ctx_2048"]
    B, S, D = x_h.shape
    CTX_LEN, CTX_DIM = ctx_h.shape[1:]
    TT = S // P
    NT = B * TT
    DC = D // P
    CC = CTX_DIM // P
    HID = A["L0_attn_w_out"].shape[0]
    LHEAD = 32
    LHEADS = HID // LHEAD
    LSCALE = LHEAD ** -0.5
    INNER = A["L0_xattn_Wq"].shape[1]
    DH = A["L0_xattn_null_kv"].shape[1]
    HEADS = INNER // DH
    XSCALE = DH ** -0.5
    HG = 4
    GROUPS = HEADS // HG
    GW = HG * DH
    PAIRS = HG // 2
    KT = (CTX_LEN + 1 + P - 1) // P
    LASTC = CTX_LEN - (KT - 1) * P
    LASTK = LASTC + 1
    KB = 4
    KCOL = (CTX_LEN + 1 + 2 * KB - 1) // (2 * KB) * 2
    KPAD = KB * KCOL
    NULL_COL = CTX_LEN - (KB - 1) * KCOL
    assert DH == 64 and S == 512 and KPAD <= KT * P and HID == P
    EXPERTS, F, _ = A["L0_ffn_W_down"].shape
    NGROUP = A["L0_ffn_W_up"].shape[0]
    SHARE = EXPERTS // NGROUP
    CAP = B * S // EXPERTS
    FC = (F + P - 1) // P
    FL = F - (FC - 1) * P
    SC = CAP // P
    REP = P // EXPERTS
    assert REP == 16
    LN_EPS, X_EPS = 1e-5, 1e-6
    RAW = 3
    HIRING = 4
    LORING = 3
    LAG = 3
    SIMS = HG * KT
    FIRST_MAX_AT = (4, 6, 8, 10)
    MAX_AT = ((2, 4, 7, 9), (3, 5, 7, 9), (3, 5, 7, 9))
    TURN_AT = 11

    with ExitStack() as whole:
        wide = whole.enter_context(nc.psum_tensor("wide", [P, 4, 512], F32))
        trio = whole.enter_context(nc.psum_tensor("trio", [P, 3, 512], F32))
        pv_ps = whole.enter_context(nc.psum_tensor("pv_ps", [P, 512], F32))
        ident = whole.enter_context(nc.sbuf_tensor("ident", [P, P], F32))
        x1_dram = nc.dram_tensor("x1_scratch", (B, S, D), F32, kind="Internal").ap()
        h2_dram = nc.dram_tensor("h2_scratch", (B, P, DC * S), F32, kind="Internal").ap()
        x2_dram = nc.dram_tensor("x2_scratch", (B, S, D), F32, kind="Internal").ap()
        h3_dram = nc.dram_tensor("h3_scratch", (B, S, D), F32, kind="Internal").ap()

        linear_attention(nc, A, dict(locals()))
        cross_attention(nc, A, dict(locals()))
        experts(nc, A, out, dict(locals()))


class Chain:

    def __init__(self, eng, sem, rounds_before, per_round):
        self.eng, self.sem, self.n, self.base, self.per = eng, sem, 0, rounds_before, per_round

    def link(self, ins):
        self.n += 1
        ins.then_inc(self.sem, 1)
        self.eng.wait_ge(self.sem, self.base * self.per + self.n)

    def close(self):
        assert self.n == self.per, self.n


def rsqrt_steps(dve, chain, r, t, v, eps):
    chain.link(dve.tensor_scalar(v, v, eps, None, ALU.add))
    chain.link(dve.tensor_scalar(r.bitcast(I32), v.bitcast(I32), -0.5, 1597463007.0, ALU.mult, ALU.add))
    for _ in range(4):
        chain.link(dve.tensor_tensor(t, r, r, ALU.mult))
        chain.link(dve.scalar_tensor_tensor(out=t, in0=t, scalar=-0.5, in1=v, op0=ALU.mult, op1=ALU.mult))
        chain.link(dve.scalar_tensor_tensor(out=r, in0=t, scalar=1.5, in1=r, op0=ALU.add, op1=ALU.mult))


def moments(dve, chain, stats, mv, rstd, newton, srcs, eps):
    for i, src in enumerate(srcs):
        ins = dve.bn_stats(stats[:, i, :], src)
    chain.link(ins)
    dve.memset(newton, 0.0)
    for i in range(len(srcs)):
        ins = dve.bn_aggr(mv[:, i, :], stats[:, i, :])
    chain.link(ins)
    rsqrt_steps(dve, chain, rstd, newton, mv[:, 0:len(srcs), 1], eps)


def normalise(dve, mv, rstd, dsts, srcs):
    for i, (dst, src) in enumerate(zip(dsts, srcs)):
        ins = dve.tensor_scalar(dst, src, mv[:, i, 0:1], rstd[:, i:i + 1], ALU.subtract, ALU.mult)
    return ins


def linear_attention(nc, A, c):
    B, S, D, TT, NT, DC, LHEAD, LHEADS, HID, LSCALE, LN_EPS = (c[k] for k in (
        "B", "S", "D", "TT", "NT", "DC", "LHEAD", "LHEADS", "HID", "LSCALE", "LN_EPS"))
    wide, trio, pv_ps, ident = (c[k] for k in ("wide", "trio", "pv_ps", "ident"))
    x1_dram, h2_dram = c["x1_dram"], c["h2_dram"]

    with ExitStack() as scope:
        def sb(name, shape, dt=F32):
            return scope.enter_context(nc.sbuf_tensor(name, shape, dt))

        def sem(name):
            return scope.enter_context(nc.semaphore(name))

        w_qkv = sb("w_qkv", [P, DC, 3 * HID])
        w_lout = sb("w_lout", [P, D])
        gamma = sb("gamma", [P, DC])
        beta = sb("beta", [P, DC])
        b_lout = sb("b_lout", [P, D])
        x = sb("x", [P, NT, D])
        xn0 = sb("xn0", [P, NT, D])
        xn = sb("xn", [P, NT, D])
        xT = sb("xT", [P, 2, DC, S])
        h2T = sb("h2T", [P, B, DC, S])
        stats = sb("stats", [P, TT, 6])
        mv = sb("mv", [P, TT, 2])
        rstd = sb("rstd", [P, TT])
        newton = sb("newton", [P, TT])
        kmax = sb("kmax", [P, B])
        ksum = sb("ksum", [P, B])
        ksum_r = sb("ksum_r", [P, B])
        ek = sb("ek", [P, 2, S])
        qT = sb("qT", [P, 2, S])
        vl = sb("vl", [P, 2, TT, HID])
        ekn = sb("ekn", [P, 2, TT, HID])
        kv_bd = sb("kv_bd", [P, 2, HID])
        loT = sb("loT", [P, 2, S])

        consts, weights_in = sem("consts"), sem("weights_in")
        x_in = [sem(f"x_in_{b}") for b in range(B)]
        steps = sem("steps")
        ln_ready, turned, turn_kept = sem("ln_ready"), sem("turned"), sem("turn_kept")
        projected, kmax_ready, keys_ready, q_ready, v_ready = (
            sem("projected"), sem("kmax_ready"), sem("keys_ready"), sem("q_ready"), sem("v_ready"))
        keys_turned, keys_kept, kv_made, kv_ready = sem("keys_turned"), sem("keys_kept"), sem("kv_made"), sem("kv_ready")
        o_made, o_kept, out_made, x1_ready, h2_ready = (
            sem("o_made"), sem("o_kept"), sem("out_made"), sem("x1_ready"), sem("h2_ready"))
        x_biased, stored = sem("x_biased"), sem("stored")
        WEIGHTS = 5

        block = scope.enter_context(nc.Block())

        @block.sync
        def _(sp):
            for b in range(B):
                sp.dma_start(x[:, b * TT:(b + 1) * TT, :], A["x"][b].rearrange("(t p) d -> p t d", p=P)).then_inc(x_in[b], 16)
            for dst, src in (
                (w_qkv[:, :, :], A["L0_attn_w_qkv"].rearrange("(c p) f -> p c f", p=P)),
                (w_lout[:, :], A["L0_attn_w_out"]),
                (b_lout[:, :], A["L0_attn_b_out"].rearrange("(a d) -> a d", a=1).to_broadcast([P, D])),
            ):
                sp.dma_start(dst, src).then_inc(weights_in, 16)
            with nc.allow_non_contiguous_dma(reason="a column of the model dimension on partitions"):
                for dst, src in ((gamma, "L0_attn_gamma"), (beta, "L0_attn_beta")):
                    sp.dma_start(dst[:, :], A[src].rearrange("a b (c p) -> p (a b c)", p=P)).then_inc(weights_in, 16)
            for b in range(B):
                sp.wait_ge(x1_ready, b + 1)
                sp.dma_start(x1_dram[b].rearrange("(t p) d -> p t d", p=P), xn0[:, b * TT:(b + 1) * TT, :])\
                  .then_inc(stored, 16)
            for b in range(B):
                sp.wait_ge(h2_ready, b + 1)
                sp.dma_start(h2_dram[b], h2T[:, b, :, :].rearrange("p c s -> p (c s)")).then_inc(stored, 16)
            sp.wait_ge(stored, 2 * B * 16)

        @block.gpsimd
        def _(pool):
            pool.memset(ident[:, :], 0.0).then_inc(consts, 1)
            pool.wait_ge(consts, 1)
            pool.affine_select(out=ident[:, :], in_=ident[:, :], compare_op=ALU.not_equal, fill=1.0, base=0,
                               pattern=[[-1, P]], channel_multiplier=1).then_inc(consts, 1)
            pool.memset(kv_bd[:, :, :], 0.0).then_inc(consts, 1)
            pool.wait_ge(weights_in, WEIGHTS * 16)
            for b in range(B):
                pool.wait_ge(ln_ready, b + 1)
                for i in range(b * TT, (b + 1) * TT):
                    pool.tensor_tensor(x[:, i, :], x[:, i, :], b_lout[:, :], ALU.add).then_inc(x_biased, 1)

        CONSTS = 3

        @block.tensor
        def _(pe):
            pe.wait_ge(consts, CONSTS)
            pe.wait_ge(weights_in, WEIGHTS * 16)

            def turn(n):
                b = n % B
                pe.wait_ge(ln_ready, n + 1)
                if n >= 1:
                    pe.wait_ge(turn_kept, n)
                for ck in range(DC):
                    for i in range(TT):
                        ins = pe.transpose(wide[:, ck, i * P:(i + 1) * P], xn[:, b * TT + i, ck * P:(ck + 1) * P],
                                           ident[:, :])
                ins.then_inc(turned, 1)

            def project(b):
                pe.wait_ge(turn_kept, b + 1)
                if b >= 1:
                    pe.wait_ge(q_ready, b)
                    pe.wait_ge(v_ready, b)
                for n in range(2):
                    for ck in range(DC):
                        pe.matmul(trio[:, n, :], w_qkv[:, ck, (1 - n) * HID:(2 - n) * HID], xT[:, b % 2, ck, :],
                                  start=ck == 0, stop=ck == DC - 1)
                for i in range(TT):
                    for ck in range(DC):
                        ins = pe.matmul(wide[:, 2, i * HID:(i + 1) * HID], xT[:, b % 2, ck, i * P:(i + 1) * P],
                                        w_qkv[:, ck, 2 * HID:3 * HID], start=ck == 0, stop=ck == DC - 1)
                ins.then_inc(projected, 1)

            def turn_keys(b):
                pe.wait_ge(keys_ready, b + 1)
                if b >= 1:
                    pe.wait_ge(keys_kept, b)
                for i in range(TT):
                    ins = pe.transpose(wide[:, 3, i * P:(i + 1) * P], ek[:, b % 2, i * P:(i + 1) * P], ident[:, :])
                ins.then_inc(keys_turned, 1)

            def keys_values(b):
                pe.wait_ge(keys_kept, b + 1)
                pe.wait_ge(v_ready, b + 1)
                if b >= 1:
                    pe.wait_ge(x1_ready, b)
                for i in range(TT):
                    ins = pe.matmul(trio[:, 2, 0:HID], ekn[:, b % 2, i, :], vl[:, b % 2, i, :], start=i == 0,
                                    stop=i == TT - 1)
                ins.then_inc(kv_made, 1)

            def attend(b):
                pe.wait_ge(kv_ready, b + 1)
                pe.wait_ge(q_ready, b + 1)
                pe.matmul(pv_ps[:, :], kv_bd[:, b % 2, :], qT[:, b % 2, :], start=True, stop=True).then_inc(o_made, 1)

            def project_out(b):
                pe.wait_ge(o_kept, b + 1)
                for i in range(TT):
                    bank = (trio[:, 2, :], pv_ps[:, :])[i // 2]
                    ins = pe.matmul(bank[:, (i % 2) * D:(i % 2 + 1) * D], loT[:, b % 2, i * P:(i + 1) * P],
                                    w_lout[:, :], start=True, stop=True)
                ins.then_inc(out_made, 1)

            turn(0)
            project(0)
            turn(1)
            turn_keys(0)
            for b in range(B):
                if b + 1 < B:
                    project(b + 1)
                keys_values(b)
                turn(b + 2)
                attend(b)
                if b + 1 < B:
                    turn_keys(b + 1)
                project_out(b)
            turn(6)
            turn(7)

        @block.scalar
        def _(act):
            act.wait_ge(weights_in, WEIGHTS * 16)

            def keep_turned(n):
                act.wait_ge(turned, n + 1)
                b = n % B
                for ck in range(DC):
                    if n < B:
                        ins = act.activation(xT[:, b % 2, ck, :], wide[:, ck, :], ACT.Identity, bias=beta[:, ck:ck + 1],
                                             scale=gamma[:, ck:ck + 1])
                    else:
                        ins = act.activation(h2T[:, b, ck, :], wide[:, ck, :], ACT.Copy)
                ins.then_inc(turn_kept, 1)
                if n >= B:
                    act.wait_ge(turn_kept, n + 1)
                    act.sem_inc(h2_ready, 1)

            def keys(b):
                act.wait_ge(kmax_ready, b + 1)
                act.activation(ek[:, b % 2, :], trio[:, 0, :], ACT.Exp, bias=kmax[:, b:b + 1],
                               accum_out=ksum[:, b:b + 1]).then_inc(keys_ready, 1)
                act.activation(qT[:, b % 2, :], trio[:, 1, :], ACT.Copy, scale=LSCALE).then_inc(q_ready, 1)

            def keep_keys(b):
                act.wait_ge(keys_turned, b + 1)
                act.activation(ekn[:, b % 2, :, :].rearrange("p t h -> p (t h)"), wide[:, 3, :], ACT.Copy)\
                   .then_inc(keys_kept, 1)

            def keep_o(b):
                act.wait_ge(o_made, b + 1)
                act.activation(loT[:, b % 2, :], pv_ps[:, :], ACT.Copy).then_inc(o_kept, 1)

            keep_turned(0)
            keys(0)
            keep_turned(1)
            keep_keys(0)
            for b in range(B):
                if b + 1 < B:
                    keys(b + 1)
                keep_turned(b + 2)
                keep_o(b)
                if b + 1 < B:
                    keep_keys(b + 1)
            keep_turned(6)
            keep_turned(7)

        @block.vector
        def _(dve):
            chain = Chain(dve, steps, 0, 216)
            dve.wait_ge(consts, CONSTS)

            def tiles(buf, b):
                return [buf[:, b * TT + i, :] for i in range(TT)]

            def norm_twice(b):
                dve.wait_ge(x_in[b], 16)
                moments(dve, chain, stats, mv, rstd[:, :], newton[:, :], tiles(x, b), LN_EPS)
                chain.link(normalise(dve, mv, rstd, tiles(xn0, b), tiles(x, b)))
                moments(dve, chain, stats, mv, rstd[:, :], newton[:, :], tiles(xn0, b), LN_EPS)
                chain.link(normalise(dve, mv, rstd, tiles(xn, b), tiles(xn0, b)))
                dve.sem_inc(ln_ready, 1)

            def norm_out(b):
                dve.wait_ge(turned, b + 1)
                moments(dve, chain, stats, mv, rstd[:, :], newton[:, :], tiles(xn0, b), LN_EPS)
                chain.link(normalise(dve, mv, rstd, tiles(xn, b), tiles(xn0, b)))
                dve.sem_inc(ln_ready, 1)

            def key_max(b):
                dve.wait_ge(projected, b + 1)
                dve.tensor_reduce(kmax[:, b:b + 1], trio[:, 0, :], AX.X, ALU.max, negate=True).then_inc(kmax_ready, 1)
                dve.tensor_copy(vl[:, b % 2, :, :].rearrange("p t h -> p (t h)"), wide[:, 2, :]).then_inc(v_ready, 1)

            def weigh_kv(b):
                dve.wait_ge(keys_ready, b + 1)
                chain.link(dve.reciprocal(ksum_r[:, b:b + 1], ksum[:, b:b + 1]))
                dve.wait_ge(kv_made, b + 1)
                for h in range(LHEADS):
                    r = slice(h * LHEAD, (h + 1) * LHEAD)
                    ins = dve.tensor_scalar(kv_bd[r, b % 2, r], trio[r, 2, r], ksum_r[r, b:b + 1], None, ALU.mult)
                ins.then_inc(kv_ready, 1)

            def add(b):
                dve.wait_ge(out_made, b + 1)
                for n, bank in enumerate((trio[:, 2, :], pv_ps[:, :])):
                    flat = xn0[:, b * TT + 2 * n:b * TT + 2 * n + 2, :].rearrange("p t d -> p (t d)")
                    ins = dve.tensor_tensor(flat, bank, flat, ALU.add)
                chain.link(ins)
                dve.wait_ge(x_biased, (b + 1) * TT)
                rows = slice(b * TT, (b + 1) * TT)
                chain.link(dve.tensor_tensor(xn0[:, rows, :], xn0[:, rows, :], x[:, rows, :], ALU.add))
                dve.sem_inc(x1_ready, 1)

            norm_twice(0)
            norm_twice(1)
            key_max(0)
            norm_twice(2)
            key_max(1)
            weigh_kv(0)
            norm_twice(3)
            add(0)
            key_max(2)
            weigh_kv(1)
            norm_out(0)
            add(1)
            key_max(3)
            weigh_kv(2)
            norm_out(1)
            add(2)
            weigh_kv(3)
            norm_out(2)
            add(3)
            norm_out(3)
            chain.close()


def cross_attention(nc, A, c):
    (B, S, D, TT, DC, CC, CTX_LEN, HG, GROUPS, GW, PAIRS, KT, LASTC, LASTK, KB, KCOL, KPAD, DH, RAW,
     HIRING, LORING, LAG, SIMS, FIRST_MAX_AT, MAX_AT, TURN_AT, INNER, XSCALE, LN_EPS, X_EPS) = (c[k] for k in (
        "B", "S", "D", "TT", "DC", "CC", "CTX_LEN", "HG", "GROUPS", "GW", "PAIRS", "KT", "LASTC", "LASTK", "KB",
        "KCOL", "KPAD", "DH", "RAW", "HIRING", "LORING", "LAG", "SIMS", "FIRST_MAX_AT", "MAX_AT", "TURN_AT", "INNER", "XSCALE",
        "LN_EPS", "X_EPS"))
    wide, trio, pv_ps, ident = (c[k] for k in ("wide", "trio", "pv_ps", "ident"))
    x1_dram, h2_dram, x2_dram, h3_dram = (c[k] for k in ("x1_dram", "h2_dram", "x2_dram", "h3_dram"))
    CRING = RAW + 2 * PAIRS
    VRAW = 4
    WRING = 2
    CHUNKS = 2 * CC
    NULL_ROWS = slice(LASTC // 32 * 32, LASTK)
    ONES = 32
    T = B * GROUPS
    BANKS = PAIRS * KB
    BANK_ORDER = (1, 2, 3, 0)
    NORM_AT = (4, 6, 8, 10)
    ON_DVE = [k for k in range(KT) if k % 2 == 0]
    ON_POOL = [k for k in range(KT) if k % 2 == 1]
    W_TILES = [n for n in range(2, SIMS) if n % KT not in ON_POOL][:2 * CHUNKS]
    assert len(W_TILES) == 2 * CHUNKS and KB == 4 and RAW * S >= TT * D + 2 * D

    with ExitStack() as scope:
        def sb(name, shape, dt=F32):
            return scope.enter_context(nc.sbuf_tensor(name, shape, dt))

        def sem(name):
            return scope.enter_context(nc.semaphore(name))

        null_k = sb("null_k", [DH, 1])
        zero = sb("zero", [P, 1])
        acc = sb("acc", [P, TT, D])
        null_v = acc[:, 0, 0:DH]
        null_wide = acc[0:DH, 1, 0:HG * (KPAD - CTX_LEN)].rearrange("p (j n) -> p j n", j=HG)
        xT = sb("h2T_in", [P, DC, S])
        stats = sb("x_stats", [P, TT, 6])
        mv = sb("x_mv", [P, TT, 2])
        rstd = sb("x_rstd", [P, TT])
        newton = sb("x_newton", [P, TT])
        c_hi = sb("c_hi", [P, CC, KPAD], F32R)
        c_lo = sb("c_lo", [P, CC, KPAD], F32R)
        wq = sb("wq", [P, DC, GW])
        wo = sb("wo", [P, PAIRS, D])
        w_in = sb("w_in", [P, WRING, GW])
        w_hi, w_lo = sb("w_hi", [P, 2, CC, GW], F32R), sb("w_lo", [P, 2, CC, GW], F32R)
        q_hi = sb("q_hi", [P, HG, S], F32R)
        q_lo = sb("q_lo", [P, HG, S], F32R)
        k_hl = sb("k_hl", [P, HG, KPAD], F32R)
        k_h1 = sb("k_h1", [P, HG, KPAD], F32R)
        v_one = sb("v_one", [P, KT, HG, DH + ONES], F32R)
        v_lo = sb("v_lo", [P, KT, HG, DH], F32R)
        probs = sb("probs", [P, RAW, S])
        p_hi = sb("p_hi", [P, HIRING, S], F32R)
        p_lo = sb("p_lo", [P, LORING, S], F32R)
        neg_max = sb("neg_max", [P, 2, TT])
        den_pair = sb("den_pair", [P, PAIRS, S])
        oT = sb("oT", [P, PAIRS, S])
        ctx_in = [probs[:, n, :] for n in range(RAW)] + [b_[:, n, :] for b_ in (den_pair, oT) for n in range(PAIRS)]
        x1 = probs[:, 0:2, :].rearrange("p a (i d) -> p (a i) d", d=D)
        ln_scale, ln_bias = probs[:, 2, 0:D], probs[:, 2, D:2 * D]
        v_raw = oT[:, :, :].rearrange("p h (n d) -> p (h n) d", d=GW)

        pool_step, consts_in, null_ready = sem("pool_step"), sem("consts_in"), sem("null_ready")
        h2_in, x1_in, rows_stored = sem("h2_in"), sem("x1_in"), sem("rows_stored")
        ctx_in_s = [sem(f"ctx_in_{k}") for k in range(KT)]
        wq_in_s, wo_in_s = sem("wq_in_s"), sem("wo_in_s")
        w_in_s = [sem(f"w_in_{k}") for k in range(WRING)]
        w_rounded, w_split = sem("w_rounded"), sem("w_split")
        dve_batch, dve_norm = sem("dve_batch"), sem("dve_norm")
        ctx_turned, c_rounded, c_split = sem("ctx_turned"), sem("c_rounded"), sem("c_split")
        q_made, q_rounded, q_split = sem("q_made"), sem("q_rounded"), sem("q_split")
        k_made, k_rounded, k_split = sem("k_made"), sem("k_rounded"), sem("k_split")
        v_made, v_kept, v_split = sem("v_made"), sem("v_kept"), sem("v_split")
        max_scores, max_taken, max_turned, max_row = (
            sem("max_scores"), sem("max_taken"), sem("max_turned"), sem("max_row"))
        scores_ready, probs_ready, p_rounded, split_dve, split_pool, probs_used = (
            sem("scores_ready"), sem("probs_ready"), sem("p_rounded"), sem("split_dve"), sem("split_pool"),
            sem("probs_used"))
        o_kept, o_normed, x_out, acc_added = sem("o_kept"), sem("o_normed"), sem("x_out"), sem("acc_added")
        x2_ready, h3_ready = sem("x2_ready"), sem("h3_ready")

        block = scope.enter_context(nc.Block())
        w_v = A["L0_xattn_Wq"].rearrange("(c p) f -> p c f", p=P)
        wo_v = A["L0_xattn_Wout"].rearrange("(g h p) f -> g p h f", p=P, h=PAIRS)
        CONSTS_IN = 2
        POOL_STEPS = 12
        NULLS = 4
        FINISH = 37
        acc_rows = [acc[:, i, :] for i in range(TT)]

        def split_by(n, t):
            j, k = divmod(n, KT)
            s, tiles = (split_dve, ON_DVE) if k in ON_DVE else (split_pool, ON_POOL)
            return s, (t * HG + j) * len(tiles) + tiles.index(k) + 1

        def rows_of(k):
            return P if k < KT - 1 else LASTK

        @block.sync
        def _(sp):
            def load_chunk(t, g, i):
                w, ck = divmod(i, CC)
                sp.dma_start(w_in[:, i % WRING, :],
                             A["L0_xattn_Wkv"][ck * P:(ck + 1) * P, bass.ds(g * GW + w * INNER, GW)])\
                  .then_inc(w_in_s[i % WRING], 16)

            def load_ctx(b, k):
                sp.wait_ge(ctx_turned, b * KT + max(k - CRING + 1, 0) + CRING)
                rows = P if k < KT - 1 else LASTC
                ctx_b = A["ctx_2048"][bass.ds(b, 1)].rearrange("a s d -> (a s) d")
                sp.dma_start(ctx_in[k % CRING][0:rows, :], ctx_b[k * P:k * P + rows, :]).then_inc(ctx_in_s[k], 16)

            def load_h2(b):
                sp.dma_start(xT[:, :, :].rearrange("p c s -> p (c s)"),
                             h2_dram[bass.ds(b, 1)].rearrange("a p n -> (a p) n")).then_inc(h2_in, 16)

            def load_weights(b):
                with sp.Fori(0, GROUPS) as g:
                    t = b * GROUPS + g
                    after = (g + 1) % GROUPS
                    sp.wait_ge(q_made, (t + 1) * PAIRS)
                    sp.dma_start(wq[:, :, :], w_v[:, :, bass.ds(after * GW, GW)]).then_inc(wq_in_s, 16)
                    sp.wait_ge(x_out, t + 1)
                    sp.dma_start(wo[:, :, :], wo_v[bass.ds(g, 1)].rearrange("a p h f -> p (a h) f")).then_inc(wo_in_s, 16)
                    for i in range(CHUNKS):
                        sp.wait_ge(w_split, (t + 1) * CHUNKS + i - WRING + 1)
                        load_chunk(t + 1, after, i)
                after = (b + 1) % B
                sp.wait_ge(q_made, (b + 1) * GROUPS * PAIRS)
                load_h2(after)

            def probs_free(t):
                sp.wait_ge(probs_used, t * SIMS + HIRING)

            def finish_rows(b):
                sp.dma_start(x1, x1_dram[bass.ds(b, 1)].rearrange("a (t p) d -> p (a t) d", p=P)).then_inc(x1_in, 16)
                for dst, src in ((ln_scale, "L0_xattn_ln_scale"), (ln_bias, "L0_xattn_ln_bias")):
                    sp.dma_start(dst, A[src].rearrange("(a d) -> a d", a=1).to_broadcast([P, D])).then_inc(x1_in, 16)
                for buf, ready, rows in ((x1, x2_ready, x2_dram), (acc[:, :, :], h3_ready, h3_dram)):
                    sp.wait_ge(ready, b + 1)
                    sp.dma_start(rows[bass.ds(b, 1)].rearrange("a (t p) d -> p (a t) d", p=P), buf)\
                      .then_inc(rows_stored, 16)

            load_h2(0)
            sp.dma_start(wq[:, :, :], w_v[:, :, 0:GW]).then_inc(wq_in_s, 16)
            for k in range(KT):
                load_ctx(0, k)
                if k == RAW:
                    with nc.allow_non_contiguous_dma(reason="a column of the head dimension on partitions"):
                        sp.dma_start(null_k[:, :], A["L0_xattn_null_kv"][0:1, :].rearrange("a d -> d a")).then_inc(consts_in, 16)
                    sp.wait_ge(pool_step, 1)
                    sp.dma_start(null_v[LASTC:LASTK, :], A["L0_xattn_null_kv"][1:2, :]).then_inc(consts_in, 16)
                if k < CHUNKS:
                    if k >= WRING:
                        sp.wait_ge(w_split, k - WRING + 1)
                    load_chunk(0, 0, k)
            load_weights(0)
            with sp.Fori(1, B) as b:
                probs_free(b * GROUPS)
                for k in range(KT):
                    if k == RAW:
                        sp.wait_ge(x_out, b * GROUPS + 1)
                    load_ctx(b, k)
                sp.wait_ge(ctx_turned, (b + 1) * KT + CRING)
                finish_rows(b - 1)
                load_weights(b)
            probs_free(T)
            finish_rows(B - 1)
            sp.wait_ge(rows_stored, B * 32 + 1)
            sp.wait_ge(h2_in, (B + 1) * 16)
            sp.wait_ge(wq_in_s, (T + 1) * 16)
            for k in range(WRING):
                sp.wait_ge(w_in_s[k], (T + 1) * CHUNKS // WRING * 16)

        @block.gpsimd
        def _(pool):
            for n, (dst, value) in enumerate((
                (null_v, 0.0),
                (zero[:, :], 0.0),
                (v_one[:, KT - 1, :, :].bitcast(F32), 0.0),
                (v_one[0:LASTK, KT - 1, :, DH:DH + ONES].bitcast(F32), 1.0),
                (v_one[:, 0:KT - 1, :, DH:DH + ONES].bitcast(F32), 1.0),
                (v_lo[:, KT - 1, :, :].bitcast(F32), 0.0),
                (null_wide, 0.0),
                (q_lo[DH:P, :, :].bitcast(F32), 0.0),
                (k_h1[DH:P, :, :].bitcast(F32), 0.0),
                (k_h1[DH:DH + 1, :, :].bitcast(F32), 1.0),
                (c_hi[:, :, CTX_LEN:KPAD].bitcast(F32), 0.0),
                (c_lo[:, :, CTX_LEN:KPAD].bitcast(F32), 0.0),
            )):
                pool.memset(dst, value).then_inc(pool_step, 1)
                pool.wait_ge(pool_step, n + 1)

            def split_weights(t, n):
                i, low = divmod(n, 2)
                src, hi, lo = w_in[:, i % WRING, :], w_hi[:, i // CC, i % CC, :], w_lo[:, i // CC, i % CC, :]
                if low:
                    pool.wait_ge(w_rounded, t * CHUNKS + i + 1)
                    pool.tensor_tensor(lo, src, hi.bitcast(F32), ALU.subtract).then_inc(w_split, 1)
                else:
                    pool.wait_ge(w_in_s[i % WRING], (t * (CHUNKS // WRING) + i // WRING + 1) * 16)
                    pool.tensor_tensor(hi, src, zero[:, :].to_broadcast([P, GW]), ALU.add).then_inc(w_rounded, 1)

            for n in range(2 * CHUNKS):
                split_weights(0, n)
            with pool.Fori(0, T) as t:
                for k in range(KT):
                    pool.wait_ge(v_kept, t * KT + k + 1)
                    rows = P if k < KT - 1 else LASTC
                    pool.tensor_tensor(v_lo[0:rows, k, :, :],
                                       v_raw[0:rows, k % VRAW, :].rearrange("p (j d) -> p j d", j=HG),
                                       v_one[0:rows, k, :, 0:DH].bitcast(F32), ALU.subtract).then_inc(v_split, 1)
                for n in range(SIMS):
                    k = n % KT
                    if k in ON_POOL:
                        pool.wait_ge(p_rounded, t * SIMS + n + 1)
                        pool.wait_ge(probs_used, t * SIMS + n + 1 - LORING + HIRING)
                        pool.tensor_tensor(p_lo[0:rows_of(k), n % LORING, :], probs[0:rows_of(k), n % RAW, :],
                                           p_hi[0:rows_of(k), n % HIRING, :].bitcast(F32), ALU.subtract)\
                            .then_inc(split_pool, 1)
                    if n in W_TILES:
                        split_weights(t + 1, W_TILES.index(n))

        @block.tensor
        def _(pe):
            pe.sem_inc(ctx_turned, CRING)
            pe.sem_inc(x_out, 1)
            pe.sem_inc(probs_used, HIRING)

            def products(out_, hi, lo, hi2, lo2):
                terms = ((hi, hi2), (hi, lo2), (lo, hi2))
                for ck in range(CC):
                    for n, (w, m) in enumerate(terms):
                        ins = pe.matmul(out_, w(ck), m(ck), start=ck == 0 and n == 0, stop=ck == CC - 1 and n == 2)
                return ins

            def queries(t, batch):
                pe.wait_ge(h2_in, batch * 16 + 16)
                pe.wait_ge(wq_in_s, t * 16 + 16)
                for p in range(PAIRS):
                    for ck in range(DC):
                        ins = pe.matmul(trio[:, p, :], wq[:, ck, p * P:(p + 1) * P], xT[:, ck, :],
                                        start=ck == 0, stop=ck == DC - 1)
                    ins.then_inc(q_made, 1)

            queries(0, 0)
            with pe.Fori(0, B) as b:
                for k in range(KT):
                    rows = P if k < KT - 1 else LASTC
                    pe.wait_ge(ctx_in_s[k], b * 16 + 16)
                    if k == 0:
                        pe.wait_ge(q_split, (b * GROUPS + 1) * PAIRS)
                        pe.wait_ge(acc_added, b * GROUPS + 1)
                    if k >= 3:
                        pe.wait_ge(c_split, b * KT + k - 2)
                    for ck in range(CC):
                        ins = pe.transpose(trio[:, k % 3, ck * P:ck * P + rows],
                                           ctx_in[k % CRING][0:rows, ck * P:(ck + 1) * P], ident[0:rows, 0:rows])
                    ins.then_inc(ctx_turned, 1)

                with pe.Fori(0, GROUPS) as g:
                    t = b * GROUPS + g

                    def keys(p):
                        for n in range(KB):
                            if p >= 1 and BANK_ORDER[n] == 0:
                                pe.wait_ge(max_row, t * HG + 1)
                            m = BANK_ORDER[n]
                            cols = slice(m * KCOL, (m + 1) * KCOL)
                            products(wide[:, m, 0:KCOL], lambda ck: w_hi[:, 0, ck, p * P:(p + 1) * P],
                                     lambda ck: w_lo[:, 0, ck, p * P:(p + 1) * P], lambda ck: c_hi[:, ck, cols],
                                     lambda ck: c_lo[:, ck, cols]).then_inc(k_made, 1)

                    def values(k):
                        if k == 0:
                            pe.wait_ge(q_split, (t + 1) * PAIRS)
                            pe.wait_ge(acc_added, t + 1)
                        elif k >= 3:
                            pe.wait_ge(v_kept, t * KT + k - 2)
                        rows = P if k < KT - 1 else LASTC
                        cols = slice(k * P, k * P + rows)
                        products(trio[0:rows, k % 3, 0:GW], lambda ck: c_hi[:, ck, cols], lambda ck: c_lo[:, ck, cols],
                                 lambda ck: w_hi[:, 1, ck, :], lambda ck: w_lo[:, 1, ck, :]).then_inc(v_made, 1)

                    def scores_for_max(j, i):
                        if i:
                            pe.wait_ge(max_taken, t * HG * TT + j * TT + i)
                        elif j:
                            pe.wait_ge(max_row, t * HG + j)
                        for n in range(KB):
                            ins = pe.matmul(wide[:, n, 0:KCOL], q_hi[:, j, i * P:(i + 1) * P],
                                            k_hl[:, j, n * KCOL:(n + 1) * KCOL], start=True, stop=True)
                        ins.then_inc(max_scores, 1)

                    def turn_max(j):
                        pe.wait_ge(max_taken, t * HG * TT + (j + 1) * TT)
                        for i in range(TT):
                            ins = pe.transpose(wide[0:1, 0, i * P:(i + 1) * P], neg_max[:, j % 2, i:i + 1], ident[:, :])
                        ins.then_inc(max_turned, 1)

                    def scores(n):
                        j, k = divmod(n, KT)
                        if k == 0:
                            pe.wait_ge(max_row, t * HG + j + 1)
                        if n >= 3:
                            pe.wait_ge(p_rounded, t * SIMS + n - 2)
                        cols = slice(k * P, k * P + rows_of(k))
                        bank = trio[0:rows_of(k), n % 3, :]
                        pe.matmul(bank, k_hl[:, j, cols], q_hi[:, j, :], start=True, stop=False)
                        pe.matmul(bank, k_h1[:, j, cols], q_lo[:, j, :], start=False, stop=True).then_inc(scores_ready, 1)

                    def weigh(n):
                        j, k = divmod(n, KT)
                        pe.wait_ge(*split_by(n, t))
                        if k == 0:
                            pe.wait_ge(o_kept, t * HG + j + 1)
                        made = pv_ps[0:DH + ONES, :]
                        pe.matmul(made, v_one[:, k, j, :], p_hi[:, n % HIRING, :], start=k == 0, stop=False)
                        pe.matmul(pv_ps[0:DH, :], v_lo[:, k, j, :], p_hi[:, n % HIRING, :], start=False, stop=False)
                        pe.matmul(made, v_one[:, k, j, :], p_lo[:, n % LORING, :], start=False, stop=k == KT - 1)\
                          .then_inc(probs_used, 1)

                    def ahead(n):
                        return n // KT >= 1 and n % KT == LAG

                    pe.wait_ge(null_ready, NULLS)
                    pe.wait_ge(c_split, (b + 1) * KT)
                    pe.wait_ge(w_split, (t + 1) * CHUNKS)
                    keys(0)
                    for k in range(KT):
                        values(k)
                        if k == FIRST_MAX_AT[0]:
                            pe.wait_ge(k_split, t * BANKS + KB)
                        if k in FIRST_MAX_AT:
                            scores_for_max(0, FIRST_MAX_AT.index(k))
                    turn_max(0)
                    keys(1)
                    pe.wait_ge(v_kept, (t + 1) * KT)
                    pe.wait_ge(v_split, (t + 1) * KT)
                    for n in range(SIMS):
                        j, k = divmod(n, KT)
                        if not ahead(n - 1):
                            scores(n)
                        if j + 1 < HG:
                            if k in MAX_AT[j]:
                                if j == 0 and k == MAX_AT[0][0]:
                                    pe.wait_ge(k_split, (t + 1) * BANKS)
                                scores_for_max(j + 1, MAX_AT[j].index(k))
                            if k == TURN_AT:
                                turn_max(j + 1)
                        if ahead(n):
                            scores(n + 1)
                        if n >= LAG:
                            weigh(n - LAG)
                    for n in range(SIMS - LAG, SIMS):
                        weigh(n)
                    queries(t + 1, (t + 1) // GROUPS)
                    pe.wait_ge(wo_in_s, t * 16 + 16)
                    for i in range(TT):
                        pe.wait_ge(o_normed, (t + 1) * PAIRS * TT - TT + i + 1)
                        bank = (trio[:, 2, :], pv_ps[:, :])[i // 2]
                        for h in range(PAIRS):
                            ins = pe.matmul(bank[:, (i % 2) * D:(i % 2 + 1) * D], oT[:, h, i * P:(i + 1) * P], wo[:, h, :],
                                            start=h == 0, stop=h == PAIRS - 1)
                    ins.then_inc(x_out, 1)

        @block.scalar
        def _(act):
            act.sem_inc(o_kept, 1)

            def round_queries(t):
                for p in range(PAIRS):
                    act.wait_ge(q_made, t * PAIRS + p + 1)
                    for n in range(2):
                        j, rows = 2 * p + n, slice(n * DH, (n + 1) * DH)
                        for half in range(2):
                            ins = act.activation(q_hi[half * DH:(half + 1) * DH, j, :], trio[rows, p, :], ACT.Copy,
                                                 scale=XSCALE)
                    ins.then_inc(q_rounded, 1)

            round_queries(0)
            with act.Fori(0, B) as b:
                for k in range(KT):
                    act.wait_ge(ctx_turned, b * KT + k + 1 + CRING)
                    rows = P if k < KT - 1 else LASTC
                    act.activation(c_hi[:, :, k * P:k * P + rows],
                                   trio[:, k % 3, :].rearrange("p (c n) -> p c n", c=CC)[:, :, 0:rows],
                                   ACT.Copy).then_inc(c_rounded, 1)
                with act.Fori(0, GROUPS) as g:
                    t = b * GROUPS + g

                    def round_keys(p):
                        for n in range(KB):
                            m = BANK_ORDER[n]
                            act.wait_ge(k_made, t * BANKS + p * KB + n + 1)
                            cols = slice(m * KCOL, min((m + 1) * KCOL, CTX_LEN))
                            for dst in (k_hl, k_h1):
                                for half in range(2):
                                    j, rows = 2 * p + half, slice(half * DH, (half + 1) * DH)
                                    ins = act.activation(dst[0:DH, j, cols], wide[rows, m, 0:cols.stop - cols.start],
                                                         ACT.Copy)
                            ins.then_inc(k_rounded, 1)

                    def keep_o(j):
                        act.wait_ge(probs_used, t * SIMS + (j + 1) * KT + HIRING)
                        rows = (j % 2) * DH
                        act.activation(oT[rows:rows + DH, j // 2, :], pv_ps[0:DH, :], ACT.Copy)
                        for r in range(rows, rows + DH, ONES):
                            ins = act.activation(den_pair[r:r + ONES, j // 2, :], pv_ps[DH:DH + ONES, :], ACT.Copy)
                        ins.then_inc(o_kept, 1)

                    round_keys(0)
                    for k in range(KT):
                        act.wait_ge(v_made, t * KT + k + 1)
                        if k >= VRAW:
                            act.wait_ge(v_split, t * KT + k - VRAW + 1)
                        rows = P if k < KT - 1 else LASTC
                        act.activation(v_raw[0:rows, k % VRAW, :], trio[0:rows, k % 3, 0:GW], ACT.Copy)
                        act.activation(v_one[0:rows, k, :, 0:DH],
                                       trio[0:rows, k % 3, 0:GW].rearrange("p (j d) -> p j d", j=HG), ACT.Copy).then_inc(v_kept, 1)
                    round_keys(1)
                    act.wait_ge(rows_stored, b * 32 + 1)
                    for n in range(SIMS):
                        j, k = divmod(n, KT)
                        act.wait_ge(scores_ready, t * SIMS + n + 1)
                        if k == LAG and j >= 1:
                            keep_o(j - 1)
                        if n >= RAW:
                            act.wait_ge(*split_by(n - RAW, t))
                        bank = trio[0:rows_of(k), n % 3, :]
                        act.activation(probs[0:rows_of(k), n % RAW, :], bank, ACT.Exp).then_inc(probs_ready, 1)
                        act.wait_ge(probs_used, t * SIMS + n + 1)
                        act.activation(p_hi[0:rows_of(k), n % HIRING, :], bank, ACT.Exp).then_inc(p_rounded, 1)
                    keep_o(HG - 1)
                    round_queries(t + 1)

        @block.vector
        def _(dve):
            dve.sem_inc(rows_stored, 1)
            def split_queries(t):
                for p in range(PAIRS):
                    dve.wait_ge(q_rounded, t * PAIRS + p + 1)
                    for n in range(2):
                        j, rows = 2 * p + n, slice(n * DH, (n + 1) * DH)
                        ins = dve.scalar_tensor_tensor(out=q_lo[0:DH, j, :], in0=trio[rows, p, :], scalar=XSCALE,
                                                       in1=q_hi[0:DH, j, :].bitcast(F32), op0=ALU.mult,
                                                       op1=ALU.subtract)
                    ins.then_inc(q_split, 1)

            def split_context(b):
                for k in range(KT):
                    dve.wait_ge(c_rounded, b * KT + k + 1)
                    rows = P if k < KT - 1 else LASTC
                    cols = slice(k * P, k * P + rows)
                    dve.tensor_tensor(c_lo[:, :, cols], trio[:, k % 3, :].rearrange("p (c n) -> p c n", c=CC)[:, :, 0:rows],
                                      c_hi[:, :, cols].bitcast(F32), ALU.subtract).then_inc(c_split, 1)

            def norm_rows(b):
                chain = Chain(dve, dve_batch, b, FINISH)
                dve.wait_ge(acc_added, (b + 1) * GROUPS + 1)
                moments(dve, chain, stats, mv, rstd[:, :], newton[:, :], acc_rows, X_EPS)
                chain.link(normalise(dve, mv, rstd, acc_rows, acc_rows))
                return chain

            def finish_rows(b, chain):
                dve.wait_ge(x1_in, (b + 1) * 48)
                for i in range(TT):
                    ins = dve.tensor_tensor(acc[:, i, :], acc[:, i, :], ln_scale, ALU.mult)
                chain.link(ins)
                for i in range(TT):
                    ins = dve.tensor_tensor(acc[:, i, :], acc[:, i, :], ln_bias, ALU.add)
                chain.link(ins)
                chain.link(dve.tensor_tensor(x1, x1, acc[:, :, :], ALU.add))
                dve.sem_inc(x2_ready, 1)
                out_rows = [x1[:, i, :] for i in range(TT)]
                moments(dve, chain, stats, mv, rstd[:, :], newton[:, :], out_rows, LN_EPS)
                chain.link(normalise(dve, mv, rstd, acc_rows, out_rows))
                dve.sem_inc(h3_ready, 1)
                chain.close()

            def split_keys(t, p):
                for n in range(KB):
                    m = BANK_ORDER[n]
                    dve.wait_ge(k_rounded, t * BANKS + p * KB + n + 1)
                    cols = slice(m * KCOL, min((m + 1) * KCOL, CTX_LEN))
                    for half in range(2):
                        j, rows = 2 * p + half, slice(half * DH, (half + 1) * DH)
                        ins = dve.tensor_tensor(k_hl[DH:P, j, cols], wide[rows, m, 0:cols.stop - cols.start],
                                                k_hl[0:DH, j, cols].bitcast(F32), ALU.subtract)
                    ins.then_inc(k_split, 1)

            def take_max(t, j, i):
                dve.wait_ge(max_scores, t * HG * TT + j * TT + i + 1)
                dve.tensor_reduce(neg_max[:, j % 2, i:i + 1], wide[:, :, 0:KCOL], AX.XY, ALU.max,
                                  negate=True).then_inc(max_taken, 1)

            def keep_max(t, j):
                dve.wait_ge(max_turned, t * HG + j + 1)
                dve.tensor_copy(q_lo[DH:DH + 1, j, :], wide[0:1, 0, :]).then_inc(max_row, 1)

            def split_probs(t, n):
                k = n % KT
                if k in ON_DVE:
                    dve.wait_ge(p_rounded, t * SIMS + n + 1)
                    dve.wait_ge(probs_used, t * SIMS + n + 1 - LORING + HIRING)
                    dve.tensor_tensor(p_lo[0:rows_of(k), n % LORING, :], probs[0:rows_of(k), n % RAW, :],
                                      p_hi[0:rows_of(k), n % HIRING, :].bitcast(F32), ALU.subtract).then_inc(split_dve, 1)

            def norm(t, h, i):
                cols = slice(i * P, (i + 1) * P)
                if i == 0:
                    dve.wait_ge(o_kept, t * HG + 2 * h + 3)
                dve.reciprocal(den_pair[:, h, cols], den_pair[:, h, cols]).then_inc(dve_norm, 1)
                dve.wait_ge(dve_norm, (t * PAIRS + h) * TT + i + 1)
                dve.tensor_tensor(oT[:, h, cols], oT[:, h, cols], den_pair[:, h, cols], ALU.mult).then_inc(o_normed, 1)

            def group(t, first=False, before=None):
                if before is not None:
                    chain = norm_rows(before)
                split_keys(t, 0)
                if before is not None:
                    finish_rows(before, chain)
                for i in range(TT):
                    take_max(t, 0, i)
                keep_max(t, 0)
                split_keys(t, 1)
                for n in range(SIMS):
                    j, k = divmod(n, KT)
                    if n >= 1:
                        split_probs(t, n - 1)
                    if j + 1 < HG:
                        if k in MAX_AT[j]:
                            take_max(t, j + 1, MAX_AT[j].index(k))
                        if k == TURN_AT:
                            keep_max(t, j + 1)
                    elif k in NORM_AT:
                        norm(t, 0, NORM_AT.index(k))
                split_probs(t, SIMS - 1)
                for i in range(TT):
                    norm(t, 1, i)
                split_queries(t + 1)
                if before is not None:
                    dve.wait_ge(rows_stored, (before + 1) * 32 + 1)
                dve.wait_ge(acc_added, t + 1)
                dve.wait_ge(x_out, t + 2)
                for n, bank in enumerate((trio[:, 2, :], pv_ps[:, :])):
                    rows = acc[:, 2 * n:2 * n + 2, :].rearrange("p i d -> p (i d)")
                    if first:
                        ins = dve.tensor_copy(rows, bank)
                    else:
                        ins = dve.tensor_tensor(rows, rows, bank, ALU.add)
                ins.then_inc(acc_added, 1)

            dve.sem_inc(acc_added, 1)
            split_queries(0)
            split_context(0)
            dve.wait_ge(consts_in, CONSTS_IN * 16)
            dve.wait_ge(pool_step, POOL_STEPS)
            dve.tensor_scalar(null_wide, null_wide, null_k[:, 0:1], None, ALU.add).then_inc(null_ready, 1)
            dve.wait_ge(null_ready, 1)
            dve.tensor_copy(k_hl[0:DH, :, CTX_LEN:KPAD], null_wide)
            dve.tensor_copy(k_h1[0:DH, :, CTX_LEN:KPAD], null_wide).then_inc(null_ready, 1)
            for j in range(HG):
                ins = dve.tensor_copy(v_one[NULL_ROWS, KT - 1, j, 0:DH], null_v[NULL_ROWS, :])
            ins.then_inc(null_ready, 1)
            dve.wait_ge(null_ready, 3)
            for j in range(HG):
                dve.tensor_tensor(v_lo[NULL_ROWS, KT - 1, j, :], null_v[NULL_ROWS, :],
                                  v_one[NULL_ROWS, KT - 1, j, 0:DH].bitcast(F32), ALU.subtract)
            dve.tensor_tensor(k_hl[DH:P, :, CTX_LEN:KPAD], null_wide, k_hl[0:DH, :, CTX_LEN:KPAD].bitcast(F32),
                              ALU.subtract).then_inc(null_ready, 1)
            group(0, True)
            with dve.Fori(1, GROUPS) as g:
                group(g)
            with dve.Fori(1, B) as b:
                split_context(b)
                group(b * GROUPS, True, b - 1)
                with dve.Fori(1, GROUPS) as g:
                    group(b * GROUPS + g)
            finish_rows(B - 1, norm_rows(B - 1))


def experts(nc, A, out, c):
    (B, S, D, NT, DC, EXPERTS, F, SHARE, CAP, FC, FL, SC, REP) = (c[k] for k in (
        "B", "S", "D", "NT", "DC", "EXPERTS", "F", "SHARE", "CAP", "FC", "FL", "SC", "REP"))
    wide, trio, pv_ps, ident = (c[k] for k in ("wide", "trio", "pv_ps", "ident"))
    x2_dram, h3_dram = c["x2_dram"], c["h3_dram"]
    N = B * S
    SHIFTS = [28, 24, 20, 16, 12, 8, 4, 0]
    FIRST_FOLD = 2
    assert NT == REP

    with ExitStack() as scope:
        def sb(name, shape, dt=F32):
            return scope.enter_context(nc.sbuf_tensor(name, shape, dt))

        def sem(name):
            return scope.enter_context(nc.semaphore(name))

        x2 = sb("x2", [P, NT, D])
        h3 = sb("h3", [P, NT, D])
        h3_hi = sb("h3_hi", [P, NT, D], F32R)
        h3_lo = sb("h3_lo", [P, NT, D], F32R)
        ones_row = sb("e_ones_row", [1, P])
        w_r = sb("w_r", [P, DC, EXPERTS])
        b_r = sb("b_r", [P, EXPERTS])
        lmax = sb("lmax", [P, NT])
        lsum = sb("lsum", [P, NT])
        lexp = sb("lexp", [P, NT, EXPERTS])
        gate = sb("gate", [P, NT, EXPERTS])
        same = sb("same", [P, EXPERTS, REP])
        digit = sb("digit", [P, 1], I32)
        base = sb("base", [P, 1], I32)
        tried = sb("tried", [P, 1], I32)
        step = sb("step", [P, 1], I32)
        count = sb("count", [P, 1])
        enough = sb("enough", [P, 1])
        gateT = sb("gateT", [P, N])
        above = sb("above", [P, N])
        gate_by = sb("gate_by", [P, P])
        higher = sb("higher", [P, P])
        equal = sb("equal", [P, P])
        run = sb("run", [P, P])
        rank = sb("rank", [P, P])
        zeros = sb("zeros", [P, P])
        tallies = sb("tallies", [P, 2])
        need = sb("need", [P, 1])
        offset = sb("offset", [P, 1])
        before = sb("before", [P, EXPERTS, REP])
        digits = sb("digits", [P, len(SHIFTS)], I32)
        slot = sb("slot", [P, NT, EXPERTS + 1])
        slot_no = sb("slot_no", [P, CAP])
        slot_i = sb("slot_i", [P, CAP], I32)
        picks = sb("picks", [P, 2, NT, CAP], F32R)
        h3T = sb("h3T", [P, DC, N])
        gate_rep = sb("gate_rep", [P, NT, EXPERTS, REP])
        pickT = sb("pickT", [P, SC, N], F32R)
        w_up = h3[:, :, :].rearrange("p t d -> p (t d)")[:, 0:DC * F].rearrange("p (c f) -> p c f", c=DC)
        w_dn = gate_rep[:, :, :, :].rearrange("p t e r -> p (t e r)")[:, 0:FC * D].rearrange("p (c d) -> p c d", c=FC)
        mid = above[:, 0:FC * CAP].rearrange("p (c n) -> p c n", c=FC)
        up_hi, up_lo = sb("up_hi", [P, DC, F], F32R), sb("up_lo", [P, DC, F], F32R)
        dn_hi, dn_lo = sb("dn_hi", [P, FC, D], F32R), sb("dn_lo", [P, FC, D], F32R)
        zero = sb("e_zero", [P, 1])
        b_up = sb("b_up", [P, FC])
        b_dn = sb("b_dn", [1, D])
        taken_hi, taken_lo = sb("taken_hi", [P, DC, CAP], F32R), sb("taken_lo", [P, DC, CAP], F32R)
        mid_hi, mid_lo = sb("mid_hi", [P, FC, CAP], F32R), sb("mid_lo", [P, FC, CAP], F32R)
        made_hi = sb("made_hi", [P, SC, D], F32R)
        made_lo = sb("made_lo", [P, SC, D], F32R)

        e_const, e_chain, router_in = sem("e_const"), sem("e_chain"), sem("router_in")
        TT = NT // B
        assert TT == 4
        h3_in = [sem(f"h3_in_{b}") for b in range(B)]
        x2_in, h3_turned, h3_kept, h3_split = (
            sem("x2_in"), sem("h3_turned"), sem("h3_kept"), sem("h3_split"))
        logits_ready, l_shift, l_exp = sem("logits_ready"), sem("l_shift"), sem("l_exp")
        spread, gate_turned, gate_kept, tried_count, tried_sum = (
            sem("spread"), sem("gate_turned"), sem("gate_kept"), sem("tried_count"), sem("tried_sum"))
        gate_dealt, tallied, summed = sem("gate_dealt"), sem("tallied"), sem("summed")
        slots_known, slots_turned, slots_kept = sem("slots_known"), sem("slots_turned"), sem("slots_kept")
        up_in, dn_in = sem("up_in"), sem("dn_in")
        picked, pick_turned, pick_kept = sem("picked"), sem("pick_turned"), sem("pick_kept")
        gathered, taken_rounded, taken_split = sem("gathered"), sem("taken_rounded"), sem("taken_split")
        up_rounded, up_split, dn_rounded, dn_split, mid_split = (
            sem("up_rounded"), sem("up_split"), sem("dn_rounded"), sem("dn_split"), sem("mid_split"))
        up_done, mid_ready, dn_done, made_rounded, made_split = (
            sem("up_done"), sem("mid_ready"), sem("dn_done"), sem("made_rounded"), sem("made_split"))
        spread_back, added = sem("spread_back"), sem("added")
        stored = sem("e_stored")

        block = scope.enter_context(nc.Block())
        SUMS = len(SHIFTS)
        TURNS = NT * SC // 4
        H_TURNS = NT * DC // 4

        @block.sync
        def _(sp):
            for b in range(B):
                sp.dma_start(h3[:, b * TT:(b + 1) * TT, :], h3_dram[b].rearrange("(t p) d -> p t d", p=P))\
                  .then_inc(h3_in[b], 16)
            sp.dma_start(w_r[:, :, :], A["L0_ffn_Wr"].rearrange("(c p) f -> p c f", p=P)).then_inc(router_in, 16)
            sp.dma_start(b_r[:, :], A["L0_ffn_br"].rearrange("(a d) -> a d", a=1).to_broadcast([P, EXPERTS])).then_inc(router_in, 16)
            sp.dma_start(x2[:, :, :], x2_dram.rearrange("b (t p) d -> p (b t) d", p=P)).then_inc(x2_in, 16)
            sp.wait_ge(gate_kept, 1)
            for r in range(REP):
                sp.dma_start(gate_by[r:P:REP, :], gateT[r:P:REP, r * P:(r + 1) * P]).then_inc(gate_dealt, 16)
            sp.wait_ge(h3_split, 2)
            with sp.Fori(0, EXPERTS // SHARE) as g:
                sp.wait_ge(mid_ready, (g + 1) * SHARE * FC)
                up = A["L0_ffn_W_up"][bass.ds(g, 1)].rearrange("a (c p) f -> p (a c) f", p=P)
                sp.dma_start(w_up[:, :, :], up).then_inc(up_in, 16)
                bu = A["L0_ffn_b_up"][bass.ds(g, 1)]
                with nc.allow_non_contiguous_dma(reason="a column of the hidden dimension on partitions"):
                    sp.dma_start(b_up[:, 0:FC - 1], bu[:, 0:(FC - 1) * P].rearrange("a (c p) -> p (a c)", p=P))\
                      .then_inc(up_in, 16)
                    sp.dma_start(b_up[0:FL, FC - 1:FC], bu[:, (FC - 1) * P:F].rearrange("a p -> p a")).then_inc(up_in, 16)
                for n in range(SHARE):
                    e = g * SHARE + n
                    sp.wait_ge(dn_done, e + 1)
                    dn = A["L0_ffn_W_down"][bass.ds(e, 1)].rearrange("a f d -> (a f) d")
                    sp.dma_start(w_dn[:, 0:FC - 1, :], dn[0:(FC - 1) * P, :].rearrange("(c p) d -> p c d", p=P))\
                      .then_inc(dn_in, 16)
                    sp.dma_start(w_dn[0:FL, FC - 1, :], dn[(FC - 1) * P:F, :]).then_inc(dn_in, 16)
                    sp.dma_start(b_dn[:, :], A["L0_ffn_b_down"][bass.ds(e, 1)]).then_inc(dn_in, 16)
            for b in range(B):
                sp.wait_ge(added, EXPERTS * NT + (b + 1) * NT // B)
                sp.dma_start(out[b].rearrange("(t p) d -> p t d", p=P), x2[:, b * NT // B:(b + 1) * NT // B, :])\
                  .then_inc(stored, 16)
            sp.wait_ge(stored, B * 16)

        @block.gpsimd
        def _(pool):
            n = 0

            def link(ins):
                nonlocal n
                n += 1
                ins.then_inc(e_const, 1)
                pool.wait_ge(e_const, n)

            link(pool.memset(ones_row[:, :], 1.0))
            link(pool.memset(zero[:, :], 0.0))
            link(pool.memset(same[:, :, :], 1.0))
            link(pool.affine_select(out=same[:, :, :], in_=same[:, :, :], compare_op=ALU.is_ge, fill=0.0, base=0,
                                    pattern=[[-REP, EXPERTS], [0, REP]], channel_multiplier=1))
            link(pool.affine_select(out=same[:, :, :], in_=same[:, :, :], compare_op=ALU.is_ge, fill=0.0, base=REP - 1,
                                    pattern=[[REP, EXPERTS], [0, REP]], channel_multiplier=-1))
            link(pool.affine_select(out=before[:, :, :], in_=same[:, :, :], compare_op=ALU.is_ge, fill=0.0, base=-1,
                                    pattern=[[REP, EXPERTS], [1, REP]], channel_multiplier=-1))
            link(pool.iota(slot_i[:, :], [[1, CAP]], base=1, channel_multiplier=0))
            link(pool.iota(digit[:, :], [[0, 1]], base=0, channel_multiplier=1))
            link(pool.memset(zeros[:, :], 0.0))
            link(pool.memset(slot[:, :, EXPERTS:EXPERTS + 1], -1.0))
            for b in range(B):
                pool.wait_ge(h3_in[b], 16)
            pool.tensor_copy(h3_hi[:, :, :], h3[:, :, :]).then_inc(h3_split, 1)
            pool.wait_ge(h3_split, 1)
            pool.tensor_tensor(h3_lo[:, :, :], h3[:, :, :], h3_hi[:, :, :].bitcast(F32), ALU.subtract).then_inc(h3_split, 1)

            def zeros_of(rows, a, cols):
                return zero[0:rows, :].rearrange("p (a b) -> p a b", a=1).to_broadcast([rows, a, cols])

            with pool.Fori(0, EXPERTS // SHARE) as g:
                pool.wait_ge(up_in, g * 48 + 48)
                pool.tensor_tensor(up_hi[:, :, :], w_up[:, :, :], zeros_of(P, DC, F), ALU.add).then_inc(up_rounded, 1)
                pool.wait_ge(up_rounded, g + 1)
                pool.tensor_tensor(up_lo[:, :, :], w_up[:, :, :], up_hi[:, :, :].bitcast(F32), ALU.subtract)\
                    .then_inc(up_split, 1)
                for n in range(SHARE):
                    e = g * SHARE + n
                    pool.wait_ge(dn_in, e * 48 + 48)
                    parts = ((slice(0, P), slice(0, FC - 1)), (slice(0, FL), slice(FC - 1, FC)))
                    for r, f in parts:
                        pool.tensor_tensor(dn_hi[r, f, :], w_dn[r, f, :], zeros_of(r.stop, f.stop - f.start, D), ALU.add)\
                            .then_inc(dn_rounded, 1)
                    pool.wait_ge(dn_rounded, (e + 1) * 2)
                    for r, f in parts:
                        pool.tensor_tensor(dn_lo[r, f, :], w_dn[r, f, :], dn_hi[r, f, :].bitcast(F32), ALU.subtract)\
                            .then_inc(dn_split, 1)

        CONSTS = 10

        @block.tensor
        def _(pe):
            pe.sem_inc(dn_done, 1)
            for n in range(H_TURNS):
                b, ck = divmod(n, DC)
                pe.wait_ge(h3_in[b], 16)
                if n >= 4:
                    pe.wait_ge(h3_kept, n - 3)
                for m in range(TT):
                    i = b * TT + m
                    ins = pe.transpose(wide[:, n % 4, m * P:(m + 1) * P], h3[:, i, ck * P:(ck + 1) * P], ident[:, :])
                ins.then_inc(h3_turned, 1)
            pe.wait_ge(e_const, 1)
            pe.wait_ge(router_in, 32)
            pe.wait_ge(h3_kept, H_TURNS)
            for i in range(NT):
                bank = pv_ps[:, i * EXPERTS:(i + 1) * EXPERTS]
                for ck in range(DC):
                    ins = pe.matmul(bank, h3T[:, ck, i * P:(i + 1) * P], w_r[:, ck, :], start=ck == 0, stop=ck == DC - 1)
            ins.then_inc(logits_ready, 1)
            pe.wait_ge(e_const, CONSTS)
            pe.wait_ge(spread, 1)
            for i in range(NT):
                ins = pe.transpose(wide[:, i // 4, (i % 4) * P:(i % 4 + 1) * P],
                                   gate_rep[:, i, :, :].rearrange("p e r -> p (e r)"), ident[:, :])
            ins.then_inc(gate_turned, 1)
            for n in range(len(SHIFTS)):
                pe.wait_ge(tried_count, n + 1)
                pe.matmul(pv_ps[:, n:n + 1], same[:, :, :].rearrange("p e r -> p (e r)"), enough[:, :], start=True,
                          stop=True).then_inc(tried_sum, 1)
            pe.wait_ge(tallied, 2)
            pe.matmul(pv_ps[:, SUMS:SUMS + 1], same[:, :, :].rearrange("p e r -> p (e r)"), tallies[:, 0:1], start=True,
                      stop=True)
            pe.matmul(pv_ps[:, SUMS + 1:SUMS + 2], before[:, :, :].rearrange("p e r -> p (e r)"), tallies[:, 1:2],
                      start=True, stop=True).then_inc(summed, 1)
            pe.wait_ge(tallied, 3)
            pe.matmul(pv_ps[:, SUMS + 2:SUMS + 3], before[:, :, :].rearrange("p e r -> p (e r)"), run[:, P - 1:P],
                      start=True, stop=True).then_inc(summed, 1)
            pe.wait_ge(slots_known, 1)
            pe.transpose(wide[:, 0, 0:P], rank[:, :], ident[:, :]).then_inc(slots_turned, 1)
            pe.wait_ge(slots_kept, 1)
            pe.wait_ge(h3_split, 2)
            with pe.Fori(0, EXPERTS // SHARE) as g:
                for n in range(SHARE):
                    e = g * SHARE + n
                    pick = picks[:, n % 2, :, :]

                    def turn_picks(first, last):
                        for k in range(first, last):
                            if k == 0:
                                pe.wait_ge(added, (e + 1) * NT)
                            if k >= 3:
                                pe.wait_ge(pick_kept, e * TURNS + k - 2)
                            for m in range(4):
                                sc, i = divmod(k * 4 + m, NT)
                                ins = pe.transpose(trio[:, k % 3, m * P:(m + 1) * P],
                                                   pick[:, i, sc * P:(sc + 1) * P].bitcast(F32), ident[:, :])
                            ins.then_inc(pick_turned, 1)

                    for i in range(NT):
                        pe.wait_ge(picked, e * NT + i + 1)
                        for ck in range(DC):
                            for m, part in enumerate((h3_hi, h3_lo)):
                                ins = pe.matmul(wide[:, ck, 0:CAP], part[:, i, ck * P:(ck + 1) * P], pick[:, i, :],
                                                start=i == 0 and m == 0, stop=i == NT - 1 and m == 1)
                    ins.then_inc(gathered, 1)
                    turn_picks(0, TURNS // 2)
                    pe.wait_ge(up_split, g + 1)
                    pe.wait_ge(taken_split, e + 1)
                    for f in range(FC):
                        M = P if f < FC - 1 else FL
                        if f >= 3:
                            pe.wait_ge(mid_ready, e * FC + f - 2 + SHARE * FC)
                        bank = (pv_ps[:, :], wide[:, 0, :], wide[:, 1, :])[f % 3]
                        for ck in range(DC):
                            for m, (w, rows) in enumerate(((up_hi, taken_hi), (up_hi, taken_lo), (up_lo, taken_hi))):
                                ins = pe.matmul(bank[0:M, 0:CAP], w[:, ck, f * P:f * P + M], rows[:, ck, :],
                                                start=ck == 0 and m == 0, stop=ck == DC - 1 and m == 2)
                        ins.then_inc(up_done, 1)
                    pe.wait_ge(dn_split, (e + 1) * 2)
                    for f in range(FC):
                        M = P if f < FC - 1 else FL
                        pe.wait_ge(mid_split, e * FC + f + 1)
                        for sc in range(SC):
                            for m, (rows, w) in enumerate(((mid_hi, dn_hi), (mid_hi, dn_lo), (mid_lo, dn_hi))):
                                pe.matmul(wide[:, 2 + sc, 0:D], rows[0:M, f, sc * P:(sc + 1) * P], w[0:M, f, :],
                                          start=f == 0 and m == 0, stop=False)
                    for sc in range(SC):
                        ins = pe.matmul(wide[:, 2 + sc, 0:D], ones_row[:, :], b_dn[:, :], start=False, stop=True)
                    ins.then_inc(dn_done, 1)
                    turn_picks(TURNS // 2, TURNS)
                    pe.wait_ge(made_split, e + 1)
                    pe.wait_ge(pick_kept, (e + 1) * TURNS)
                    for i in range(NT):
                        if i >= 3:
                            pe.wait_ge(added, (e + 1) * NT + i - 2)
                        for sc in range(SC):
                            for m, part in enumerate((made_hi, made_lo)):
                                ins = pe.matmul(trio[:, i % 3, 0:D], pickT[:, sc, i * P:(i + 1) * P], part[:, sc, :],
                                                start=sc == 0 and m == 0, stop=sc == SC - 1 and m == 1)
                        ins.then_inc(spread_back, 1)

        @block.scalar
        def _(act):
            act.sem_inc(mid_ready, SHARE * FC)
            for n in range(H_TURNS):
                act.wait_ge(h3_turned, n + 1)
                b, ck = divmod(n, DC)
                act.activation(h3T[:, ck, b * TT * P:(b + 1) * TT * P], wide[:, n % 4, :], ACT.Copy).then_inc(h3_kept, 1)
            act.wait_ge(l_shift, 1)
            act.activation(lexp[:, :, :], lexp[:, :, :], ACT.Exp).then_inc(l_exp, 1)
            act.wait_ge(gate_turned, 1)
            act.activation(gateT[:, :], wide[:, :, :].rearrange("p b n -> p (b n)"), ACT.Copy).then_inc(gate_kept, 1)
            with act.Fori(0, EXPERTS // SHARE) as g:
                for n in range(SHARE):
                    e = g * SHARE + n

                    def keep_picks(first, last):
                        for k in range(first, last):
                            act.wait_ge(pick_turned, e * TURNS + k + 1)
                            sc, i = divmod(k * 4, NT)
                            act.activation(pickT[:, sc, i * P:(i + 4) * P], trio[:, k % 3, :], ACT.Copy)\
                               .then_inc(pick_kept, 1)

                    act.wait_ge(gathered, e + 1)
                    act.activation(taken_hi[:, :, :], wide[:, 0:DC, 0:CAP], ACT.Copy).then_inc(taken_rounded, 1)
                    keep_picks(0, TURNS // 2)
                    for f in range(FC):
                        M = P if f < FC - 1 else FL
                        act.wait_ge(up_done, e * FC + f + 1)
                        bank = (pv_ps[:, :], wide[:, 0, :], wide[:, 1, :])[f % 3]
                        act.activation(mid[0:M, f, :], bank[0:M, 0:CAP], ACT.Silu, bias=b_up[0:M, f:f + 1])
                        act.activation(mid_hi[0:M, f, :], bank[0:M, 0:CAP], ACT.Silu,
                                       bias=b_up[0:M, f:f + 1]).then_inc(mid_ready, 1)
                    act.wait_ge(dn_done, e + 2)
                    act.activation(made_hi[:, :, :], wide[:, 2:2 + SC, 0:D], ACT.Copy).then_inc(made_rounded, 1)
                    keep_picks(TURNS // 2, TURNS)

        @block.vector
        def _(dve):
            n = 0

            def link(ins):
                nonlocal n
                n += 1
                ins.then_inc(e_chain, 1)
                dve.wait_ge(e_chain, n)

            def over_experts(v):
                return v[:, :].rearrange("p (t a) -> p t a", a=1).to_broadcast([P, NT, EXPERTS])

            dve.wait_ge(e_const, CONSTS)
            link(dve.tensor_copy(slot_no[:, :], slot_i[:, :]))
            link(dve.tensor_single_scalar(digit[:, :], digit[:, :], REP - 1, ALU.bitwise_and))
            link(dve.memset(base[:, :], 0))
            for k, shift in enumerate(SHIFTS):
                fold = FIRST_FOLD if k == 0 else 0
                ins = dve.tensor_scalar(digits[:, k:k + 1], digit[:, :], fold, shift, ALU.logical_shift_right,
                                        ALU.logical_shift_left)
            link(ins)
            dve.sem_inc(added, NT)
            dve.wait_ge(logits_ready, 1)
            logits = pv_ps[:, 0:NT * EXPERTS].rearrange("p (t e) -> p t e", e=EXPERTS)
            dve.wait_ge(router_in, 32)
            link(dve.tensor_tensor(lexp[:, :, :], logits,
                                   b_r[:, :].rearrange("p (a e) -> p a e", a=1).to_broadcast([P, NT, EXPERTS]), ALU.add))
            link(dve.tensor_reduce(lmax[:, :], lexp[:, :, :], AX.X, ALU.max))
            dve.tensor_tensor(lexp[:, :, :], lexp[:, :, :], over_experts(lmax), ALU.subtract).then_inc(l_shift, 1)
            dve.wait_ge(l_exp, 1)
            link(dve.tensor_reduce(lsum[:, :], lexp[:, :, :], AX.X, ALU.add))
            link(dve.reciprocal(lsum[:, :], lsum[:, :]))
            link(dve.tensor_tensor(gate[:, :, :], lexp[:, :, :], over_experts(lsum), ALU.mult))
            dve.tensor_copy(gate_rep[:, :, :, :],
                            gate[:, :, :].rearrange("p t (e a) -> p t e a", a=1).to_broadcast([P, NT, EXPERTS, REP]))\
               .then_inc(spread, 1)
            dve.wait_ge(gate_kept, 1)
            for k, shift in enumerate(SHIFTS):
                fold = FIRST_FOLD if k == 0 else 0
                link(dve.tensor_tensor(tried[:, :], digits[:, k:k + 1], base[:, :], ALU.bitwise_or))
                link(dve.tensor_scalar(above[:, :], gateT[:, :], tried[:, 0:1].bitcast(F32), 0.0, ALU.is_ge, ALU.add,
                                       accum_out=count[:, :]))
                dve.tensor_single_scalar(enough[:, :], count[:, :], float(CAP), ALU.is_ge).then_inc(tried_count, 1)
                dve.wait_ge(tried_sum, k + 1)
                link(dve.tensor_scalar(step[:, :], pv_ps[:, k:k + 1], 1.0 / (1 << fold), -1.0, ALU.mult, ALU.add))
                link(dve.tensor_single_scalar(step[:, :], step[:, :], shift, ALU.logical_shift_left))
                link(dve.tensor_tensor(base[:, :], base[:, :], step[:, :], ALU.bitwise_or))
            cut = base[:, 0:1].bitcast(F32)
            dve.wait_ge(gate_dealt, REP * 16)
            dve.tensor_scalar(higher[:, :], gate_by[:, :], cut, 0.0, ALU.is_gt, ALU.add, accum_out=tallies[:, 0:1])\
               .then_inc(tallied, 1)
            dve.tensor_scalar(equal[:, :], gate_by[:, :], cut, 0.0, ALU.is_equal, ALU.add, accum_out=tallies[:, 1:2])\
               .then_inc(tallied, 1)
            dve.wait_ge(tallied, 2)
            link(dve.tensor_tensor_scan(run[:, :], equal[:, :], zeros[:, :], 0.0, ALU.add, ALU.add))
            dve.wait_ge(summed, 1)
            link(dve.tensor_scalar(need[:, :], pv_ps[:, SUMS:SUMS + 1], -1.0, float(CAP), ALU.mult, ALU.add))
            link(dve.tensor_tensor(need[:, :], need[:, :], pv_ps[:, SUMS + 1:SUMS + 2], ALU.subtract))
            link(dve.scalar_tensor_tensor(out=equal[:, :], in0=run[:, :], scalar=need[:, 0:1], in1=equal[:, :],
                                          op0=ALU.is_le, op1=ALU.mult))
            dve.tensor_tensor_scan(run[:, :], higher[:, :], equal[:, :], 0.0, ALU.add, ALU.add).then_inc(tallied, 1)
            link(dve.tensor_tensor(higher[:, :], higher[:, :], equal[:, :], ALU.add))
            dve.wait_ge(summed, 2)
            link(dve.tensor_copy(offset[:, :], pv_ps[:, SUMS + 2:SUMS + 3]))
            dve.scalar_tensor_tensor(out=rank[:, :], in0=run[:, :], scalar=offset[:, 0:1], in1=higher[:, :], op0=ALU.add,
                                     op1=ALU.mult).then_inc(slots_known, 1)
            dve.wait_ge(slots_turned, 1)
            dve.tensor_copy(slot[:, :, 0:EXPERTS], wide[:, 0, 0:P].rearrange("p (e i) -> p i e", e=EXPERTS))\
               .then_inc(slots_kept, 1)
            dve.wait_ge(slots_kept, 1)
            dve.wait_ge(x2_in, 16)

            def choose(e, half):
                for i in range(NT):
                    col = e if isinstance(e, slice) else bass.ds(e, 1)
                    dve.tensor_scalar(picks[:, half, i, :], slot_no[:, :], slot[:, i, col], None,
                                      ALU.is_equal).then_inc(picked, 1)

            choose(slice(0, 1), 0)
            with dve.Fori(0, EXPERTS // SHARE) as g:
                for m in range(SHARE):
                    e = g * SHARE + m
                    if m:
                        dve.wait_ge(pick_turned, e * TURNS)
                    dve.wait_ge(taken_rounded, e + 1)
                    dve.tensor_tensor(taken_lo[:, :, :], wide[:, 0:DC, 0:CAP], taken_hi[:, :, :].bitcast(F32),
                                      ALU.subtract).then_inc(taken_split, 1)
                    for f in range(FC):
                        M = P if f < FC - 1 else FL
                        dve.wait_ge(mid_ready, e * FC + f + 1 + SHARE * FC)
                        dve.tensor_tensor(mid_lo[0:M, f, :], mid[0:M, f, :], mid_hi[0:M, f, :].bitcast(F32),
                                          ALU.subtract).then_inc(mid_split, 1)
                    choose(e + 1, (m + 1) % 2)
                    dve.wait_ge(made_rounded, e + 1)
                    dve.tensor_tensor(made_lo[:, :, :], wide[:, 2:2 + SC, 0:D], made_hi[:, :, :].bitcast(F32),
                                      ALU.subtract).then_inc(made_split, 1)
                    for i in range(NT):
                        dve.wait_ge(spread_back, e * NT + i + 1)
                        dve.scalar_tensor_tensor(out=x2[:, i, :], in0=trio[:, i % 3, 0:D],
                                                 scalar=gate[:, i, bass.ds(e, 1)],
                                                 in1=x2[:, i, :], op0=ALU.mult, op1=ALU.add).then_inc(added, 1)


_INS = ['x', 'ctx_2048', 'L0_attn_gamma', 'L0_attn_beta', 'L0_attn_w_qkv', 'L0_attn_w_out', 'L0_attn_b_out',
        'L0_xattn_Wq', 'L0_xattn_Wkv', 'L0_xattn_null_kv', 'L0_xattn_Wout', 'L0_xattn_ln_scale', 'L0_xattn_ln_bias',
        'L0_ffn_Wr', 'L0_ffn_br', 'L0_ffn_W_up', 'L0_ffn_b_up', 'L0_ffn_W_down', 'L0_ffn_b_down']


def kernel(**inputs):
    import numpy as _np
    import concourse.bacc as _bacc
    from concourse import mybir as _mybir
    from concourse.bass_utils import run_bass_kernel_spmd as _run

    nc = _bacc.Bacc("TRN2", target_bir_lowering=False, num_devices=1)
    arrays, aps = {}, {}
    for name in _INS:
        a = _np.ascontiguousarray(inputs[name])
        arrays[f"in_{name}_dram"] = a
        aps[name] = nc.dram_tensor(f"in_{name}_dram", a.shape, _mybir.dt.from_np(a.dtype), kind="ExternalInput").ap()
    shape = inputs["x"].shape
    res = nc.dram_tensor("out_0_dram", shape, _mybir.dt.float32, kind="ExternalOutput").ap()
    build(nc, aps, res)
    r = _run(nc, [arrays], core_ids=[0])
    return r.results[0]["out_0_dram"]
```
